# Optimizing a Trainium2 kernel written in Bass

```python
import numpy as np
import jax
import jax.numpy as jnp

def _softmax(x, axis=-1):
    return jax.nn.softmax(x, axis=axis)

def _gelu(x):
    return jax.nn.gelu(x, approximate=True)

def _silu(x):
    return jax.nn.silu(x)

def _sigmoid(x):
    return jax.nn.sigmoid(x)

def _layernorm(x, axis=-1, eps=1e-05):
    m = jnp.mean(x, axis=axis, keepdims=True)
    v = jnp.var(x, axis=axis, keepdims=True)
    return (x - m) / jnp.sqrt(v + eps)

def _scatter_add(tgt, idx, src, axis=0):
    return tgt.at[idx].add(src)

def _segment_sum(src, seg, n):
    return jax.ops.segment_sum(src, seg, n)
kernel_name = 'mk_decoder_postln_d4_seqx_r8_be37ab'

def setup_inputs(seed: int=0):
    np.random.seed(seed)
    _w = jnp.asarray

    def _rec_inputs():
        import jax
        import jax.numpy as jnp
        _rk = jax.random.key(seed)
        x = 7.22e-05 + 1 * jax.random.normal(jax.random.fold_in(_rk, 1), (4, 512, 128), jnp.float32)
        _lenS = 512 - jax.random.randint(jax.random.fold_in(_rk, 7), (4,), 0, max(1, 512 // 4) + 1, jnp.int32)
        _lenS2 = 77 - jax.random.randint(jax.random.fold_in(_rk, 8), (4,), 0, max(1, 77 // 4) + 1, jnp.int32)
        _ctx_768P = jax.random.normal(jax.random.fold_in(_rk, 11), (4, 16, 96), jnp.float32)
        _ctx_768c = jax.random.dirichlet(jax.random.fold_in(_rk, 511), 0.3 * jnp.ones((16,), jnp.float32), (4, 77))
        _ctx_768t = jnp.einsum('bsk,bkd->bsd', _ctx_768c, _ctx_768P)
        _ctx_768t = _ctx_768t * jax.lax.rsqrt(jnp.mean(jnp.square(_ctx_768t)) + 1e-12) * 0.953939
        ctx_768 = -0.000191848 + 0.999787 * (_ctx_768t + 0.3 * jax.random.normal(jax.random.fold_in(_rk, 611), (4, 77, 96), jnp.float32))
        _validS = jnp.arange(512)[None, :] < _lenS[:, None]
        _validS2 = jnp.arange(77)[None, :] < _lenS2[:, None]
        _causal = jnp.tril(jnp.ones((512, 512), dtype=bool))
        mask_BxS2_bk0 = jnp.logical_not(jnp.broadcast_to(_validS2[:, :], (4, 77)))
        mask_BxS2_bf1 = jnp.ones((4, 77), dtype=bool)
        return (x, ctx_768, mask_BxS2_bk0, mask_BxS2_bf1)
    x, ctx_768, mask_BxS2_bk0, mask_BxS2_bf1 = _rec_inputs()

    def _L0_attn_setup():
        import jax, jax.numpy as jnp
        import numpy as np
        B, T, H, S = (4, 512, 128, 64)
        LN_EPS = 1e-05

        def _reference_tuple_inner(x, A_log, WB, WC, D, Wg, bg, Wout, bout, gamma, beta):
            A = jnp.exp(A_log)
            gate = jax.nn.sigmoid(jnp.einsum('bth,sh->bts', x, Wg) + bg)
            Bx = jnp.einsum('bth,sh->bts', x, WB)
            u = gate * Bx

            def step(state, u_t):
                state = A * state + u_t
                return (state, state)
            s0 = jnp.zeros((x.shape[0], A.shape[0]), x.dtype)
            final_state, states = jax.lax.scan(step, s0, jnp.swapaxes(u, 0, 1))
            states = jnp.swapaxes(states, 0, 1)
            y = jnp.einsum('bts,hs->bth', states, WC) + D * x
            h = y + x
            mu = jnp.mean(h, axis=-1, keepdims=True)
            var = jnp.mean(jnp.square(h - mu), axis=-1, keepdims=True)
            hn = (h - mu) * jax.lax.rsqrt(var + LN_EPS) * gamma + beta
            out = jnp.einsum('bth,oh->bto', hn, Wout) + bout
            return (out, final_state)
        key = jax.random.key(seed)
        ks = jax.random.split(key, 12)
        x = jax.random.normal(ks[0], (B, T, H), jnp.float32)
        A_log = jnp.log(jnp.exp(-0.5 * jnp.ones(S, jnp.float32)) + 0.1 * jax.random.normal(ks[1], (S,), jnp.float32))
        sH = 1.0 / np.sqrt(H)
        sS = 1.0 / np.sqrt(S)
        WB = jax.random.uniform(ks[2], (S, H), jnp.float32, -sH, sH)
        WC = jax.random.uniform(ks[3], (H, S), jnp.float32, -sS, sS)
        D = jax.random.normal(ks[4], (H,), jnp.float32)
        Wg = jax.random.uniform(ks[5], (S, H), jnp.float32, -sH, sH)
        bg = jax.random.uniform(ks[6], (S,), jnp.float32, -sH, sH)
        Wout = jax.random.uniform(ks[7], (H, H), jnp.float32, -sH, sH)
        bout = jax.random.uniform(ks[8], (H,), jnp.float32, -sH, sH)
        gamma = jnp.ones((H,), jnp.float32)
        beta = jnp.zeros((H,), jnp.float32)
        return {'x': x, 'A_log': A_log, 'WB': WB, 'WC': WC, 'D': D, 'Wg': Wg, 'bg': bg, 'Wout': Wout, 'bout': bout, 'gamma': gamma, 'beta': beta}
    _L0_attn_all = _L0_attn_setup()
    _L0_attn_in = {k: v for k, v in _L0_attn_all.items() if k in ('A_log', 'WB', 'WC', 'D', 'Wg', 'bg', 'Wout', 'bout', 'gamma', 'beta')}
    del _L0_attn_all

    def _L0_xattn_setup():
        import jax, jax.numpy as jnp
        import numpy as np
        NUM_HEADS = 16
        EMB_DIM = 128
        CTX_DIM = 96
        D_HEAD = EMB_DIM // NUM_HEADS
        key = jax.random.key(seed)
        ks = jax.random.split(key, 6)
        B, SQ, SKV = (4, 256, 256)
        x = jax.random.normal(ks[0], (B, SQ, EMB_DIM), dtype=jnp.float32)
        ctx = jax.random.normal(ks[1], (B, SKV, CTX_DIM), dtype=jnp.float32)
        sc_q = 1.0 / np.sqrt(EMB_DIM)
        sc_kv = 1.0 / np.sqrt(CTX_DIM)
        Wq = jax.random.normal(ks[2], (EMB_DIM, EMB_DIM), dtype=jnp.float32) * sc_q
        Wk = jax.random.normal(ks[3], (CTX_DIM, EMB_DIM), dtype=jnp.float32) * sc_kv
        Wv = jax.random.normal(ks[4], (CTX_DIM, EMB_DIM), dtype=jnp.float32) * sc_kv
        Wo = jax.random.normal(ks[5], (EMB_DIM, EMB_DIM), dtype=jnp.float32) * sc_q
        return {'x': x, 'contenoised_img': ctx, 'Wq': Wq, 'Wk': Wk, 'Wv': Wv, 'Wo': Wo}
    _L0_xattn_all = _L0_xattn_setup()
    _L0_xattn_in = {k: v for k, v in _L0_xattn_all.items() if k in ('Wq', 'Wk', 'Wv', 'Wo')}
    del _L0_xattn_all

    def _L0_ffn_setup():
        import jax, jax.numpy as jnp
        import numpy as np
        import math
        D_IN = 128
        FEATURES = (512, 512, 128)
        BATCH, SEQ = (8, 256)

        def _conn_dense(kernel_bool, x):
            w = jnp.where(kernel_bool, jnp.float32(1.0), jnp.float32(-1.0))
            return x @ w
        key = jax.random.key(seed)
        kx, kk0, kk1, kk2 = jax.random.split(key, 4)
        x = jax.random.normal(kx, (BATCH, SEQ, D_IN), dtype=jnp.float32)
        k0 = jax.random.randint(kk0, (2 * D_IN, FEATURES[0]), 0, 2).astype(jnp.bool_)
        k1 = jax.random.randint(kk1, (FEATURES[0], FEATURES[1]), 0, 2).astype(jnp.bool_)
        k2 = jax.random.randint(kk2, (FEATURES[1], FEATURES[2]), 0, 2).astype(jnp.bool_)
        s0 = jnp.asarray(1.0 / math.sqrt(2 * D_IN), dtype=jnp.float32)
        s1 = jnp.asarray(1.0 / math.sqrt(FEATURES[0]), dtype=jnp.float32)
        s2 = jnp.asarray(1.0 / math.sqrt(FEATURES[1]), dtype=jnp.float32)
        return {'x': x, 'k0': k0, 'k1': k1, 'k2': k2, 's0': s0, 's1': s1, 's2': s2}
    _L0_ffn_all = _L0_ffn_setup()
    _L0_ffn_in = {k: v for k, v in _L0_ffn_all.items() if k in ('k0', 'k1', 'k2', 's0', 's1', 's2')}
    del _L0_ffn_all

    def _L1_attn_setup():
        import jax, jax.numpy as jnp
        import numpy as np
        DIM = 128
        N_QUAT = DIM // 4
        LN_EPS = 1e-05
        NORM_EPS = 1e-12

        def quat_mul(q1, q2):
            r1, i1, j1, k1 = (q1[..., 0], q1[..., 1], q1[..., 2], q1[..., 3])
            r2, i2, j2, k2 = (q2[..., 0], q2[..., 1], q2[..., 2], q2[..., 3])
            r = r1 * r2 - i1 * i2 - j1 * j2 - k1 * k2
            i = r1 * i2 + i1 * r2 + j1 * k2 - k1 * j2
            j = r1 * j2 - i1 * k2 + j1 * r2 + k1 * i2
            k = r1 * k2 + i1 * j2 - j1 * i2 + k1 * r2
            return jnp.stack([r, i, j, k], axis=-1)

        def quat_conj(q):
            return q * jnp.array([1.0, -1.0, -1.0, -1.0], dtype=q.dtype)
        key = jax.random.key(seed)
        ks = jax.random.split(key, 7)
        B, L, D = (4, 512, DIM)
        s = 1.0 / np.sqrt(D)
        return {'x': jax.random.normal(ks[0], (B, L, D), dtype=jnp.float32), 'Wk': jax.random.normal(ks[1], (D, D), dtype=jnp.float32) * s, 'bk': jnp.zeros((D,), dtype=jnp.float32), 'Wv': jax.random.normal(ks[2], (D, D), dtype=jnp.float32) * s, 'bv': jnp.zeros((D,), dtype=jnp.float32), 'ln_g': jnp.ones((D,), dtype=jnp.float32), 'ln_b': jnp.zeros((D,), dtype=jnp.float32), 'Wo': jax.random.normal(ks[3], (D, D), dtype=jnp.float32) * s, 'bo': jnp.zeros((D,), dtype=jnp.float32)}
    _L1_attn_all = _L1_attn_setup()
    _L1_attn_in = {k: v for k, v in _L1_attn_all.items() if k in ('Wk', 'bk', 'Wv', 'bv', 'ln_g', 'ln_b', 'Wo', 'bo')}
    del _L1_attn_all

    def _L1_xattn_setup():
        import jax, jax.numpy as jnp
        import numpy as np
        HEADS = 16
        DIM_HEAD = 64
        key = jax.random.key(seed)
        ks = jax.random.split(key, 7)
        b, n, m = (2, 256, 128)
        query_dim, context_dim = (128, 96)
        inner = HEADS * DIM_HEAD
        s_q = 1.0 / np.sqrt(query_dim)
        s_c = 1.0 / np.sqrt(context_dim)
        s_i = 1.0 / np.sqrt(inner)
        return {'x': jax.random.normal(ks[0], (b, n, query_dim), jnp.float32), 'context': jax.random.normal(ks[1], (b, m, context_dim), jnp.float32), 'Wq': jax.random.normal(ks[2], (query_dim, inner), jnp.float32) * s_q, 'Wk': jax.random.normal(ks[3], (context_dim, inner), jnp.float32) * s_c, 'Wv': jax.random.normal(ks[4], (context_dim, inner), jnp.float32) * s_c, 'Wo': jax.random.normal(ks[5], (inner, query_dim), jnp.float32) * s_i, 'bo': jax.random.normal(ks[6], (query_dim,), jnp.float32) * 0.01}
    _L1_xattn_all = _L1_xattn_setup()
    _L1_xattn_in = {k: v for k, v in _L1_xattn_all.items() if k in ('Wq', 'Wk', 'Wv', 'Wo', 'bo')}
    del _L1_xattn_all

    def _L1_ffn_setup():
        import jax, jax.numpy as jnp
        import numpy as np
        NUM_GROUPS = 2
        EXPERT_CAPACITY = 80
        NUM_SELECTED = 2
        key = jax.random.key(seed)
        k1, k2, k3, k4 = jax.random.split(key, 4)
        B, S, H, E, F = (4, 256, 128, 8, 512)
        return {'input_emb': jax.random.normal(k1, (B, S, H), dtype=jnp.float32), 'w_router': jax.random.normal(k2, (H, E), dtype=jnp.float32) * 0.02, 'wi': jax.random.normal(k3, (E, H, F), dtype=jnp.float32) * 0.02, 'wo': jax.random.normal(k4, (E, F, H), dtype=jnp.float32) * 0.02}
    _L1_ffn_all = _L1_ffn_setup()
    _L1_ffn_in = {k: v for k, v in _L1_ffn_all.items() if k in ('w_router', 'wi', 'wo')}
    del _L1_ffn_all

    def _L2_attn_setup():
        import jax, jax.numpy as jnp
        import numpy as np
        EPS = 1e-05

        def layer_norm(x, w, b):
            mu = jnp.mean(x, axis=-1, keepdims=True)
            var = jnp.var(x, axis=-1, keepdims=True)
            return (x - mu) / jnp.sqrt(var + EPS) * w + b
        key = jax.random.key(seed)
        B, N, C = (4, 512, 128)
        H = 16
        MW = 4 * C
        ks = jax.random.split(key, 8)
        s = 0.02
        return {'x': jax.random.normal(ks[0], (B, N, C), dtype=jnp.float32), 'ln1_w': jnp.ones((C,), jnp.float32), 'ln1_b': jnp.zeros((C,), jnp.float32), 'q_w': jax.random.normal(ks[1], (C, C), jnp.float32) * s, 'q_b': jnp.zeros((C,), jnp.float32), 'k_w': jax.random.normal(ks[2], (C, C), jnp.float32) * s, 'k_b': jnp.zeros((C,), jnp.float32), 'v_w': jax.random.normal(ks[3], (C, C), jnp.float32) * s, 'v_b': jnp.zeros((C,), jnp.float32), 'o_w': jax.random.normal(ks[4], (C, C), jnp.float32) * s, 'o_b': jnp.zeros((C,), jnp.float32), 'ln2_w': jnp.ones((C,), jnp.float32), 'ln2_b': jnp.zeros((C,), jnp.float32), 'fc_w': jax.random.normal(ks[5], (MW, C), jnp.float32) * s, 'fc_b': jnp.zeros((MW,), jnp.float32), 'proj_w': jax.random.normal(ks[6], (C, MW), jnp.float32) * s, 'proj_b': jnp.zeros((C,), jnp.float32)}
    _L2_attn_all = _L2_attn_setup()
    _L2_attn_in = {k: v for k, v in _L2_attn_all.items() if k in ('ln1_w', 'ln1_b', 'q_w', 'q_b', 'k_w', 'k_b', 'v_w', 'v_b', 'o_w', 'o_b', 'ln2_w', 'ln2_b', 'fc_w', 'fc_b', 'proj_w', 'proj_b')}
    del _L2_attn_all

    def _L2_xattn_setup():
        import jax, jax.numpy as jnp
        import numpy as np
        DIM_IN, DIM_LAT, DIM_HEAD = (96, 128, 64)
        INNER = max(DIM_LAT, DIM_IN)
        HEADS = INNER // DIM_HEAD
        SCALE = DIM_HEAD ** (-0.5)
        RMS_EPS = 1e-08
        LN_EPS = 1e-05

        def layernorm(x, g, b):
            mu = jnp.mean(x, axis=-1, keepdims=True)
            var = jnp.mean((x - mu) ** 2, axis=-1, keepdims=True)
            return (x - mu) * jax.lax.rsqrt(var + LN_EPS) * g + b

        def rmsnorm(x, gamma):
            norm = jnp.sqrt(jnp.sum(x * x, axis=-1, keepdims=True)) * x.shape[-1] ** (-0.5)
            return x / jnp.maximum(norm, RMS_EPS) * gamma
        key = jax.random.key(seed)
        ks = jax.random.split(key, 12)
        b, n, m = (4, 512, 64)
        x = jax.random.normal(ks[0], (b, n, DIM_IN), jnp.float32)
        latents = jax.random.normal(ks[1], (b, m, DIM_LAT), jnp.float32)
        mask = jax.random.randint(ks[2], (b, n), 0, 2).astype(bool)
        s = lambda k, sh, fan: jax.random.normal(k, sh, jnp.float32) * fan ** (-0.5)
        return {'x': x, 'latents': latents, 'mask': mask, 'ln_x_g': jnp.ones((DIM_IN,), jnp.float32), 'ln_x_b': jnp.zeros((DIM_IN,), jnp.float32), 'ln_l_g': jnp.ones((DIM_LAT,), jnp.float32), 'ln_l_b': jnp.zeros((DIM_LAT,), jnp.float32), 'qn_g': jnp.ones((DIM_HEAD,), jnp.float32), 'kn_g': jnp.ones((DIM_HEAD,), jnp.float32), 'Wq': s(ks[3], (INNER, DIM_LAT), DIM_LAT), 'Wkv': s(ks[4], (2 * INNER, DIM_IN), DIM_IN), 'Wlkv': s(ks[5], (2 * INNER, DIM_LAT), DIM_LAT), 'Wo': s(ks[6], (DIM_LAT, INNER), INNER), 'bo': jnp.zeros((DIM_LAT,), jnp.float32)}
    _L2_xattn_all = _L2_xattn_setup()
    _L2_xattn_in = {k: v for k, v in _L2_xattn_all.items() if k in ('ln_x_g', 'ln_x_b', 'ln_l_g', 'ln_l_b', 'qn_g', 'kn_g', 'Wq', 'Wkv', 'Wlkv', 'Wo', 'bo')}
    del _L2_xattn_all

    def _L2_ffn_setup():
        import jax, jax.numpy as jnp
        import numpy as np
        E, D, H = (8, 128, 512)
        B, S = (4, 512)
        TEMPERATURE = 1.0
        key = jax.random.key(seed)
        ks = jax.random.split(key, 7)
        sc = 0.02
        return {'x': jax.random.normal(ks[0], (B, S, D), dtype=jnp.float32), 'W1': jax.random.normal(ks[1], (E, D, H), dtype=jnp.float32) * sc, 'b1': jax.random.normal(ks[2], (E, H), dtype=jnp.float32) * sc, 'W2': jax.random.normal(ks[3], (E, H, D), dtype=jnp.float32) * sc, 'b2': jax.random.normal(ks[4], (E, D), dtype=jnp.float32) * sc, 'Wr': jax.random.normal(ks[5], (D, E), dtype=jnp.float32) * sc, 'br': jax.random.normal(ks[6], (E,), dtype=jnp.float32) * sc}
    _L2_ffn_all = _L2_ffn_setup()
    _L2_ffn_in = {k: v for k, v in _L2_ffn_all.items() if k in ('W1', 'b1', 'W2', 'b2', 'Wr', 'br')}
    del _L2_ffn_all

    def _L3_attn_setup():
        import jax, jax.numpy as jnp
        import numpy as np
        N_HEADS = 16
        BLOCK_SIZE = 64
        D_MODEL = 128
        ROUTER_HIDDEN = 128
        NEG_BIG = -1000000000.0
        key = jax.random.key(seed)
        ks = jax.random.split(key, 8)
        B, S, D = (2, 256, D_MODEL)
        s = lambda fan_in: 1.0 / np.sqrt(fan_in)
        return {'x': jax.random.normal(ks[0], (B, S, D), dtype=jnp.float32), 'w_qkv': jax.random.normal(ks[1], (3 * D, D), dtype=jnp.float32) * s(D), 'w_r1': jax.random.normal(ks[2], (ROUTER_HIDDEN, D), dtype=jnp.float32) * s(D), 'b_r1': jnp.zeros((ROUTER_HIDDEN,), dtype=jnp.float32), 'w_r2': jax.random.normal(ks[3], (1, ROUTER_HIDDEN), dtype=jnp.float32) * s(ROUTER_HIDDEN), 'b_r2': jnp.zeros((1,), dtype=jnp.float32), 'w_out': jax.random.normal(ks[4], (D, D), dtype=jnp.float32) * s(D), 'b_out': jnp.zeros((D,), dtype=jnp.float32)}
    _L3_attn_all = _L3_attn_setup()
    _L3_attn_in = {k: v for k, v in _L3_attn_all.items() if k in ('w_qkv', 'w_r1', 'b_r1', 'w_r2', 'b_r2', 'w_out', 'b_out')}
    del _L3_attn_all

    def _L3_xattn_setup():
        import jax, jax.numpy as jnp
        import numpy as np
        DIM = 128
        CTX_DIM = 96
        HEADS = 16
        key = jax.random.key(seed)
        ks = jax.random.split(key, 7)
        B, N, M = (4, 512, 32)
        x = jax.random.normal(ks[0], (B, N, DIM), dtype=jnp.float32)
        context = jax.random.normal(ks[1], (B, M, CTX_DIM), dtype=jnp.float32)
        context_mask = jnp.ones((B, M), dtype=bool)
        s_d = 1.0 / np.sqrt(DIM)
        s_c = 1.0 / np.sqrt(CTX_DIM)
        Wq = jax.random.normal(ks[2], (DIM, DIM), dtype=jnp.float32) * s_d
        Wk = jax.random.normal(ks[3], (CTX_DIM, DIM), dtype=jnp.float32) * s_c
        Wv = jax.random.normal(ks[4], (CTX_DIM, DIM), dtype=jnp.float32) * s_c
        Wo = jax.random.normal(ks[5], (DIM, DIM), dtype=jnp.float32) * s_d
        return {'x': x, 'context': context, 'context_mask': context_mask, 'Wq': Wq, 'Wk': Wk, 'Wv': Wv, 'Wo': Wo}
    _L3_xattn_all = _L3_xattn_setup()
    _L3_xattn_in = {k: v for k, v in _L3_xattn_all.items() if k in ('Wq', 'Wk', 'Wv', 'Wo')}
    del _L3_xattn_all

    def _L3_ffn_setup():
        import jax, jax.numpy as jnp
        import numpy as np
        HIDDEN = 128
        INNER = 512

        def _weight_quant(w):
            scale = 1.0 / jnp.clip(jnp.mean(jnp.abs(w)), 1e-05)
            wq = jnp.clip(jnp.round(w * scale), -1.0, 1.0) / scale
            return w + jax.lax.stop_gradient(wq - w)

        def _act_quant(x):
            scale = 127.0 / jnp.clip(jnp.max(jnp.abs(x), axis=-1, keepdims=True), 1e-05)
            xq = jnp.clip(jnp.round(x * scale), -128.0, 127.0) / scale
            return x + jax.lax.stop_gradient(xq - x)

        def _bitlinear(x, w):
            return jnp.einsum('bsi,oi->bso', _act_quant(x), _weight_quant(w))
        key = jax.random.key(seed)
        k0, k1, k2, k3 = jax.random.split(key, 4)
        x = jax.random.normal(k0, (4, 256, HIDDEN), dtype=jnp.float32)
        w_gate = jax.random.normal(k1, (INNER, HIDDEN), dtype=jnp.float32) / np.sqrt(HIDDEN)
        w_up = jax.random.normal(k2, (INNER, HIDDEN), dtype=jnp.float32) / np.sqrt(HIDDEN)
        w_down = jax.random.normal(k3, (HIDDEN, INNER), dtype=jnp.float32) / np.sqrt(INNER)
        return {'x': x, 'w_gate': w_gate, 'w_up': w_up, 'w_down': w_down}
    _L3_ffn_all = _L3_ffn_setup()
    _L3_ffn_in = {k: v for k, v in _L3_ffn_all.items() if k in ('w_gate', 'w_up', 'w_down')}
    del _L3_ffn_all
    return {'x': x, 'ctx_768': ctx_768, 'mask_BxS2_bk0': mask_BxS2_bk0, 'mask_BxS2_bf1': mask_BxS2_bf1, 'L0_attn_A_log': _L0_attn_in['A_log'], 'L0_attn_WB': _L0_attn_in['WB'], 'L0_attn_WC': _L0_attn_in['WC'], 'L0_attn_D': _L0_attn_in['D'], 'L0_attn_Wg': _L0_attn_in['Wg'], 'L0_attn_bg': _L0_attn_in['bg'], 'L0_attn_Wout': _L0_attn_in['Wout'], 'L0_attn_bout': _L0_attn_in['bout'], 'L0_attn_gamma': _L0_attn_in['gamma'], 'L0_attn_beta': _L0_attn_in['beta'], 'L0_xattn_Wq': _L0_xattn_in['Wq'], 'L0_xattn_Wk': _L0_xattn_in['Wk'], 'L0_xattn_Wv': _L0_xattn_in['Wv'], 'L0_xattn_Wo': _L0_xattn_in['Wo'], 'L0_ffn_k0': _L0_ffn_in['k0'], 'L0_ffn_k1': _L0_ffn_in['k1'], 'L0_ffn_k2': _L0_ffn_in['k2'], 'L0_ffn_s0': _L0_ffn_in['s0'], 'L0_ffn_s1': _L0_ffn_in['s1'], 'L0_ffn_s2': _L0_ffn_in['s2'], 'L1_attn_Wk': _L1_attn_in['Wk'], 'L1_attn_bk': _L1_attn_in['bk'], 'L1_attn_Wv': _L1_attn_in['Wv'], 'L1_attn_bv': _L1_attn_in['bv'], 'L1_attn_ln_g': _L1_attn_in['ln_g'], 'L1_attn_ln_b': _L1_attn_in['ln_b'], 'L1_attn_Wo': _L1_attn_in['Wo'], 'L1_attn_bo': _L1_attn_in['bo'], 'L1_xattn_Wq': _L1_xattn_in['Wq'], 'L1_xattn_Wk': _L1_xattn_in['Wk'], 'L1_xattn_Wv': _L1_xattn_in['Wv'], 'L1_xattn_Wo': _L1_xattn_in['Wo'], 'L1_xattn_bo': _L1_xattn_in['bo'], 'L1_ffn_w_router': _L1_ffn_in['w_router'], 'L1_ffn_wi': _L1_ffn_in['wi'], 'L1_ffn_wo': _L1_ffn_in['wo'], 'L2_attn_ln1_w': _L2_attn_in['ln1_w'], 'L2_attn_ln1_b': _L2_attn_in['ln1_b'], 'L2_attn_q_w': _L2_attn_in['q_w'], 'L2_attn_q_b': _L2_attn_in['q_b'], 'L2_attn_k_w': _L2_attn_in['k_w'], 'L2_attn_k_b': _L2_attn_in['k_b'], 'L2_attn_v_w': _L2_attn_in['v_w'], 'L2_attn_v_b': _L2_attn_in['v_b'], 'L2_attn_o_w': _L2_attn_in['o_w'], 'L2_attn_o_b': _L2_attn_in['o_b'], 'L2_attn_ln2_w': _L2_attn_in['ln2_w'], 'L2_attn_ln2_b': _L2_attn_in['ln2_b'], 'L2_attn_fc_w': _L2_attn_in['fc_w'], 'L2_attn_fc_b': _L2_attn_in['fc_b'], 'L2_attn_proj_w': _L2_attn_in['proj_w'], 'L2_attn_proj_b': _L2_attn_in['proj_b'], 'L2_xattn_ln_x_g': _L2_xattn_in['ln_x_g'], 'L2_xattn_ln_x_b': _L2_xattn_in['ln_x_b'], 'L2_xattn_ln_l_g': _L2_xattn_in['ln_l_g'], 'L2_xattn_ln_l_b': _L2_xattn_in['ln_l_b'], 'L2_xattn_qn_g': _L2_xattn_in['qn_g'], 'L2_xattn_kn_g': _L2_xattn_in['kn_g'], 'L2_xattn_Wq': _L2_xattn_in['Wq'], 'L2_xattn_Wkv': _L2_xattn_in['Wkv'], 'L2_xattn_Wlkv': _L2_xattn_in['Wlkv'], 'L2_xattn_Wo': _L2_xattn_in['Wo'], 'L2_xattn_bo': _L2_xattn_in['bo'], 'L2_ffn_W1': _L2_ffn_in['W1'], 'L2_ffn_b1': _L2_ffn_in['b1'], 'L2_ffn_W2': _L2_ffn_in['W2'], 'L2_ffn_b2': _L2_ffn_in['b2'], 'L2_ffn_Wr': _L2_ffn_in['Wr'], 'L2_ffn_br': _L2_ffn_in['br'], 'L3_attn_w_qkv': _L3_attn_in['w_qkv'], 'L3_attn_w_r1': _L3_attn_in['w_r1'], 'L3_attn_b_r1': _L3_attn_in['b_r1'], 'L3_attn_w_r2': _L3_attn_in['w_r2'], 'L3_attn_b_r2': _L3_attn_in['b_r2'], 'L3_attn_w_out': _L3_attn_in['w_out'], 'L3_attn_b_out': _L3_attn_in['b_out'], 'L3_xattn_Wq': _L3_xattn_in['Wq'], 'L3_xattn_Wk': _L3_xattn_in['Wk'], 'L3_xattn_Wv': _L3_xattn_in['Wv'], 'L3_xattn_Wo': _L3_xattn_in['Wo'], 'L3_ffn_w_gate': _L3_ffn_in['w_gate'], 'L3_ffn_w_up': _L3_ffn_in['w_up'], 'L3_ffn_w_down': _L3_ffn_in['w_down']}

def reference(x, ctx_768, mask_BxS2_bk0, mask_BxS2_bf1, L0_attn_A_log, L0_attn_WB, L0_attn_WC, L0_attn_D, L0_attn_Wg, L0_attn_bg, L0_attn_Wout, L0_attn_bout, L0_attn_gamma, L0_attn_beta, L0_xattn_Wq, L0_xattn_Wk, L0_xattn_Wv, L0_xattn_Wo, L0_ffn_k0, L0_ffn_k1, L0_ffn_k2, L0_ffn_s0, L0_ffn_s1, L0_ffn_s2, L1_attn_Wk, L1_attn_bk, L1_attn_Wv, L1_attn_bv, L1_attn_ln_g, L1_attn_ln_b, L1_attn_Wo, L1_attn_bo, L1_xattn_Wq, L1_xattn_Wk, L1_xattn_Wv, L1_xattn_Wo, L1_xattn_bo, L1_ffn_w_router, L1_ffn_wi, L1_ffn_wo, L2_attn_ln1_w, L2_attn_ln1_b, L2_attn_q_w, L2_attn_q_b, L2_attn_k_w, L2_attn_k_b, L2_attn_v_w, L2_attn_v_b, L2_attn_o_w, L2_attn_o_b, L2_attn_ln2_w, L2_attn_ln2_b, L2_attn_fc_w, L2_attn_fc_b, L2_attn_proj_w, L2_attn_proj_b, L2_xattn_ln_x_g, L2_xattn_ln_x_b, L2_xattn_ln_l_g, L2_xattn_ln_l_b, L2_xattn_qn_g, L2_xattn_kn_g, L2_xattn_Wq, L2_xattn_Wkv, L2_xattn_Wlkv, L2_xattn_Wo, L2_xattn_bo, L2_ffn_W1, L2_ffn_b1, L2_ffn_W2, L2_ffn_b2, L2_ffn_Wr, L2_ffn_br, L3_attn_w_qkv, L3_attn_w_r1, L3_attn_b_r1, L3_attn_w_r2, L3_attn_b_r2, L3_attn_w_out, L3_attn_b_out, L3_xattn_Wq, L3_xattn_Wk, L3_xattn_Wv, L3_xattn_Wo, L3_ffn_w_gate, L3_ffn_w_up, L3_ffn_w_down):
    import jax
    import jax.numpy as jnp

    def _L0_attn_ref(x, A_log, WB, WC, D, Wg, bg, Wout, bout, gamma, beta):
        import jax, jax.numpy as jnp
        import numpy as np
        B, T, H, S = (4, 512, 128, 64)
        LN_EPS = 1e-05

        def _reference_tuple_inner(x, A_log, WB, WC, D, Wg, bg, Wout, bout, gamma, beta):
            A = jnp.exp(A_log)
            gate = jax.nn.sigmoid(jnp.einsum('bth,sh->bts', x, Wg) + bg)
            Bx = jnp.einsum('bth,sh->bts', x, WB)
            u = gate * Bx

            def step(state, u_t):
                state = A * state + u_t
                return (state, state)
            s0 = jnp.zeros((x.shape[0], A.shape[0]), x.dtype)
            final_state, states = jax.lax.scan(step, s0, jnp.swapaxes(u, 0, 1))
            states = jnp.swapaxes(states, 0, 1)
            y = jnp.einsum('bts,hs->bth', states, WC) + D * x
            h = y + x
            mu = jnp.mean(h, axis=-1, keepdims=True)
            var = jnp.mean(jnp.square(h - mu), axis=-1, keepdims=True)
            hn = (h - mu) * jax.lax.rsqrt(var + LN_EPS) * gamma + beta
            out = jnp.einsum('bth,oh->bto', hn, Wout) + bout
            return (out, final_state)
        return _reference_tuple_inner(x, A_log, WB, WC, D, Wg, bg, Wout, bout, gamma, beta)[0]

    def _L0_xattn_ref(x, contenoised_img, Wq, Wk, Wv, Wo):
        import jax, jax.numpy as jnp
        import numpy as np
        NUM_HEADS = 16
        EMB_DIM = 128
        CTX_DIM = 96
        D_HEAD = EMB_DIM // NUM_HEADS
        B, SQ, E = x.shape
        SKV = contenoised_img.shape[1]
        q = x @ Wq
        k = contenoised_img @ Wk
        v = contenoised_img @ Wv
        q = q.reshape(B, SQ, NUM_HEADS, D_HEAD).transpose(0, 2, 1, 3)
        k = k.reshape(B, SKV, NUM_HEADS, D_HEAD).transpose(0, 2, 1, 3)
        v = v.reshape(B, SKV, NUM_HEADS, D_HEAD).transpose(0, 2, 1, 3)
        scale = 1.0 / jnp.sqrt(jnp.asarray(D_HEAD, dtype=q.dtype))
        scores = jnp.einsum('bhqd,bhkd->bhqk', q, k) * scale
        weights = jax.nn.softmax(scores, axis=-1)
        out = jnp.einsum('bhqk,bhkd->bhqd', weights, v)
        out = out.transpose(0, 2, 1, 3).reshape(B, SQ, E)
        return out @ Wo

    def _L0_ffn_ref(x, k0, k1, k2, s0, s1, s2):
        import jax, jax.numpy as jnp
        import numpy as np
        import math
        D_IN = 128
        FEATURES = (512, 512, 128)
        BATCH, SEQ = (8, 256)

        def _conn_dense(kernel_bool, x):
            w = jnp.where(kernel_bool, jnp.float32(1.0), jnp.float32(-1.0))
            return x @ w
        h = jnp.concatenate([x, -x], axis=-1)
        h = s0 * _conn_dense(k0, h)
        h = jax.nn.relu(h) * 2
        h = s1 * _conn_dense(k1, h)
        h = jax.nn.relu(h) * 2
        h = s2 * _conn_dense(k2, h)
        return h

    def _L1_attn_ref(x, Wk, bk, Wv, bv, ln_g, ln_b, Wo, bo):
        import jax, jax.numpy as jnp
        import numpy as np
        DIM = 128
        N_QUAT = DIM // 4
        LN_EPS = 1e-05
        NORM_EPS = 1e-12

        def quat_mul(q1, q2):
            r1, i1, j1, k1 = (q1[..., 0], q1[..., 1], q1[..., 2], q1[..., 3])
            r2, i2, j2, k2 = (q2[..., 0], q2[..., 1], q2[..., 2], q2[..., 3])
            r = r1 * r2 - i1 * i2 - j1 * j2 - k1 * k2
            i = r1 * i2 + i1 * r2 + j1 * k2 - k1 * j2
            j = r1 * j2 - i1 * k2 + j1 * r2 + k1 * i2
            k = r1 * k2 + i1 * j2 - j1 * i2 + k1 * r2
            return jnp.stack([r, i, j, k], axis=-1)

        def quat_conj(q):
            return q * jnp.array([1.0, -1.0, -1.0, -1.0], dtype=q.dtype)
        B, L, D = x.shape
        keys = (x @ Wk.T + bk).reshape(B, L, N_QUAT, 4)
        knorm = jnp.linalg.norm(keys, axis=-1, keepdims=True)
        keys = keys / jnp.maximum(knorm, NORM_EPS)
        values = (x @ Wv.T + bv).reshape(B, L, N_QUAT, 4)
        bound = quat_mul(values, keys)
        memory = jnp.cumsum(bound, axis=1)
        retrieved = quat_mul(memory, quat_conj(keys)).reshape(B, L, D)
        positions = jnp.arange(1, L + 1, dtype=x.dtype)
        retrieved = retrieved / jnp.sqrt(positions)[None, :, None]
        mu = jnp.mean(retrieved, axis=-1, keepdims=True)
        var = jnp.var(retrieved, axis=-1, keepdims=True)
        normed = (retrieved - mu) / jnp.sqrt(var + LN_EPS) * ln_g + ln_b
        return x + (normed @ Wo.T + bo)

    def _L1_xattn_ref(x, context, Wq, Wk, Wv, Wo, bo):
        import jax, jax.numpy as jnp
        import numpy as np
        HEADS = 16
        DIM_HEAD = 64
        b, n, _ = x.shape
        h, d = (HEADS, DIM_HEAD)
        scale = d ** (-0.5)
        q = (x @ Wq).reshape(b, n, h, d).transpose(0, 2, 1, 3)
        k = (context @ Wk).reshape(b, -1, h, d).transpose(0, 2, 1, 3)
        v = (context @ Wv).reshape(b, -1, h, d).transpose(0, 2, 1, 3)
        sim = jnp.einsum('bhid,bhjd->bhij', q, k) * scale
        attn = jax.nn.softmax(sim, axis=-1)
        out = jnp.einsum('bhij,bhjd->bhid', attn, v)
        out = out.transpose(0, 2, 1, 3).reshape(b, n, h * d)
        return out @ Wo + bo

    def _L1_ffn_ref(input_emb, w_router, wi, wo):
        import jax, jax.numpy as jnp
        import numpy as np
        NUM_GROUPS = 2
        EXPERT_CAPACITY = 80
        NUM_SELECTED = 2
        B, S, H = input_emb.shape
        E = w_router.shape[1]
        G = NUM_GROUPS
        T = B * S // G
        C = EXPERT_CAPACITY
        K = NUM_SELECTED
        x = input_emb.reshape(G, T, H)
        router_logits = jnp.einsum('gth,he->gte', x.astype(jnp.float32), w_router.astype(jnp.float32))
        router_probs = jax.nn.softmax(router_logits, axis=-1)
        gate, idx = jax.lax.top_k(router_probs, K)
        mask = jax.nn.one_hot(idx, E, dtype=jnp.float32)
        mask_kt = jnp.swapaxes(mask, 1, 2).reshape(G, K * T, E)
        pos = jnp.cumsum(mask_kt, axis=1) * mask_kt - 1.0
        pos = jnp.swapaxes(pos.reshape(G, K, T, E), 1, 2)
        disp_k = jax.nn.one_hot(pos, C, dtype=jnp.float32) * mask[..., None]
        dispatch = disp_k.sum(axis=2)
        combine = jnp.einsum('gtk,gtkec->gtec', gate, disp_k)
        expert_in = jnp.einsum('gtec,gth->egch', dispatch, x)
        h = jax.nn.relu(jnp.einsum('egch,ehf->egcf', expert_in, wi))
        expert_out = jnp.einsum('egcf,efh->egch', h, wo)
        y = jnp.einsum('gtec,egch->gth', combine, expert_out)
        return y.reshape(B, S, H)

    def _L2_attn_ref(x, ln1_w, ln1_b, q_w, q_b, k_w, k_b, v_w, v_b, o_w, o_b, ln2_w, ln2_b, fc_w, fc_b, proj_w, proj_b):
        import jax, jax.numpy as jnp
        import numpy as np
        EPS = 1e-05

        def layer_norm(x, w, b):
            mu = jnp.mean(x, axis=-1, keepdims=True)
            var = jnp.var(x, axis=-1, keepdims=True)
            return (x - mu) / jnp.sqrt(var + EPS) * w + b
        B, N, C = x.shape
        H = 16
        D = C // H
        xn = layer_norm(x, ln1_w, ln1_b)
        q = (xn @ q_w.T + q_b).reshape(B, N, H, D).transpose(0, 2, 1, 3)
        k = (xn @ k_w.T + k_b).reshape(B, N, H, D).transpose(0, 2, 1, 3)
        v = (xn @ v_w.T + v_b).reshape(B, N, H, D).transpose(0, 2, 1, 3)
        q = jax.nn.elu(q) + 1.0
        k = jax.nn.elu(k) + 1.0
        kv = jnp.einsum('bhnd,bhne->bnde', k, v)
        qkv = jnp.einsum('bhnd,bnde->bhne', q, kv)
        k_sum = k.sum(axis=1)
        qk = jnp.einsum('bhnd,bnd->bhn', q, k_sum)
        attn = qkv / qk[..., None]
        attn = attn.transpose(0, 2, 1, 3).reshape(B, N, C)
        attn = attn @ o_w.T + o_b
        x = x + attn
        xn2 = layer_norm(x, ln2_w, ln2_b)
        h = jax.nn.gelu(xn2 @ fc_w.T + fc_b, approximate=False)
        x = x + (h @ proj_w.T + proj_b)
        return x

    def _L2_xattn_ref(x, latents, mask, ln_x_g, ln_x_b, ln_l_g, ln_l_b, qn_g, kn_g, Wq, Wkv, Wlkv, Wo, bo):
        import jax, jax.numpy as jnp
        import numpy as np
        DIM_IN, DIM_LAT, DIM_HEAD = (96, 128, 64)
        INNER = max(DIM_LAT, DIM_IN)
        HEADS = INNER // DIM_HEAD
        SCALE = DIM_HEAD ** (-0.5)
        RMS_EPS = 1e-08
        LN_EPS = 1e-05

        def layernorm(x, g, b):
            mu = jnp.mean(x, axis=-1, keepdims=True)
            var = jnp.mean((x - mu) ** 2, axis=-1, keepdims=True)
            return (x - mu) * jax.lax.rsqrt(var + LN_EPS) * g + b

        def rmsnorm(x, gamma):
            norm = jnp.sqrt(jnp.sum(x * x, axis=-1, keepdims=True)) * x.shape[-1] ** (-0.5)
            return x / jnp.maximum(norm, RMS_EPS) * gamma
        b, n, _ = x.shape
        m = latents.shape[1]
        xn = layernorm(x, ln_x_g, ln_x_b)
        ln = layernorm(latents, ln_l_g, ln_l_b)
        q = ln @ Wq.T
        kv = jnp.concatenate([xn @ Wkv.T, ln @ Wlkv.T], axis=1)
        k, v = (kv[..., :INNER], kv[..., INNER:])
        split_heads = lambda t: t.reshape(t.shape[0], t.shape[1], HEADS, DIM_HEAD).transpose(0, 2, 1, 3)
        q, k, v = (split_heads(q), split_heads(k), split_heads(v))
        qn = rmsnorm(q, qn_g) * SCALE
        kn = rmsnorm(k, kn_g)
        attn = jnp.einsum('bhid,bhjd->bhij', qn, kn)
        full_mask = jnp.pad(mask, ((0, 0), (0, m)), constant_values=True)
        attn = jnp.where(full_mask[:, None, None, :], attn, -jnp.finfo(attn.dtype).max)
        attn = jax.nn.softmax(attn, axis=-1)
        out = jnp.einsum('bhij,bhjd->bhid', attn, v)
        out = out.transpose(0, 2, 1, 3).reshape(b, m, INNER)
        return out @ Wo.T + bo

    def _L2_ffn_ref(x, W1, b1, W2, b2, Wr, br):
        import jax, jax.numpy as jnp
        import numpy as np
        E, D, H = (8, 128, 512)
        B, S = (4, 512)
        TEMPERATURE = 1.0
        routing_logits = (x @ Wr + br) / TEMPERATURE
        routing_probs = jax.nn.softmax(routing_logits, axis=-1)
        indices = jnp.argmax(routing_probs, axis=-1)
        out = jnp.zeros_like(x)
        num_experts = W1.shape[0]
        for i in range(num_experts):
            mask = (indices == i).astype(x.dtype)[..., None]
            xi = x * mask
            h = jax.nn.relu(xi @ W1[i] + b1[i])
            out = out + (h @ W2[i] + b2[i])
        return out

    def _L3_attn_ref(x, w_qkv, w_r1, b_r1, w_r2, b_r2, w_out, b_out):
        import jax, jax.numpy as jnp
        import numpy as np
        N_HEADS = 16
        BLOCK_SIZE = 64
        D_MODEL = 128
        ROUTER_HIDDEN = 128
        NEG_BIG = -1000000000.0
        B, S, D = x.shape
        H, hd, bs = (N_HEADS, D // N_HEADS, BLOCK_SIZE)
        nb = S // bs
        qkv = x @ w_qkv.T
        q, k, v = jnp.split(qkv, 3, axis=-1)
        kp = k
        q = q.reshape(B, S, H, hd).transpose(0, 2, 1, 3)
        k = k.reshape(B, S, H, hd).transpose(0, 2, 1, 3)
        v = v.reshape(B, S, H, hd).transpose(0, 2, 1, 3)
        attn = jnp.einsum('bhqd,bhkd->bhqk', q, k) / jnp.sqrt(jnp.float32(D))
        blk = kp.reshape(B, nb, bs, D).mean(axis=2)
        h1 = jax.nn.relu(blk @ w_r1.T + b_r1)
        score = (h1 @ w_r2.T + b_r2)[..., 0]
        keep_blk = jax.nn.sigmoid(score[0]) > 0.5
        keep_tok = jnp.repeat(keep_blk, bs)
        allowed = keep_tok[:, None] & keep_tok[None, :]
        attn = jnp.where(allowed[None, None], attn, NEG_BIG)
        causal = jnp.triu(jnp.ones((S, S), dtype=bool), k=1)
        attn = jnp.where(causal[None, None], -jnp.inf, attn)
        p = jax.nn.softmax(attn, axis=-1)
        out = jnp.einsum('bhqk,bhkd->bhqd', p, v)
        out = out.transpose(0, 2, 1, 3).reshape(B, S, D)
        return out @ w_out.T + b_out

    def _L3_xattn_ref(x, context, context_mask, Wq, Wk, Wv, Wo):
        import jax, jax.numpy as jnp
        import numpy as np
        DIM = 128
        CTX_DIM = 96
        HEADS = 16
        B, N, _ = x.shape
        M = context.shape[1]
        hd = DIM // HEADS
        scale = hd ** (-0.5)
        q = (x @ Wq).reshape(B, N, HEADS, hd).transpose(0, 2, 1, 3)
        k = (context @ Wk).reshape(B, M, HEADS, hd).transpose(0, 2, 1, 3)
        v = (context @ Wv).reshape(B, M, HEADS, hd).transpose(0, 2, 1, 3)
        scores = jnp.einsum('bhid,bhjd->bhij', q, k) * scale
        max_neg = -jnp.finfo(scores.dtype).max
        scores = jnp.where(context_mask[:, None, None, :], scores, max_neg)
        attn = jax.nn.softmax(scores, axis=-1)
        out = jnp.einsum('bhij,bhjd->bhid', attn, v)
        out = out.transpose(0, 2, 1, 3).reshape(B, N, DIM)
        return out @ Wo

    def _L3_ffn_ref(x, w_gate, w_up, w_down):
        import jax, jax.numpy as jnp
        import numpy as np
        HIDDEN = 128
        INNER = 512

        def _weight_quant(w):
            scale = 1.0 / jnp.clip(jnp.mean(jnp.abs(w)), 1e-05)
            wq = jnp.clip(jnp.round(w * scale), -1.0, 1.0) / scale
            return w + jax.lax.stop_gradient(wq - w)

        def _act_quant(x):
            scale = 127.0 / jnp.clip(jnp.max(jnp.abs(x), axis=-1, keepdims=True), 1e-05)
            xq = jnp.clip(jnp.round(x * scale), -128.0, 127.0) / scale
            return x + jax.lax.stop_gradient(xq - x)

        def _bitlinear(x, w):
            return jnp.einsum('bsi,oi->bso', _act_quant(x), _weight_quant(w))
        gate = jax.nn.silu(_bitlinear(x, w_gate))
        up = _bitlinear(x, w_up)
        return _bitlinear(gate * up, w_down)
    x = _layernorm(x + _L0_attn_ref(x, L0_attn_A_log, L0_attn_WB, L0_attn_WC, L0_attn_D, L0_attn_Wg, L0_attn_bg, L0_attn_Wout, L0_attn_bout, L0_attn_gamma, L0_attn_beta), axis=-1)
    x = _layernorm(x + _L0_xattn_ref(x, ctx_768, L0_xattn_Wq, L0_xattn_Wk, L0_xattn_Wv, L0_xattn_Wo), axis=-1)
    x = _layernorm(x + _L0_ffn_ref(x, L0_ffn_k0, L0_ffn_k1, L0_ffn_k2, L0_ffn_s0, L0_ffn_s1, L0_ffn_s2), axis=-1)
    x = _layernorm(x + _L1_attn_ref(x, L1_attn_Wk, L1_attn_bk, L1_attn_Wv, L1_attn_bv, L1_attn_ln_g, L1_attn_ln_b, L1_attn_Wo, L1_attn_bo), axis=-1)
    x = _layernorm(x + _L1_xattn_ref(x, ctx_768, L1_xattn_Wq, L1_xattn_Wk, L1_xattn_Wv, L1_xattn_Wo, L1_xattn_bo), axis=-1)
    x = _layernorm(x + _L1_ffn_ref(x, L1_ffn_w_router, L1_ffn_wi, L1_ffn_wo), axis=-1)
    x = _layernorm(x + _L2_attn_ref(x, L2_attn_ln1_w, L2_attn_ln1_b, L2_attn_q_w, L2_attn_q_b, L2_attn_k_w, L2_attn_k_b, L2_attn_v_w, L2_attn_v_b, L2_attn_o_w, L2_attn_o_b, L2_attn_ln2_w, L2_attn_ln2_b, L2_attn_fc_w, L2_attn_fc_b, L2_attn_proj_w, L2_attn_proj_b), axis=-1)
    x = _layernorm(x + _L2_xattn_ref(ctx_768, x, mask_BxS2_bk0, L2_xattn_ln_x_g, L2_xattn_ln_x_b, L2_xattn_ln_l_g, L2_xattn_ln_l_b, L2_xattn_qn_g, L2_xattn_kn_g, L2_xattn_Wq, L2_xattn_Wkv, L2_xattn_Wlkv, L2_xattn_Wo, L2_xattn_bo), axis=-1)
    x = _layernorm(x + _L2_ffn_ref(x, L2_ffn_W1, L2_ffn_b1, L2_ffn_W2, L2_ffn_b2, L2_ffn_Wr, L2_ffn_br), axis=-1)
    x = _layernorm(x + _L3_attn_ref(x, L3_attn_w_qkv, L3_attn_w_r1, L3_attn_b_r1, L3_attn_w_r2, L3_attn_b_r2, L3_attn_w_out, L3_attn_b_out), axis=-1)
    x = _layernorm(x + _L3_xattn_ref(x, ctx_768, mask_BxS2_bf1, L3_xattn_Wq, L3_xattn_Wk, L3_xattn_Wv, L3_xattn_Wo), axis=-1)
    x = _layernorm(x + _L3_ffn_ref(x, L3_ffn_w_gate, L3_ffn_w_up, L3_ffn_w_down), axis=-1)
    return x

_drawn_inputs = setup_inputs


def setup_inputs(seed=0):
    import zlib

    import numpy as np

    out = dict(_drawn_inputs(seed))
    spreads = {'L0_attn_gamma': (1.0, 0.2),
     'L0_attn_beta': (0.0, 0.1),
     'L1_attn_bk': (0.0, 0.1),
     'L1_attn_bv': (0.0, 0.1),
     'L1_attn_ln_g': (1.0, 0.2),
     'L1_attn_ln_b': (0.0, 0.1),
     'L1_attn_bo': (0.0, 0.1),
     'L2_attn_ln1_w': (1.0, 0.6),
     'L2_attn_ln1_b': (0.0, 0.8),
     'L2_attn_q_b': (0.0, 0.8),
     'L2_attn_k_b': (0.0, 0.8),
     'L2_attn_v_b': (0.0, 0.8),
     'L2_attn_o_b': (0.0, 0.1),
     'L2_attn_ln2_w': (1.0, 0.6),
     'L2_attn_ln2_b': (0.0, 2.0),
     'L2_attn_fc_b': (0.0, 0.578),
     'L2_attn_proj_b': (0.0, 0.1),
     'L2_xattn_ln_x_g': (1.0, 0.6),
     'L2_xattn_ln_x_b': (0.0, 0.8),
     'L2_xattn_ln_l_g': (1.0, 0.2),
     'L2_xattn_ln_l_b': (0.0, 0.1),
     'L2_xattn_qn_g': (1.0, 0.6),
     'L2_xattn_kn_g': (1.0, 0.6),
     'L2_xattn_bo': (0.0, 0.1),
     'L3_attn_b_r1': (0.0, 0.1),
     'L3_attn_b_out': (0.0, 0.1)}
    factors = {'L0_attn_A_log': 5.312,
     'L0_attn_Wg': 4.782,
     'L0_attn_bg': 8.0,
     'L1_xattn_bo': 4.652,
     'L1_ffn_w_router': 8.0,
     'L1_ffn_wi': 8.0,
     'L1_ffn_wo': 8.0,
     'L2_attn_q_w': 8.0,
     'L2_attn_k_w': 8.0,
     'L2_attn_v_w': 8.0,
     'L2_attn_o_w': 7.544,
     'L2_xattn_Wkv': 3.038,
     'L2_ffn_b1': 4.097,
     'L2_ffn_br': 4.319,
     'L3_attn_w_r2': 3.573}
    for name, (base, spread) in spreads.items():
        noise = np.random.default_rng([zlib.crc32(name.encode()), seed]).standard_normal(out[name].shape)
        drawn = base * np.exp(spread * noise) if base else spread * noise
        out[name] = jnp.asarray(drawn.astype(out[name].dtype))
    for name, factor in factors.items():
        out[name] = (out[name] * factor).astype(out[name].dtype)
    return out
```

```python
from contextlib import ExitStack

import concourse.bass as bass
from concourse import mybir

F32 = mybir.dt.float32
BF16 = mybir.dt.bfloat16
U8 = mybir.dt.uint8
ALU = mybir.AluOpType
ACT = mybir.ActivationFunctionType
AX = mybir.AxisListType

B, T, D = 4, 512, 128
LANES = (0, 1)
P = 128
NT = T // P
CTX, CD = 77, 96
H = 16
DH = D // H
DW = 64
EPS = 1e-5
E = 8
FF = 512
FC = FF // P
CAP = 80
FAR = 1e30
NEVER = 3e38
ROUND = 12582912.0

WEIGHTS = {
    "L0": [("gate", 64), ("inB", 64), ("Wout", 128), ("q0", 128), ("o0", 128)],
    "L1": [("k1", 128), ("v1", 128), ("o1", 128), ("xq1", 1024), ("xo1", 1024), ("router1", 8)],
    "L1wi": [("wi", E * FF)],
    "L1wo": [("wo", E * FF)],
    "L2": [("qkv2", 384), ("o2", 128), ("fc", 512), ("proj", 512),
           ("xqkv2", 384), ("xo2", 128), ("router2", 8)],
    "L2w1": [("W1", E * FF)],
    "L2w2": [("W2", E * FF)],
    "L3": [("q3", 512), ("k3", 512), ("v3", 128), ("r1", 512), ("r2", 128), ("o3", 128),
           ("xq3", 128), ("xo3", 128), ("wgate", 512), ("wup", 512), ("wdown", 512)],
}
CTX_WEIGHTS = [("k0", 128), ("v0", 128), ("xk1", 1024), ("xv1", 1024), ("xkv2", 256),
               ("xk3", 128), ("xv3", 128)]
VECTORS = [("bg", 1), ("A_log", 1), ("D", 1), ("gamma", 1), ("beta", 1), ("bout", 1),
           ("s0", 1), ("s1", 1), ("s2", 1), ("ln_g", 1), ("ln_b", 1), ("bo1", 1), ("xbo1", 1),
           ("ln1_w", 1), ("ln1_b", 1), ("o_b", 1), ("ln2_w", 1), ("ln2_b", 1), ("fc_b", FC),
           ("proj_b", 1), ("ln_x_g", 1), ("ln_x_b", 1), ("ln_l_g", 1), ("ln_l_b", 1),
           ("qn_g", 1), ("kn_g", 1), ("xbo2", 1), ("b1", E * FC), ("b2", E),
           ("b_r1", 1), ("b_r2", 1), ("b_out", 1)]
ROWS = [("bk1", 128), ("bv1", 128), ("bqkv2", 384), ("br", 8)]
CONSTS = [("ident", P), ("tri", P), ("ones", P), ("headmask", H), ("rpos", NT), ("slot", CAP),
          ("down8", E), ("causal", P), ("low", 1), ("high", 1), ("restart", 16 * E)]


def places(columns):
    at, out = 0, {}
    for name, n in columns:
        out[name] = (at, at + n)
        at += n
    return out, at


class Chain:

    def __init__(self, eng, sem):
        self.eng, self.sem, self.n = eng, sem, 0

    def mark(self, ins):
        self.n += 1
        ins.then_inc(self.sem, 1)
        return self.n

    def wait(self, n):
        self.eng.wait_ge(self.sem, n)

    def link(self, ins):
        self.wait(self.mark(ins))


def rep(ap, axis, n):
    ap = ap.unsqueeze(axis)
    shape = list(ap.shape)
    shape[axis] = n
    return ap.broadcast_to(shape)


class Net:

    def __init__(self, nc, stack, dram):
        self.nc, self.stack, self.dram = nc, stack, dram
        self.w, self.loaded, self.group = {}, {}, {}
        self.layer_no = 0
        for group, columns in WEIGHTS.items():
            self.hold(group, columns, P)
        self.hold("ctxw", CTX_WEIGHTS, CD)
        self.hold("vec", VECTORS, P)
        self.hold("rows", ROWS, P)
        self.hold("const", CONSTS, P)
        self.hold("WC", [("WC", D)], 64)
        self.raw0 = self.sb("signs0_raw", [P, 2, FF], U8)
        self.raw1 = self.sb("signs1_raw", [P, FC, FF], U8)
        self.raw2 = self.sb("signs2_raw", [P, FC, D], U8)
        self.signs0 = self.sb("signs0", [P, FF])
        self.signs1 = self.sb("signs1", [P, FC, FF])
        self.signs2 = self.sb("signs2", [P, FC, D])
        self.signs_loaded = self.sem("signs_loaded")
        self.ps = [stack.enter_context(nc.psum_tensor(f"psum_lane{j}", [P, 4, 512], F32)) for j in LANES]
        self.X = [self.sb(f"X{j}", [P, NT, D]) for j in LANES]
        self.XT = [self.sb(f"XT{j}", [P, T]) for j in LANES]
        self.ctxT = [self.sb(f"ctxT{j}", [CD, CTX]) for j in LANES]
        self.ctx = [self.sb(f"ctx{j}", [CTX, CD]) for j in LANES]
        self.maskrow = [[self.sb(f"mask_row{m}{j}", [1, CTX], U8) for j in LANES] for m in (0, 1)]
        self.half = self.sb("minus_half", [P, 512])
        self.one16 = self.sb("ones_bf16", [1, P], BF16)
        self.ident16 = self.sb("ident_bf16", [P, P], BF16)
        self.tri16 = self.sb("tri_bf16", [P, P], BF16)
        self.ones16 = self.sb("all_ones_bf16", [P, P], BF16)
        self.first_pair = self.sb("first_pair", [P, 1])
        self.keep8 = self.sb("keep_block", [P, 8])
        self.pool = [stack.enter_context(nc.semaphore(f"step{i}")) for i in range(40)]
        nums = sorted(s.num for s in self.pool)
        assert nums[-1] - nums[0] == len(nums) - 1
        self.pool_range = range(nums[0], nums[-1] + 1)

    def sb(self, name, shape, dtype=F32):
        return self.stack.enter_context(self.nc.sbuf_tensor(name, shape, dtype))

    def sem(self, name):
        return self.stack.enter_context(self.nc.semaphore(name))

    def hold(self, group, columns, rows):
        where, n = places(columns)
        tile = self.sb("in_" + group, [rows, n])
        self.loaded[group] = self.sem("loaded_" + group)
        self.group[group] = tile
        for name, (a, b) in where.items():
            self.w[name] = tile[:, a:b]

    def signals(self, names):
        names = names.split()
        assert len(names) <= len(self.pool) and len(set(names)) == len(names)
        return dict(zip(names, self.pool))

    def have(self, eng, *groups):
        for group in groups:
            eng.wait_ge(self.loaded[group], 16)

    def scratch(self):
        self.layer = ExitStack()
        self.layer_no = self.layer_no + 1
        return self.layer

    def tmp(self, name, shape, dtype=F32):
        return self.layer.enter_context(self.nc.sbuf_tensor(f"{name}_{self.layer_no}", shape, dtype))

    def close(self):
        self.nc.sync.sem_clear(self.pool_range)
        self.nc.all_engine_barrier(sem_only=True)



LN_SIGNALS = " ln_var ln_rs"


def vector_layernorm(k, dve, c, S, src, out, st, done, n_rows=P, tiles=NT, lanes=LANES, base=0):
    last = {}
    for j in lanes:
        for t in range(tiles):
            ins = dve.bn_stats(st[j][0:n_rows, t, 0:6], src(j, t))
        last[j] = c.mark(ins)
    for j in lanes:
        c.wait(last[j])
        for t in range(tiles):
            ins = dve.bn_aggr(st[j][0:n_rows, t, 6:8], st[j][0:n_rows, t, 0:6])
        last[j] = c.mark(ins)
    for j in lanes:
        c.wait(last[j])
        dve.tensor_scalar(st[j][0:n_rows, 0:tiles, 8], st[j][0:n_rows, 0:tiles, 7], EPS, None,
                          ALU.add).then_inc(S["ln_var"], 1)
    for i, j in enumerate(lanes):
        dve.wait_ge(S["ln_rs"], base + i + 1)
        for t in range(tiles):
            ins = dve.tensor_scalar(out(j, t), src(j, t), st[j][0:n_rows, t, 6:7],
                                    st[j][0:n_rows, t, 9:10], ALU.subtract, ALU.mult)
        ins.then_inc(S[done], 1)


def pool_layernorm(k, pool, S, st, n_rows=P, tiles=NT, lanes=LANES, base=0):
    for i, j in enumerate(lanes):
        pool.wait_ge(S["ln_var"], base + i + 1)
        pool.tensor_tensor(st[j][0:n_rows, 0:tiles, 9], st[j][0:n_rows, 0:tiles, 8],
                           k.half[0:n_rows, 0:tiles], ALU.pow).then_inc(S["ln_rs"], 1)


TAIL_SIGNALS = " tail_yT_sb tail_y tail_x tail_xT"


class Tail:

    def __init__(self, k, S, st, base=0, via=None, ready=None, bias=None, bank=3, yT=None,
                 bank_x=2, x_factor=1.0, y_scale=None, y_at=("tail_y", 1, 0), tile_scale=None, ready_from=0):
        self.k, self.S, self.st, self.base, self.via = k, S, st, base, via
        self.ready, self.bias, self.bank, self.yT = ready, bias, bank, yT
        self.bank_x, self.x_factor, self.y_scale = bank_x, x_factor, y_scale
        self.ready_from = ready_from
        self.tile_scale = tile_scale
        self.y_at = y_at
        self.Y = ([v[:, 0:T].rearrange("p (t n) -> p t n", t=NT) for v in yT] if yT is not None else
                  [k.tmp(f"tail_y{j}", [P, NT, D])[:, :, :] for j in LANES])

    def scalar(self, act):
        k, S = self.k, self.S
        if self.via is not None:
            for j in LANES:
                act.wait_ge(S[self.ready], self.ready_from + j + 1)
                act.activation(self.yT[j][:, 0:T], k.ps[j][:, self.via, :], ACT.Identity,
                               bias=self.bias, scale=1.0).then_inc(S["tail_yT_sb"], 1)
        for j in LANES:
            act.wait_ge(S["tail_xT"], j + 1)
            act.activation(k.XT[j][:, :], k.ps[j][:, self.bank_x, :], ACT.Copy)

    def tensor(self, pe):
        k, S = self.k, self.S
        if self.via is not None:
            for j in LANES:
                pe.wait_ge(S["tail_yT_sb"], j + 1)
                for t in range(NT):
                    ins = pe.transpose(k.ps[j][:, self.bank, t * P:(t + 1) * P],
                                       self.yT[j][:, t * P:(t + 1) * P], k.w["ident"])
                ins.then_inc(S["tail_y"], 1)
        for j in LANES:
            pe.wait_ge(S["tail_x"], j + 1)
            for t in range(NT):
                ins = pe.transpose(k.ps[j][:, self.bank_x, t * P:(t + 1) * P], k.X[j][:, t, :],
                                   k.w["ident"])
            ins.then_inc(S["tail_xT"], 1)

    def vector(self, dve, c):
        k, S = self.k, self.S
        last = {}
        for j in LANES:
            name, each, before = self.y_at
            dve.wait_ge(S[name], before + (j + 1) * each)
            y = k.ps[j][:, self.bank, :]
            x = k.X[j][:, :, :].rearrange("p t n -> p (t n)")
            out = self.Y[j][:, :, :].rearrange("p t n -> p (t n)")
            if self.tile_scale is not None:
                for t in range(NT):
                    ins = dve.scalar_tensor_tensor(out=self.Y[j][:, t, :], in0=y[:, t * P:(t + 1) * P],
                                                   scalar=self.tile_scale[j][:, t:t + 1], in1=k.X[j][:, t, :],
                                                   op0=ALU.mult, op1=ALU.add)
            elif self.y_scale is not None:
                ins = dve.scalar_tensor_tensor(out=out, in0=y, scalar=self.y_scale, in1=x,
                                               op0=ALU.mult, op1=ALU.add)
            else:
                ins = dve.scalar_tensor_tensor(out=out, in0=x, scalar=self.x_factor, in1=y,
                                               op0=ALU.mult, op1=ALU.add)
            last[j] = c.mark(ins)
        for j in LANES:
            c.wait(last[j])
        self.normalise(dve, c)

    def normalise(self, dve, c):
        k, S = self.k, self.S
        last = {}
        for j in LANES:
            for t in range(NT):
                ins = dve.bn_stats(self.st[j][:, t, 0:6], self.Y[j][:, t, :])
            last[j] = c.mark(ins)
        for j in LANES:
            c.wait(last[j])
            for t in range(NT):
                ins = dve.bn_aggr(self.st[j][:, t, 6:8], self.st[j][:, t, 0:6])
            last[j] = c.mark(ins)
        for j in LANES:
            c.wait(last[j])
            dve.tensor_scalar(self.st[j][:, 0:NT, 8], self.st[j][:, 0:NT, 7], EPS, None,
                              ALU.add).then_inc(S["ln_var"], 1)
        for j in LANES:
            dve.wait_ge(S["ln_rs"], self.base + j + 1)
            for t in range(NT):
                ins = dve.tensor_scalar(k.X[j][:, t, :], self.Y[j][:, t, :],
                                        self.st[j][:, t, 6:7], self.st[j][:, t, 9:10],
                                        ALU.subtract, ALU.mult)
            ins.then_inc(S["tail_x"], 1)

    def gpsimd(self, pool):
        pool_layernorm(self.k, pool, self.S, self.st, base=self.base)



def setup(k):
    nc = k.nc
    S = k.signals("filled")
    with nc.Block(no_gpsimd_drain=True) as block:

        @block.sync
        def _(sp):
            for group in ("const", "vec"):
                sp.dma_start(k.group[group][:, :], k.dram[group]).then_inc(k.loaded[group], 16)
            sp.dma_start(k.raw0[:, :, :], k.dram["k0"].rearrange("(a p) n -> p a n", p=P)).then_inc(k.signs_loaded, 16)
            sp.dma_start(k.raw1[:, :, :], k.dram["k1"].rearrange("(a p) n -> p a n", p=P)).then_inc(k.signs_loaded, 16)
            sp.dma_start(k.raw2[:, :, :], k.dram["k2"].rearrange("(a p) n -> p a n", p=P)).then_inc(k.signs_loaded, 16)
            for group in ("L0", "WC", "ctxw", "L1", "rows", "L1wi", "L1wo", "L2", "L2w1", "L2w2", "L3"):
                sp.dma_start(k.group[group][:, :], k.dram[group]).then_inc(k.loaded[group], 16)

        @block.gpsimd
        def _(pool):
            c = Chain(pool, S["filled"])
            c.mark(pool.memset(k.half[:, :], -0.5))
            c.mark(pool.memset(k.one16[:, :], 1.0))
            c.mark(pool.memset(k.first_pair[:, :], 1.0))
            c.mark(pool.memset(k.keep8[:, :], 0.0))
            pool.wait_ge(k.signs_loaded, 48)
            for f in range(FC):
                c.mark(pool.tensor_scalar(k.signs1[:, f, :], k.raw1[:, f, :], 2.0, -1.0, ALU.mult, ALU.add))
            c.wait(c.n)

        @block.vector
        def _(dve):
            k.have(dve, "const", "vec")
            dve.tensor_copy(k.ident16[:, :], k.w["ident"])
            dve.tensor_copy(k.tri16[:, :], k.w["tri"])
            dve.tensor_copy(k.ones16[:, :], k.w["ones"])
            dve.wait_ge(k.signs_loaded, 48)
            dve.tensor_tensor(k.signs0[:, :], k.raw0[:, 0, :], k.raw0[:, 1, :], ALU.subtract)
            dve.tensor_scalar(k.signs2[:, :, :], k.raw2[:, :, :], 2.0, -1.0, ALU.mult, ALU.add)
    k.close()


def load_pair(k, g):
    nc = k.nc
    S = k.signals("x_in xT")
    x, ctx, ctxT = k.dram["x"], k.dram["ctx"], k.dram["ctxT"]
    with nc.Block(no_gpsimd_drain=True) as block:

        @block.sync
        def _(sp):
            for j in LANES:
                b = 2 * g + j
                one = bass.ds(b, 1)
                sp.dma_start(k.X[j][:, :, :], x[one, :, :].rearrange("a (t p) n -> p (a t) n", p=P)).then_inc(S["x_in"], 16)
            for j in LANES:
                one = bass.ds(2 * g + j, 1)
                sp.dma_start(k.ctxT[j][:, :], ctxT[one, :, :].rearrange("a p n -> p (a n)")).then_inc(S["x_in"], 16)
                sp.dma_start(k.ctx[j][:, :], ctx[one, :, :].rearrange("a p n -> p (a n)")).then_inc(S["x_in"], 16)
                for m in (0, 1):
                    sp.dma_start(k.maskrow[m][j][:, :], k.dram[f"mask{m}"][one, :]).then_inc(S["x_in"], 16)
            sp.wait_ge(S["x_in"], 16 * 10)

        @block.tensor
        def _(pe):
            k.have(pe, "const")
            pe.wait_ge(S["x_in"], 16 * 10)
            for j in LANES:
                for t in range(NT):
                    ins = pe.transpose(k.ps[j][:, 2, t * P:(t + 1) * P], k.X[j][:, t, :], k.w["ident"])
                ins.then_inc(S["xT"], 1)

        @block.scalar
        def _(act):
            for j in LANES:
                act.wait_ge(S["xT"], j + 1)
                act.activation(k.XT[j][:, :], k.ps[j][:, 2, :], ACT.Copy)
    k.close()


def store_pair(k, g):
    nc = k.nc
    S = k.signals("stored cleared")
    with nc.Block(no_gpsimd_drain=True) as block:

        @block.sync
        def _(sp):
            for j in LANES:
                out = k.dram["out"][bass.ds(2 * g + j, 1), :, :].rearrange("a (t p) n -> p (a t) n", p=P)
                sp.dma_start(out, k.X[j][:, :, :]).then_inc(S["stored"], 16)
            sp.wait_ge(S["stored"], 32)

        @block.gpsimd
        def _(pool):
            pool.memset(k.first_pair[:, :], 0.0).then_inc(S["cleared"], 1)
            pool.wait_ge(S["cleared"], 1)
    k.close()



def l0_state_space(k):
    nc, w = k.nc, k.w
    S = k.signals("pre gate scanned hT_ps hT h_tok hn hnT_ps hnT y step act_step"
                  + LN_SIGNALS + TAIL_SIGNALS)
    with k.scratch():
        st = [k.tmp(f"stats{j}", [P, NT, 10]) for j in LANES]
        A = k.tmp("A", [64, 1]); negbg = k.tmp("negbg", [64, 1]); D1 = k.tmp("D1", [P, 1])
        u = [k.tmp(f"u{j}", [64, T]) for j in LANES]
        gate = [k.tmp(f"gate{j}", [64, T]) for j in LANES]
        states = [k.tmp(f"states{j}", [64, T]) for j in LANES]
        hT = [k.tmp(f"hT{j}", [P, T]) for j in LANES]
        hn = [k.tmp(f"hn{j}", [P, NT, D]) for j in LANES]
        hnT = [k.tmp(f"hnT{j}", [P, T]) for j in LANES]
        tail = Tail(k, S, st, base=2, via=1, ready="y", bias=w["bout"], yT=hT)
        with nc.Block(no_gpsimd_drain=True) as block:

            @block.tensor
            def _(pe):
                k.have(pe, "L0", "WC", "const")
                for j in LANES:
                    pe.matmul(k.ps[j][0:64, 0, :], w["gate"], k.XT[j][:, :], start=True, stop=True)
                    pe.matmul(k.ps[j][0:64, 1, :], w["inB"], k.XT[j][:, :], start=True,
                              stop=True).then_inc(S["pre"], 1)
                for j in LANES:
                    pe.wait_ge(S["scanned"], j + 1)
                    pe.matmul(k.ps[j][:, 2, :], w["WC"], states[j][:, :], start=True,
                              stop=True).then_inc(S["hT_ps"], 1)
                for j in LANES:
                    pe.wait_ge(S["hT"], j + 1)
                    for t in range(NT):
                        ins = pe.transpose(k.ps[j][:, 0, t * P:(t + 1) * P], hT[j][:, t * P:(t + 1) * P], w["ident"])
                    ins.then_inc(S["h_tok"], 1)
                for j in LANES:
                    pe.wait_ge(S["hn"], j + 1)
                    for t in range(NT):
                        ins = pe.transpose(k.ps[j][:, 2, t * P:(t + 1) * P], hn[j][:, t, :], w["ident"])
                    ins.then_inc(S["hnT_ps"], 1)
                for j in LANES:
                    pe.wait_ge(S["hnT"], j + 1)
                    pe.matmul(k.ps[j][:, 1, :], w["Wout"], hnT[j][:, :], start=True,
                              stop=True).then_inc(S["y"], 1)
                tail.tensor(pe)

            @block.scalar
            def _(act):
                k.have(act, "vec")
                c = Chain(act, S["act_step"])
                act.activation(A[:, :], w["A_log"][0:64, :], ACT.Exp)
                c.link(act.activation(negbg[:, :], w["bg"][0:64, :], ACT.Copy, scale=-1.0))
                for j in LANES:
                    act.wait_ge(S["pre"], j + 1)
                    act.activation(gate[j][:, :], k.ps[j][0:64, 0, :], ACT.Exp, bias=negbg[:, :],
                                   scale=-1.0).then_inc(S["gate"], 1)
                for j in LANES:
                    act.wait_ge(S["hnT_ps"], j + 1)
                    act.activation(hnT[j][:, :], k.ps[j][:, 2, :], ACT.Identity, bias=w["beta"],
                                   scale=w["gamma"]).then_inc(S["hnT"], 1)
                tail.scalar(act)

            @block.vector
            def _(dve):
                k.have(dve, "vec")
                c = Chain(dve, S["step"])
                dve.tensor_scalar(D1[:, :], w["D"], 1.0, None, ALU.add)
                n = {}
                for j in LANES:
                    dve.wait_ge(S["gate"], j + 1)
                    n[j] = c.mark(dve.tensor_scalar(gate[j][:, :], gate[j][:, :], 1.0, None, ALU.add))
                for j in LANES:
                    c.wait(n[j])
                    n[j] = c.mark(dve.reciprocal(gate[j][:, :], gate[j][:, :]))
                for j in LANES:
                    c.wait(n[j])
                    n[j] = c.mark(dve.tensor_tensor(u[j][:, :], gate[j][:, :], k.ps[j][0:64, 1, :], ALU.mult))
                for j in LANES:
                    c.wait(n[j])
                    dve.tensor_tensor_scan(states[j][:, :], A[:, 0:1].broadcast_to([64, T]), u[j][:, :], 0.0,
                                           ALU.mult, ALU.add).then_inc(S["scanned"], 1)
                for j in LANES:
                    dve.wait_ge(S["hT_ps"], j + 1)
                    dve.scalar_tensor_tensor(out=hT[j][:, :], in0=k.XT[j][:, :], scalar=D1[:, :],
                                             in1=k.ps[j][:, 2, :], op0=ALU.mult,
                                             op1=ALU.add).then_inc(S["hT"], 1)
                for j in LANES:
                    dve.wait_ge(S["h_tok"], j + 1)
                vector_layernorm(k, dve, c, S, lambda j, t: k.ps[j][:, 0, t * P:(t + 1) * P],
                                 lambda j, t: hn[j][:, t, :], st, "hn")
                tail.vector(dve, c)

            @block.gpsimd
            def _(pool):
                pool_layernorm(k, pool, S, st)
                tail.gpsimd(pool)
        k.close()



def cross_attention(k, wq, wk, wv, wo, group, wide, bias=None, mask=None):
    nc, w = k.nc, k.w
    HG = 4
    GROUPS = H // HG
    UNITS = 2 * NT * GROUPS
    dh = DW if wide else DH
    inner = H * dh
    KC = inner // P
    VW = dh + 1
    SC = HG * CTX
    scale = float(dh) ** -0.5
    S = k.signals("kT_ps kT kblock v_ps v vones qT_ps qT mask scores less exp pT_ps pT pv attn aT_ps aT y "
                  "step" + LN_SIGNALS + TAIL_SIGNALS)
    with k.scratch():
        st = [k.tmp(f"stats{j}", [P, NT, 10]) for j in LANES]
        kT = [k.tmp(f"kT{j}", [P, KC, CTX]) for j in LANES]
        V = [k.tmp(f"V{j}", [CTX, H, VW]) for j in LANES]
        qT = [k.tmp(f"qT{j}", [P, KC, T]) for j in LANES]
        prob = [k.tmp(f"prob{j}", [P, 2, SC]) for j in LANES]
        pT = [k.tmp(f"pT{j}", [CTX, HG * P]) for j in LANES]
        nmax = [k.tmp(f"nmax{j}", [P, 2, HG]) for j in LANES]
        rsum = [k.tmp(f"rsum{j}", [P, H]) for j in LANES]
        attn = [k.tmp(f"attn{j}", [P, (1 if wide else NT), inner]) for j in LANES]
        aT = qT
        if not wide:
            kblock = [k.tmp(f"kblock{j}", [P, H, CTX]) for j in LANES]
        if mask is not None:
            mrow = [k.tmp(f"mrow{j}", [1, HG, CTX], BF16) for j in LANES]
        yT = [prob[j][:, :, :].rearrange("p a n -> p (a n)") for j in LANES]
        tail = Tail(k, S, st, via=1, ready="y", bias=bias, yT=yT)
        VN = min(512, inner)
        LATE = 5

        def heads(hg):
            if wide:
                return [2 * (HG * (hg // 2) + i) + hg % 2 for i in range(HG)]
            return [HG * hg + i for i in range(HG)]

        def unit(n):
            j, u = n % 2, n // 2
            return j, u, u // GROUPS, u % GROUPS

        with nc.Block(no_gpsimd_drain=True) as block:

            @block.tensor
            def _(pe):
                k.have(pe, group, "ctxw", "const")
                for j in LANES:
                    for c in range(KC):
                        ins = pe.matmul(k.ps[j][:, c // 4, (c % 4) * CTX:(c % 4 + 1) * CTX],
                                        wk[:, c * P:(c + 1) * P], k.ctxT[j][:, :], start=True, stop=True)
                    ins.then_inc(S["kT_ps"], 1)
                    for c in range(inner // VN):
                        ins = pe.matmul(k.ps[j][0:CTX, 2 + c, 0:VN], k.ctxT[j][:, :],
                                        wv[:, c * VN:(c + 1) * VN], start=True, stop=True)
                    ins.then_inc(S["v_ps"], 1)
                for c in range(KC):
                    for j in LANES:
                        if c < 2:
                            pe.wait_ge(S["kT"], j + 1)
                        else:
                            pe.wait_ge(S["qT"], 2 * (c - 2) + j + 1)
                        pe.matmul(k.ps[j][:, c % 2, :], wq[:, c * P:(c + 1) * P], k.XT[j][:, :],
                                  start=True, stop=True).then_inc(S["qT_ps"], 1)
                if not wide:
                    pe.wait_ge(S["kblock"], 2)
                pe.wait_ge(S["qT"], 2 * KC)
                pe.wait_ge(S["v"], 2)
                pe.wait_ge(S["vones"], 2)
                if mask is not None:
                    pe.wait_ge(S["mask"], 2)

                def scores(n):
                    j, u, t, hg = unit(n)
                    if n >= 4:
                        pe.wait_ge(S["less"], n - 3)
                    bank = k.ps[j][:, u % 2, :]
                    if wide:
                        for i, h in enumerate(heads(hg)):
                            r = DW * (h % 2)
                            ins = pe.matmul(bank[:, i * CTX:(i + 1) * CTX],
                                            qT[j][r:r + DW, h // 2, t * P:(t + 1) * P],
                                            kT[j][r:r + DW, h // 2, :], start=True, stop=True)
                    else:
                        ins = pe.matmul(bank[:, 0:SC], qT[j][:, 0, t * P:(t + 1) * P],
                                        kblock[j][:, HG * hg:HG * hg + HG, :].rearrange("p h n -> p (h n)"),
                                        start=True, stop=mask is None)
                        if mask is not None:
                            ins = pe.matmul(bank[:, 0:SC], k.one16[:, :],
                                            mrow[j][:, :, :].rearrange("p h n -> p (h n)"),
                                            start=False, stop=True)
                    ins.then_inc(S["scores"], 1)

                def transposes(n):
                    j, u, t, hg = unit(n)
                    pe.wait_ge(S["exp"], n + 1)
                    if n >= 2:
                        pe.wait_ge(S["pT"], n - 1)
                    for h in range(HG):
                        ins = pe.transpose(k.ps[j][0:CTX, 2, h * P:(h + 1) * P],
                                           prob[j][:, u % 2, h * CTX:(h + 1) * CTX], w["ident"])
                    ins.then_inc(S["pT_ps"], 1)

                def values(n):
                    j, u, t, hg = unit(n)
                    pe.wait_ge(S["pT"], n + 1)
                    if wide and n >= 2:
                        pe.wait_ge(S["attn"], n - 1)
                    if not wide and hg == 0 and t > 0:
                        pe.wait_ge(S["attn"], 2 * (t - 1) + j + 1)
                    for i, h in enumerate(heads(hg)):
                        at = (0 if wide else hg * HG * VW) + i * VW
                        ins = pe.matmul(k.ps[j][:, 3, at:at + VW], pT[j][:, i * P:(i + 1) * P],
                                        V[j][:, h, :], start=True, stop=True)
                    ins.then_inc(S["pv"], 1)

                for n in range(UNITS + LATE):
                    if n < UNITS:
                        scores(n)
                    if 0 <= n - 2 < UNITS:
                        transposes(n - 2)
                    if 0 <= n - 3 < UNITS:
                        values(n - 3)
                    if wide and n >= LATE:
                        j, u, t, hg = unit(n - LATE)
                        if hg == GROUPS - 1 and j == 1:
                            pe.wait_ge(S["attn"], n - LATE + 1)
                            pe.wait_ge(S["pT"], min(n - 1, UNITS))
                            for half in range(2):
                                for jj in LANES:
                                    if half == 1:
                                        pe.wait_ge(S["aT"], 4 * t + jj + 1)
                                    for c in range(4):
                                        f = 4 * half + c
                                        ins = pe.transpose(k.ps[jj][:, 2, c * P:(c + 1) * P],
                                                           attn[jj][:, 0, f * P:(f + 1) * P], w["ident"])
                                    ins.then_inc(S["aT_ps"], 1)
                            pe.wait_ge(S["aT"], 4 * t + 4)
                if not wide:
                    for j in LANES:
                        pe.wait_ge(S["attn"], 2 * (NT - 1) + j + 1)
                        for t in range(NT):
                            ins = pe.transpose(k.ps[j][:, 2, t * P:(t + 1) * P], attn[j][:, t, :], w["ident"])
                        ins.then_inc(S["aT_ps"], 1)
                n_aT = 4 * NT if wide else 2
                for j in LANES:
                    pe.wait_ge(S["aT"], n_aT)
                    for c in range(KC):
                        ins = pe.matmul(k.ps[j][:, 1, :], wo[:, c * P:(c + 1) * P], aT[j][:, c, :],
                                        start=(c == 0), stop=(c == KC - 1))
                    ins.then_inc(S["y"], 1)
                tail.tensor(pe)

            @block.scalar
            def _(act):
                k.have(act, "vec")
                for j in LANES:
                    act.wait_ge(S["kT_ps"], j + 1)
                    if wide:
                        for half in range(2):
                            ins = act.activation(kT[j][:, 4 * half:4 * half + 4, :].rearrange("p c n -> p (c n)"),
                                                 k.ps[j][:, half, 0:4 * CTX], ACT.Copy)
                    else:
                        ins = act.activation(kT[j][:, 0, :], k.ps[j][:, 0, 0:CTX], ACT.Copy)
                    ins.then_inc(S["kT"], 1)
                for c in range(KC):
                    for j in LANES:
                        act.wait_ge(S["qT_ps"], 2 * c + j + 1)
                        act.activation(qT[j][:, c, :], k.ps[j][:, c % 2, :], ACT.Copy,
                                       scale=scale).then_inc(S["qT"], 1)
                for n in range(UNITS + LATE):
                    if n < UNITS:
                        j, u, t, hg = unit(n)
                        act.wait_ge(S["less"], n + 1)
                        act.activation(prob[j][:, u % 2, :], prob[j][:, u % 2, :], ACT.Exp).then_inc(S["exp"], 1)
                    if 0 <= n - 2 < UNITS:
                        j, u, t, hg = unit(n - 2)
                        act.wait_ge(S["pT_ps"], n - 1)
                        if n >= 4:
                            act.wait_ge(S["pv"], n - 3)
                        act.activation(pT[j][:, :], k.ps[j][0:CTX, 2, :], ACT.Copy).then_inc(S["pT"], 1)
                    if wide and n >= LATE:
                        j, u, t, hg = unit(n - LATE)
                        if hg == GROUPS - 1 and j == 1:
                            for half in range(2):
                                for jj in LANES:
                                    act.wait_ge(S["aT_ps"], 4 * t + 2 * half + jj + 1)
                                    act.activation(aT[jj][:, 4 * half:4 * half + 4, t * P:(t + 1) * P],
                                                   k.ps[jj][:, 2, :].rearrange("p (c n) -> p c n", c=4),
                                                   ACT.Copy).then_inc(S["aT"], 1)
                if not wide:
                    for j in LANES:
                        act.wait_ge(S["aT_ps"], j + 1)
                        act.activation(aT[j][:, 0, :], k.ps[j][:, 2, :], ACT.Copy).then_inc(S["aT"], 1)
                tail.scalar(act)

            @block.vector
            def _(dve):
                k.have(dve, "const")
                c = Chain(dve, S["step"])
                for j in LANES:
                    dve.wait_ge(S["v_ps"], j + 1)
                    for a in range(inner // VN):
                        hh = VN // dh
                        ins = dve.tensor_copy(V[j][:, a * hh:(a + 1) * hh, 0:dh],
                                              k.ps[j][0:CTX, 2 + a, 0:VN].rearrange("p (h d) -> p h d", d=dh))
                    ins.then_inc(S["v"], 1)
                if not wide:
                    for j in LANES:
                        dve.wait_ge(S["kT"], j + 1)
                        dve.tensor_tensor(kblock[j][:, :, :], rep(kT[j][:, 0, :], 1, H),
                                          rep(w["headmask"], 2, CTX), ALU.mult).then_inc(S["kblock"], 1)
                if mask is not None:
                    for j in LANES:
                        dve.tensor_scalar(mrow[j][:, :, :], rep(k.maskrow[mask][j][:, :], 1, HG), FAR, -FAR,
                                          ALU.mult, ALU.add).then_inc(S["mask"], 1)

                def normalise(n):
                    j, u, t, hg = unit(n)
                    if wide:
                        dve.wait_ge(S["pv"], n + 1)
                        if hg == 0 and t > 0:
                            dve.wait_ge(S["aT_ps"], 4 * (t - 1) + 2 + j + 1)
                        count = HG
                        a = attn[j][:, 0, :].rearrange("p (h two d) -> p h two d", two=2, d=dh)[
                            :, HG * (hg // 2):HG * (hg // 2) + HG, hg % 2, :]
                    else:
                        if hg != GROUPS - 1:
                            return
                        dve.wait_ge(S["pv"], n + 1)
                        count = H
                        a = attn[j][:, t, :].rearrange("p (h d) -> p h d", d=dh)
                    o = k.ps[j][:, 3, 0:count * VW].rearrange("p (h d) -> p h d", d=VW)
                    c.link(dve.reciprocal(rsum[j][:, 0:count], o[:, :, dh]))
                    dve.tensor_tensor(a, o[:, :, 0:dh], rep(rsum[j][:, 0:count], 2, dh),
                                      ALU.mult).then_inc(S["attn"], 1)

                for n in range(UNITS + 4):
                    if n < UNITS:
                        j, u, t, hg = unit(n)
                        dve.wait_ge(S["scores"], n + 1)
                        s3 = k.ps[j][:, u % 2, 0:SC].rearrange("p (h n) -> p h n", n=CTX)
                        c.link(dve.tensor_reduce(nmax[j][:, u % 2, :], s3, AX.X, ALU.max, negate=True))
                        if n >= 4:
                            dve.wait_ge(S["pT_ps"], n - 3)
                        dve.tensor_tensor(prob[j][:, u % 2, :].rearrange("p (h n) -> p h n", n=CTX), s3,
                                          rep(nmax[j][:, u % 2, :], 2, CTX), ALU.add).then_inc(S["less"], 1)
                    if n >= 4:
                        normalise(n - 4)
                tail.vector(dve, c)

            @block.gpsimd
            def _(pool):
                for j in LANES:
                    pool.memset(V[j][:, :, dh:VW], 1.0).then_inc(S["vones"], 1)
                tail.gpsimd(pool)
        k.close()


def l0_signs(k):
    nc, w = k.nc, k.w
    S = k.signals("scales h1_ps h1 h2_ps h2 yT_ps y_done step" + LN_SIGNALS + TAIL_SIGNALS)
    with k.scratch():
        st = [k.tmp(f"stats{j}", [P, NT, 10]) for j in LANES]
        w0, w1, w2 = k.signs0, k.signs1, k.signs2
        sc = k.tmp("scales", [P, 2])
        h1 = [k.tmp(f"h1{j}", [P, FC, T]) for j in LANES]
        h2 = [k.tmp(f"h2{j}", [P, FC, T]) for j in LANES]
        yT = [k.tmp(f"yT{j}", [P, T]) for j in LANES]
        tail = Tail(k, S, st, via=2, ready="yT_ps", bias=0.0, yT=yT, y_scale=w["s2"])
        with nc.Block(no_gpsimd_drain=True) as block:

            @block.gpsimd
            def _(pool):
                tail.gpsimd(pool)

            @block.tensor
            def _(pe):
                k.have(pe, "const")
                for f in range(FC):
                    for j in LANES:
                        n = 2 * f + j
                        if f >= 2:
                            pe.wait_ge(S["h1"], n - 3)
                        pe.matmul(k.ps[j][:, f % 2, :], w0[:, f * P:(f + 1) * P], k.XT[j][:, :],
                                  start=True, stop=True).then_inc(S["h1_ps"], 1)
                for f in range(FC):
                    for j in LANES:
                        n = 2 * f + j
                        pe.wait_ge(S["h1"], 2 * (FC - 1) + j + 1)
                        if f >= 2:
                            pe.wait_ge(S["h2"], n - 3)
                        for c in range(FC):
                            ins = pe.matmul(k.ps[j][:, f % 2, :], w1[:, c, f * P:(f + 1) * P],
                                            h1[j][:, c, :], start=(c == 0), stop=(c == FC - 1))
                        ins.then_inc(S["h2_ps"], 1)
                for j in LANES:
                    pe.wait_ge(S["h2"], 2 * (FC - 1) + j + 1)
                    for c in range(FC):
                        ins = pe.matmul(k.ps[j][:, 2, :], w2[:, c, :], h2[j][:, c, :],
                                        start=(c == 0), stop=(c == FC - 1))
                    ins.then_inc(S["yT_ps"], 1)
                tail.tensor(pe)

            @block.scalar
            def _(act):
                act.wait_ge(S["scales"], 1)
                for f in range(FC):
                    for j in LANES:
                        act.wait_ge(S["h1_ps"], 2 * f + j + 1)
                        act.activation(h1[j][:, f, :], k.ps[j][:, f % 2, :], ACT.Relu,
                                       scale=sc[:, 0:1]).then_inc(S["h1"], 1)
                for f in range(FC):
                    for j in LANES:
                        act.wait_ge(S["h2_ps"], 2 * f + j + 1)
                        act.activation(h2[j][:, f, :], k.ps[j][:, f % 2, :], ACT.Relu,
                                       scale=sc[:, 1:2]).then_inc(S["h2"], 1)
                tail.scalar(act)

            @block.vector
            def _(dve):
                k.have(dve, "vec")
                c = Chain(dve, S["step"])
                dve.tensor_scalar(sc[:, 0:1], w["s0"], 4.0, None, ALU.mult)
                dve.tensor_scalar(sc[:, 1:2], w["s1"], 2.0, None, ALU.mult).then_inc(S["scales"], 1)
                tail.vector(dve, c)
        k.close()



SIGN = [[1, 1, 1, 1], [-1, 1, -1, 1], [-1, 1, 1, -1], [-1, -1, 1, 1]]


def quaternion_product(dve, c, q1, q2, prod, out, conjugate):
    n = {}
    for j in LANES:
        for a in range(4):
            ins = dve.tensor_tensor(prod[j][:, a, :, :], rep(q1[j][:, :, a], 2, 4), q2[j], ALU.mult)
        n[j] = c.mark(ins)

    def sign(a, r):
        return SIGN[a][r] * (-1 if conjugate and r ^ a else 1)

    order = {}
    for r in range(4):
        terms = sorted(range(4), key=lambda a: -sign(a, r))
        assert sign(terms[0], r) > 0
        order[r] = terms
    for step in range(3):
        for j in LANES:
            c.wait(n[j])
            for r in range(4):
                a = order[r][step + 1]
                first = prod[j][:, order[r][0], :, r ^ order[r][0]] if step == 0 else out[j][:, :, r]
                ins = dve.tensor_tensor(out[j][:, :, r], first, prod[j][:, a, :, r ^ a],
                                        ALU.add if sign(a, r) > 0 else ALU.subtract)
            n[j] = c.mark(ins)
    return n


def l1_quaternion(k):
    nc, w = k.nc, k.w
    NQ = NT * D // 4
    S = k.signals("kv_ps square norm2 inv bound memory n n_ps nT y step" + LN_SIGNALS + TAIL_SIGNALS)
    with k.scratch():
        st = [k.tmp(f"stats{j}", [P, NT, 10]) for j in LANES]
        key = [k.tmp(f"key{j}", [P, NQ, 4]) for j in LANES]
        val = [k.tmp(f"val{j}", [P, NQ, 4]) for j in LANES]
        sq = [k.tmp(f"sq{j}", [P, NQ, 4]) for j in LANES]
        n2 = [k.tmp(f"n2{j}", [P, NQ]) for j in LANES]
        prod = [k.tmp(f"prod{j}", [P, 4, NQ, 4]) for j in LANES]
        bound = [k.tmp(f"bound{j}", [P, NQ, 4]) for j in LANES]
        nT = [k.tmp(f"nT{j}", [P, T]) for j in LANES]
        yT = [k.tmp(f"yT{j}", [P, T]) for j in LANES]
        tail = Tail(k, S, st, base=2, via=1, ready="y", bias=w["bo1"], yT=yT, x_factor=2.0)

        def tiles(ap):
            return ap.rearrange("p (t q) c -> p t (q c)", t=NT)

        with nc.Block(no_gpsimd_drain=True) as block:

            @block.tensor
            def _(pe):
                k.have(pe, "L1", "const")
                wkv = k.group["L1"][:, 0:2 * D]
                for j in LANES:
                    for t in range(NT):
                        ins = pe.matmul(k.ps[j][:, t // 2, (t % 2) * 256:(t % 2) * 256 + 256],
                                        k.XT[j][:, t * P:(t + 1) * P], wkv, start=True, stop=True)
                    ins.then_inc(S["kv_ps"], 1)
                for j in LANES:
                    pe.wait_ge(S["bound"], j + 1)
                    b = tiles(bound[j][:, :, :])
                    pe.matmul(k.ps[j][:, 2, :], w["tri"], b.rearrange("p t n -> p (t n)"), start=True, stop=False)
                    for t in range(NT - 1):
                        ins = pe.matmul(k.ps[j][:, 2, (t + 1) * P:], w["ones"], rep(b[:, t, :], 1, NT - 1 - t),
                                        start=False, stop=(t == NT - 2))
                    ins.then_inc(S["memory"], 1)
                for j in LANES:
                    pe.wait_ge(S["n"], j + 1)
                    for t in range(NT):
                        ins = pe.transpose(k.ps[j][:, 0, t * P:(t + 1) * P], tiles(bound[j][:, :, :])[:, t, :],
                                           w["ident"])
                    ins.then_inc(S["n_ps"], 1)
                for j in LANES:
                    pe.wait_ge(S["nT"], j + 1)
                    pe.matmul(k.ps[j][:, 1, :], w["o1"], nT[j][:, :], start=True, stop=True).then_inc(S["y"], 1)
                tail.tensor(pe)

            @block.scalar
            def _(act):
                k.have(act, "vec")
                for j in LANES:
                    act.wait_ge(S["n_ps"], j + 1)
                    act.activation(nT[j][:, :], k.ps[j][:, 0, :], ACT.Identity, bias=w["ln_b"],
                                   scale=w["ln_g"]).then_inc(S["nT"], 1)
                tail.scalar(act)

            @block.vector
            def _(dve):
                k.have(dve, "rows", "const")
                c = Chain(dve, S["step"])
                n = {}
                for j in LANES:
                    dve.wait_ge(S["kv_ps"], j + 1)
                    kv = k.ps[j][:, 0:2, :].rearrange("p b (s kv n) -> p (b s) kv n", s=2, kv=2)
                    dve.tensor_tensor(tiles(key[j][:, :, :]), kv[:, :, 0, :], rep(w["bk1"], 1, NT),
                                      ALU.add).then_inc(S["square"], 1)
                    n[j] = c.mark(dve.tensor_tensor(tiles(val[j][:, :, :]), kv[:, :, 1, :], rep(w["bv1"], 1, NT),
                                                    ALU.add))
                for j in LANES:
                    c.wait(n[j])
                    n[j] = c.mark(dve.tensor_tensor(sq[j][:, :, :], key[j][:, :, :], key[j][:, :, :], ALU.mult))
                for j in LANES:
                    c.wait(n[j])
                    n[j] = c.mark(dve.tensor_reduce(n2[j][:, :], sq[j][:, :, :], AX.X, ALU.add))
                for j in LANES:
                    c.wait(n[j])
                    dve.tensor_scalar(n2[j][:, :], n2[j][:, :], 1e-24, None, ALU.max).then_inc(S["norm2"], 1)
                for j in LANES:
                    dve.wait_ge(S["inv"], j + 1)
                    n[j] = c.mark(dve.tensor_tensor(key[j][:, :, :], key[j][:, :, :], rep(n2[j][:, :], 2, 4),
                                                    ALU.mult))
                for j in LANES:
                    c.wait(n[j])
                kq = [key[j][:, :, :] for j in LANES]
                n = quaternion_product(dve, c, [val[j][:, :, :] for j in LANES], kq, prod, bound, False)
                for j in LANES:
                    c.wait(n[j])
                    dve.tensor_copy(sq[j][:, 0:1, :], bound[j][:, 0:1, :]).then_inc(S["bound"], 1)
                for j in LANES:
                    dve.wait_ge(S["memory"], j + 1)
                memory = [k.ps[j][:, 2, :].rearrange("p (q c) -> p q c", c=4) for j in LANES]
                n = quaternion_product(dve, c, memory, kq, prod, bound, True)
                for j in LANES:
                    c.wait(n[j])
                    n[j] = c.mark(dve.tensor_tensor(tiles(sq[j][:, :, :]), tiles(bound[j][:, :, :]),
                                                    rep(w["rpos"], 2, D), ALU.mult))
                for j in LANES:
                    c.wait(n[j])
                vector_layernorm(k, dve, c, S, lambda j, t: tiles(sq[j][:, :, :])[:, t, :],
                                 lambda j, t: tiles(bound[j][:, :, :])[:, t, :], st, "n")
                tail.vector(dve, c)

            @block.gpsimd
            def _(pool):
                for j in LANES:
                    pool.wait_ge(S["norm2"], j + 1)
                    pool.tensor_tensor(n2[j][:, :], n2[j][:, :], k.half[:, 0:NQ], ALU.pow).then_inc(S["inv"], 1)
                pool_layernorm(k, pool, S, st)
                tail.gpsimd(pool)
        k.close()


def first_largest(dve, c, p, m, wk, mw, onehot, down8):
    c.link(dve.tensor_reduce(m, p, AX.X, ALU.max))
    c.link(dve.tensor_tensor(wk, p, rep(m, 2, E), ALU.is_equal))
    c.link(dve.tensor_tensor(wk, wk, rep(down8, 1, NT), ALU.mult))
    c.link(dve.tensor_reduce(mw, wk, AX.X, ALU.max))
    c.link(dve.tensor_tensor(onehot, wk, rep(mw, 2, E), ALU.is_equal))


def l1_mixture(k):
    nc, w = k.nc, k.w
    NB = 2 * NT
    SL = E * CAP
    S = k.signals("logits less exp masks cum disp taken xin h_ps h eo_ps eo gates gd ct_ps ct y_tile step"
                  + LN_SIGNALS + TAIL_SIGNALS)
    with k.scratch():
        st = [k.tmp(f"stats{j}", [P, NT, 10]) for j in LANES]
        p = [k.tmp(f"p{j}", [P, NT, E]) for j in LANES]
        wk = [k.tmp(f"wk{j}", [P, NT, E]) for j in LANES]
        small = [k.tmp(f"small{j}", [P, 4, NT]) for j in LANES]
        mask = k.tmp("mask", [P, 2, NB, E]); mask16 = k.tmp("mask16", [P, 2, NB, E], BF16)
        gate = k.tmp("gate", [P, NB, E])
        total = k.tmp("total", [P, E, 2 * NB]); upto = k.tmp("upto", [P, E, 2 * NB])
        cum = k.tmp("cum", [P, 2, NB, E]); pos = k.tmp("pos", [P, NB, E])
        disp = k.tmp("disp", [P, 2, SL])
        gd = k.tmp("gd", [P, NB, SL])
        xin = k.tmp("xin", [P, SL])
        hid = k.tmp("hid", [P, E, FC * CAP])
        eo = k.tmp("eo", [CAP, E, D])
        ct = k.tmp("ct", [CAP, 2, E * P])
        tail = Tail(k, S, st, y_at=("y_tile", NT, 0))
        wi = w["wi"].rearrange("p (e f) -> p e f", e=E)
        wo = w["wo"].rearrange("p (e c n) -> p e c n", e=E, c=FC)
        with nc.Block(no_gpsimd_drain=True) as block:

            @block.tensor
            def _(pe):
                k.have(pe, "L1", "L1wi", "L1wo", "const")
                for j in LANES:
                    for t in range(NT):
                        ins = pe.matmul(k.ps[j][:, 0, t * E:(t + 1) * E], k.XT[j][:, t * P:(t + 1) * P],
                                        w["router1"], start=True, stop=True)
                    ins.then_inc(S["logits"], 1)
                pe.wait_ge(S["masks"], 2)
                flat = mask16[:, :, :, :].rearrange("p a b e -> p (a b e)")
                pe.matmul(k.ps[0][:, 0, 0:P], k.tri16[:, :], flat, start=True, stop=True)
                pe.matmul(k.ps[0][:, 1, 0:P], k.ones16[:, :], flat, start=True, stop=True).then_inc(S["cum"], 1)
                for i in range(NB):
                    pe.wait_ge(S["disp"], i + 1)
                    for half in range(2):
                        ins = pe.matmul(k.ps[0][:, 2 + half, 0:SL // 2], k.X[i // NT][:, i % NT, :],
                                        disp[:, i % 2, half * SL // 2:(half + 1) * SL // 2],
                                        start=(i == 0), stop=(i == NB - 1))
                    ins.then_inc(S["taken"], 1)
                pe.wait_ge(S["xin"], 1)

                def up(e):
                    if e >= 2:
                        pe.wait_ge(S["h"], e - 1)
                    for c in range(FC):
                        ins = pe.matmul(k.ps[1][:, e % 2, c * CAP:(c + 1) * CAP], wi[:, e, c * P:(c + 1) * P],
                                        xin[:, e * CAP:(e + 1) * CAP], start=True, stop=True)
                    ins.then_inc(S["h_ps"], 1)

                up(0)
                for e in range(E):
                    if e + 1 < E:
                        up(e + 1)
                    pe.wait_ge(S["h"], e + 1)
                    for c in range(FC):
                        ins = pe.matmul(k.ps[1][0:CAP, 2 + e // 4, (e % 4) * D:(e % 4 + 1) * D],
                                        hid[:, e, c * CAP:(c + 1) * CAP], wo[:, e, c, :],
                                        start=(c == 0), stop=(c == FC - 1))
                    if e % 4 == 3:
                        ins.then_inc(S["eo_ps"], 1)

                def turn(i):
                    pe.wait_ge(S["gd"], i + 1)
                    if i >= 2:
                        pe.wait_ge(S["ct"], i - 1)
                    for e in range(E):
                        ins = pe.transpose(k.ps[i % 2][0:CAP, e // 4, (e % 4) * P:(e % 4 + 1) * P],
                                           gd[:, i, e * CAP:(e + 1) * CAP], w["ident"])
                    ins.then_inc(S["ct_ps"], 1)

                turn(0)
                for i in range(NB):
                    if i + 1 < NB:
                        turn(i + 1)
                    if i == 0:
                        pe.wait_ge(S["eo"], 2)
                    pe.wait_ge(S["ct"], i + 1)
                    for e in range(E):
                        ins = pe.matmul(k.ps[i // NT][:, 3, (i % NT) * P:(i % NT + 1) * P],
                                        ct[:, i % 2, e * P:(e + 1) * P], eo[:, e, :],
                                        start=(e == 0), stop=(e == E - 1))
                    ins.then_inc(S["y_tile"], 1)
                tail.tensor(pe)

            @block.scalar
            def _(act):
                for j in LANES:
                    act.wait_ge(S["less"], j + 1)
                    act.activation(p[j][:, :, :], p[j][:, :, :], ACT.Exp).then_inc(S["exp"], 1)
                act.wait_ge(S["taken"], NB)
                act.activation(xin[:, :].rearrange("p (a n) -> p a n", a=2), k.ps[0][:, 2:4, 0:SL // 2],
                               ACT.Copy).then_inc(S["xin"], 1)
                for e in range(E):
                    act.wait_ge(S["h_ps"], e + 1)
                    act.activation(hid[:, e, :], k.ps[1][:, e % 2, 0:FC * CAP], ACT.Relu).then_inc(S["h"], 1)
                for i in range(NB):
                    act.wait_ge(S["ct_ps"], i + 1)
                    if i >= 2:
                        act.wait_ge(S["y_tile"], i - 1)
                    act.activation(ct[:, i % 2, :].rearrange("p (a n) -> p a n", a=2), k.ps[i % 2][0:CAP, 0:2, :],
                                   ACT.Copy).then_inc(S["ct"], 1)
                tail.scalar(act)

            @block.vector
            def _(dve):
                k.have(dve, "const")
                c = Chain(dve, S["step"])
                for j in LANES:
                    dve.wait_ge(S["logits"], j + 1)
                    lg = k.ps[j][:, 0, 0:NT * E].rearrange("p (t e) -> p t e", e=E)
                    c.link(dve.tensor_reduce(small[j][:, 0, :], lg, AX.X, ALU.max))
                    dve.tensor_tensor(p[j][:, :, :], lg, rep(small[j][:, 0, :], 2, E),
                                      ALU.subtract).then_inc(S["less"], 1)
                for j in LANES:
                    at = slice(NT * j, NT * j + NT)
                    dve.wait_ge(S["exp"], j + 1)
                    c.link(dve.tensor_reduce(small[j][:, 0, :], p[j][:, :, :], AX.X, ALU.add))
                    c.link(dve.reciprocal(small[j][:, 1, :], small[j][:, 0, :]))
                    c.link(dve.tensor_tensor(p[j][:, :, :], p[j][:, :, :], rep(small[j][:, 1, :], 2, E), ALU.mult))
                    first_largest(dve, c, p[j][:, :, :], small[j][:, 2, :], wk[j][:, :, :], small[j][:, 0, :],
                                  mask[:, 0, at, :], w["down8"])
                    dve.tensor_tensor(gate[:, at, :], mask[:, 0, at, :], rep(small[j][:, 2, :], 2, E), ALU.mult)
                    c.link(dve.scalar_tensor_tensor(out=p[j][:, :, :], in0=mask[:, 0, at, :], scalar=-2.0,
                                                    in1=p[j][:, :, :], op0=ALU.mult, op1=ALU.add))
                    first_largest(dve, c, p[j][:, :, :], small[j][:, 3, :], wk[j][:, :, :], small[j][:, 0, :],
                                  mask[:, 1, at, :], w["down8"])
                    c.link(dve.tensor_tensor(wk[j][:, :, :], mask[:, 1, at, :], rep(small[j][:, 3, :], 2, E),
                                             ALU.mult))
                    dve.tensor_tensor(gate[:, at, :], gate[:, at, :], wk[j][:, :, :], ALU.add)
                    dve.tensor_copy(mask16[:, :, at, :], mask[:, :, at, :]).then_inc(S["masks"], 1)
                dve.wait_ge(S["cum"], 1)
                c.link(dve.tensor_copy(total[:, :, :], k.ps[0][:, 1, 0:P].rearrange("p (b e) -> p e b", e=E)))
                c.link(dve.tensor_tensor_scan(upto[:, :, :].rearrange("p e b -> p (e b)"), w["restart"],
                                              total[:, :, :].rearrange("p e b -> p (e b)"), 0.0, ALU.mult, ALU.add))
                c.link(dve.tensor_tensor(upto[:, :, :], upto[:, :, :], total[:, :, :], ALU.subtract))
                cumf = cum[:, :, :, :].rearrange("p a b e -> p (a b) e")
                c.link(dve.tensor_tensor(cumf, k.ps[0][:, 0, 0:P].rearrange("p (b e) -> p b e", e=E),
                                         upto[:, :, :].rearrange("p e b -> p b e"), ALU.add))
                c.link(dve.tensor_tensor(cumf, cumf, mask[:, :, :, :].rearrange("p a b e -> p (a b) e"), ALU.mult))
                ins = dve.scalar_tensor_tensor(out=pos[:, :, :], in0=cum[:, 0, :, :], scalar=-1.0,
                                               in1=cum[:, 1, :, :], op0=ALU.add, op1=ALU.add)
                ins.then_inc(S["gates"], 1)
                dve.wait_ge(S["gates"], 1)
                for i in range(NB):
                    if i >= 2:
                        dve.wait_ge(S["taken"], i - 1)
                    dve.tensor_tensor(disp[:, i % 2, :].rearrange("p (e s) -> p e s", s=CAP), rep(w["slot"], 1, E),
                                      rep(pos[:, i, :], 2, CAP), ALU.is_equal).then_inc(S["disp"], 1)
                for half in range(2):
                    dve.wait_ge(S["eo_ps"], half + 1)
                    dve.tensor_copy(eo[:, 4 * half:4 * half + 4, :].rearrange("p e n -> p (e n)"),
                                    k.ps[1][0:CAP, 2 + half, :]).then_inc(S["eo"], 1)
                tail.vector(dve, c)

            @block.gpsimd
            def _(pool):
                k.have(pool, "const")
                pool.wait_ge(S["gates"], 1)
                for i in range(NB):
                    for e in range(E):
                        ins = pool.tensor_scalar(gd[:, i, e * CAP:(e + 1) * CAP], w["slot"], pos[:, i, e:e + 1],
                                                 gate[:, i, e:e + 1], ALU.is_equal, ALU.mult)
                    ins.then_inc(S["gd"], 1)
                tail.gpsimd(pool)
        k.close()



def l2_linear_attention(k):
    nc, w = k.nc, k.w
    VW = DH + 1
    S = k.signals("n1 n1_ps n1T qkv_ps z expz qk vones kv_in kv_prod attn a_ps aT o_ps oT o_tok x1 n2 n2_ps n2T fc_ps h "
                  "y step" + LN_SIGNALS + TAIL_SIGNALS)
    with k.scratch():
        st = [k.tmp(f"stats{j}", [P, NT, 10]) for j in LANES]
        xn = [k.tmp(f"xn{j}", [P, NT, D]) for j in LANES]
        xnT = [k.tmp(f"xnT{j}", [P, T]) for j in LANES]
        z = [k.tmp(f"z{j}", [P, NT, 2 * D]) for j in LANES]
        ez = [k.tmp(f"ez{j}", [P, NT, 2 * D]) for j in LANES]
        V = [k.tmp(f"V{j}", [P, NT, H, VW]) for j in LANES]
        outer = [k.tmp(f"outer{j}", [P, DH, VW, H]) for j in LANES]
        inner = k.tmp("inner", [P, H, VW, DH])
        kv = [k.tmp(f"kv{j}", [P, DH, VW]) for j in LANES]
        o = [k.tmp(f"o{j}", [P, H, VW]) for j in LANES]
        rs = [k.tmp(f"rs{j}", [P, H]) for j in LANES]
        attn = [k.tmp(f"attn{j}", [P, NT, D]) for j in LANES]
        hT = [k.tmp(f"hT{j}", [P, FC, T]) for j in LANES]
        tail = Tail(k, S, st, base=4, via=2, ready="y", bias=w["proj_b"], yT=xnT)
        with nc.Block(no_gpsimd_drain=True) as block:

            @block.tensor
            def _(pe):
                k.have(pe, "L2", "const")
                for j in LANES:
                    pe.wait_ge(S["n1"], j + 1)
                    for t in range(NT):
                        ins = pe.transpose(k.ps[j][:, 0, t * P:(t + 1) * P], xn[j][:, t, :], w["ident"])
                    ins.then_inc(S["n1_ps"], 1)
                for j in LANES:
                    pe.wait_ge(S["n1T"], j + 1)
                    for t in range(NT):
                        ins = pe.matmul(k.ps[j][:, t, 0:3 * D], xnT[j][:, t * P:(t + 1) * P], w["qkv2"],
                                        start=True, stop=True)
                    ins.then_inc(S["qkv_ps"], 1)
                for j in LANES:
                    pe.wait_ge(S["attn"], (NT - 1) * 2 + j + 1)
                    for t in range(NT):
                        ins = pe.transpose(k.ps[j][:, 0, t * P:(t + 1) * P], attn[j][:, t, :], w["ident"])
                    ins.then_inc(S["a_ps"], 1)
                for j in LANES:
                    pe.wait_ge(S["aT"], j + 1)
                    pe.matmul(k.ps[j][:, 1, :], w["o2"], xnT[j][:, :], start=True, stop=True).then_inc(S["o_ps"], 1)
                for j in LANES:
                    pe.wait_ge(S["oT"], j + 1)
                    for t in range(NT):
                        ins = pe.transpose(k.ps[j][:, 2, t * P:(t + 1) * P], hT[j][:, 0, t * P:(t + 1) * P], w["ident"])
                    ins.then_inc(S["o_tok"], 1)
                for j in LANES:
                    pe.wait_ge(S["n2"], j + 1)
                    for t in range(NT):
                        ins = pe.transpose(k.ps[j][:, 0, t * P:(t + 1) * P], xn[j][:, t, :], w["ident"])
                    ins.then_inc(S["n2_ps"], 1)
                for f in range(FC):
                    for j in LANES:
                        pe.wait_ge(S["n2T"], j + 1)
                        if f >= 2:
                            pe.wait_ge(S["h"], 2 * (f - 2) + j + 1)
                        pe.matmul(k.ps[j][:, f % 2, :], w["fc"][:, f * P:(f + 1) * P], xnT[j][:, :],
                                  start=True, stop=True).then_inc(S["fc_ps"], 1)
                for j in LANES:
                    pe.wait_ge(S["h"], 2 * (FC - 1) + j + 1)
                    for f in range(FC):
                        ins = pe.matmul(k.ps[j][:, 2, :], w["proj"][:, f * P:(f + 1) * P], hT[j][:, f, :],
                                        start=(f == 0), stop=(f == FC - 1))
                    ins.then_inc(S["y"], 1)
                tail.tensor(pe)

            @block.scalar
            def _(act):
                k.have(act, "vec")
                for j in LANES:
                    act.wait_ge(S["n1_ps"], j + 1)
                    act.activation(xnT[j][:, :], k.ps[j][:, 0, :], ACT.Identity, bias=w["ln1_b"],
                                   scale=w["ln1_w"]).then_inc(S["n1T"], 1)
                for j in LANES:
                    act.wait_ge(S["z"], j + 1)
                    act.activation(ez[j][:, :, :], ez[j][:, :, :], ACT.Exp).then_inc(S["expz"], 1)
                for j in LANES:
                    act.wait_ge(S["a_ps"], j + 1)
                    act.activation(xnT[j][:, :], k.ps[j][:, 0, :], ACT.Copy).then_inc(S["aT"], 1)
                for j in LANES:
                    act.wait_ge(S["o_ps"], j + 1)
                    act.activation(hT[j][:, 0, :], k.ps[j][:, 1, :], ACT.Identity, bias=w["o_b"],
                                   scale=1.0).then_inc(S["oT"], 1)
                for j in LANES:
                    act.wait_ge(S["n2_ps"], j + 1)
                    act.activation(xnT[j][:, :], k.ps[j][:, 0, :], ACT.Identity, bias=w["ln2_b"],
                                   scale=w["ln2_w"]).then_inc(S["n2T"], 1)
                for f in range(FC):
                    for j in LANES:
                        act.wait_ge(S["fc_ps"], 2 * f + j + 1)
                        act.activation(hT[j][:, f, :], k.ps[j][:, f % 2, :], ACT.Gelu,
                                       bias=w["fc_b"][:, f:f + 1]).then_inc(S["h"], 1)
                tail.scalar(act)

            @block.vector
            def _(dve):
                k.have(dve, "rows", "const")
                c = Chain(dve, S["step"])
                vector_layernorm(k, dve, c, S, lambda j, t: k.X[j][:, t, :], lambda j, t: xn[j][:, t, :], st, "n1")
                n = {}
                for j in LANES:
                    dve.wait_ge(S["qkv_ps"], j + 1)
                    n[j] = c.mark(dve.tensor_tensor(z[j][:, :, :], k.ps[j][:, :, 0:2 * D],
                                                    rep(w["bqkv2"][:, 0:2 * D], 1, NT), ALU.add))
                    if j == 0:
                        dve.wait_ge(S["vones"], 2)
                    for t in range(NT):
                        dve.tensor_tensor(V[j][:, t, :, 0:DH],
                                          k.ps[j][:, t, 2 * D:3 * D].rearrange("p (h d) -> p h d", d=DH),
                                          w["bqkv2"][:, 2 * D:3 * D].rearrange("p (h d) -> p h d", d=DH), ALU.add)
                    c.wait(n[j])
                    dve.tensor_scalar(ez[j][:, :, :], z[j][:, :, :], 0.0, None, ALU.min).then_inc(S["z"], 1)
                for j in LANES:
                    dve.wait_ge(S["expz"], j + 1)
                    dve.scalar_tensor_tensor(out=z[j][:, :, :], in0=z[j][:, :, :], scalar=0.0,
                                             in1=ez[j][:, :, :], op0=ALU.max, op1=ALU.add).then_inc(S["qk"], 1)
                for i in range(2 * NT):
                    t, j = i // 2, i % 2
                    dve.wait_ge(S["kv_prod"], i + 1)
                    ins = dve.tensor_reduce(kv[j][:, :, :].rearrange("p d e -> p (d e)"),
                                            outer[j][:, :, :, :].rearrange("p d e h -> p (d e) h"), AX.X, ALU.add)
                    ins.then_inc(S["kv_in"], 1)
                    dve.wait_ge(S["kv_in"], i + 1)
                    q = z[j][:, t, 0:D].rearrange("p (h d) -> p h d", d=DH)
                    c.link(dve.tensor_tensor(inner[:, :, :, :], rep(q, 2, VW),
                                             rep(kv[j][:, :, :].rearrange("p d e -> p e d"), 1, H), ALU.mult))
                    c.link(dve.tensor_reduce(o[j][:, :, :].rearrange("p h e -> p (h e)"),
                                             inner[:, :, :, :].rearrange("p h e d -> p (h e) d"), AX.X, ALU.add))
                    c.link(dve.reciprocal(rs[j][:, :], o[j][:, :, DH]))
                    dve.tensor_tensor(attn[j][:, t, :].rearrange("p (h d) -> p h d", d=DH), o[j][:, :, 0:DH],
                                      rep(rs[j][:, :], 2, DH), ALU.mult).then_inc(S["attn"], 1)
                n = {}
                for j in LANES:
                    dve.wait_ge(S["o_tok"], j + 1)
                    n[j] = c.mark(dve.tensor_tensor(attn[j][:, :, :].rearrange("p t n -> p (t n)"),
                                                    k.X[j][:, :, :].rearrange("p t n -> p (t n)"),
                                                    k.ps[j][:, 2, :], ALU.add))
                for j in LANES:
                    c.wait(n[j])
                vector_layernorm(k, dve, c, S, lambda j, t: attn[j][:, t, :], lambda j, t: xn[j][:, t, :], st, "n2",
                                 base=2)
                for j in LANES:
                    n[j] = c.mark(dve.tensor_tensor(k.X[j][:, :, :], k.X[j][:, :, :], attn[j][:, :, :], ALU.add))
                for j in LANES:
                    c.wait(n[j])
                tail.vector(dve, c)

            @block.gpsimd
            def _(pool):
                for j in LANES:
                    pool.memset(V[j][:, :, :, DH:VW], 1.0).then_inc(S["vones"], 1)
                pool_layernorm(k, pool, S, st)
                for i in range(2 * NT):
                    t, j = i // 2, i % 2
                    pool.wait_ge(S["qk"], j + 1)
                    if i >= 2:
                        pool.wait_ge(S["kv_in"], i - 1)
                    key = z[j][:, t, D:2 * D].rearrange("p (h d) -> p d h", d=DH)
                    val = V[j][:, t, :, :].rearrange("p h e -> p e h")
                    pool.tensor_tensor(outer[j][:, :, :, :], rep(key, 2, VW), rep(val, 1, DH),
                                       ALU.mult).then_inc(S["kv_prod"], 1)
                pool_layernorm(k, pool, S, st, base=2)
                tail.gpsimd(pool)
        k.close()


def l2_perceiver(k):
    nc, w = k.nc, k.w
    KEYS = T + CTX
    UNITS = 2 * NT * 2
    S = k.signals("cn n cn_ps cnT n_ps nT ckv_ps ckv qkv_ps qkv v sq rms inv inv_c c_rms qk ck q_ps q_sb scl mask scores max "
                  "exp pT_ps pT pTc pv attn a_ps aT y step" + LN_SIGNALS + TAIL_SIGNALS)
    with k.scratch():
        st = [k.tmp(f"stats{j}", [P, NT, 10]) for j in LANES]
        cn = [k.tmp(f"cn{j}", [CTX, CD]) for j in LANES]
        cnT = [k.tmp(f"cnT{j}", [CD, CTX]) for j in LANES]
        xn = [k.tmp(f"xn{j}", [P, NT, D]) for j in LANES]
        xnT = [k.tmp(f"xnT{j}", [P, T]) for j in LANES]
        ckv = [k.tmp(f"ckv{j}", [CTX, 2 * D]) for j in LANES]
        qk = [k.tmp(f"qk{j}", [P, NT, 2 * D]) for j in LANES]
        V = [k.tmp(f"V{j}", [P, NT, D]) for j in LANES]
        sq = [k.tmp(f"sq{j}", [P, NT, 2 * D]) for j in LANES]
        csq = [k.tmp(f"csq{j}", [CTX, D]) for j in LANES]
        ss = [k.tmp(f"ss{j}", [P, 4 * NT]) for j in LANES]
        css = [k.tmp(f"css{j}", [CTX, 2]) for j in LANES]
        qT = [k.tmp(f"qT{j}", [P, T]) for j in LANES]
        kT = [k.tmp(f"kT{j}", [P, KEYS]) for j in LANES]
        mrow = [k.tmp(f"mrow{j}", [1, CTX], BF16) for j in LANES]
        qg = k.tmp("qg", [P, 1])
        prob = [k.tmp(f"prob{j}", [P, 2, KEYS]) for j in LANES]
        nmax = [k.tmp(f"nmax{j}", [P, 2]) for j in LANES]
        rs = [k.tmp(f"rs{j}", [P, 2]) for j in LANES]
        pT = [k.tmp(f"pT{j}", [P, T]) for j in LANES]
        pTc = [k.tmp(f"pTc{j}", [CTX, P]) for j in LANES]
        tail = Tail(k, S, st, base=4, via=1, ready="y", bias=w["xbo2"], yT=xnT)

        def unit(n):
            j, u = n % 2, n // 2
            return j, u, u // 2, u % 2

        with nc.Block(no_gpsimd_drain=True) as block:

            @block.tensor
            def _(pe):
                k.have(pe, "L2", "ctxw", "const")
                for j in LANES:
                    pe.wait_ge(S["cn"], j + 1)
                    pe.transpose(k.ps[j][0:CD, 0, 0:CTX], cn[j][:, :], w["ident"][0:CTX, 0:CTX]).then_inc(S["cn_ps"], 1)
                for j in LANES:
                    pe.wait_ge(S["n"], j + 1)
                    for t in range(NT):
                        ins = pe.transpose(k.ps[j][:, 1, t * P:(t + 1) * P], xn[j][:, t, :], w["ident"])
                    ins.then_inc(S["n_ps"], 1)
                for j in LANES:
                    pe.wait_ge(S["cnT"], j + 1)
                    pe.matmul(k.ps[j][0:CTX, 2, 0:2 * D], cnT[j][:, :], w["xkv2"], start=True,
                              stop=True).then_inc(S["ckv_ps"], 1)
                for j in LANES:
                    pe.wait_ge(S["nT"], j + 1)
                    pe.wait_ge(S["ckv"], j + 1)
                    for t in range(NT):
                        ins = pe.matmul(k.ps[j][:, t, 0:3 * D], xnT[j][:, t * P:(t + 1) * P], w["xqkv2"],
                                        start=True, stop=True)
                    ins.then_inc(S["qkv_ps"], 1)
                for j in LANES:
                    pe.wait_ge(S["qk"], j + 1)
                    pe.wait_ge(S["ck"], j + 1)
                    pe.wait_ge(S["v"], j + 1)
                    for a in range(2):
                        for t in range(NT):
                            pe.transpose(k.ps[j][:, a, t * P:(t + 1) * P], qk[j][:, t, a * D:(a + 1) * D], w["ident"])
                    pe.transpose(k.ps[j][:, 2, 0:CTX], ckv[j][:, 0:D], w["ident"][0:CTX, 0:CTX]).then_inc(S["q_ps"], 1)
                pe.wait_ge(S["q_sb"], 2)
                pe.wait_ge(S["mask"], 2)

                def scores(n):
                    j, u, t, h = unit(n)
                    if n >= 2:
                        pe.wait_ge(S["exp"], n - 1)
                    r = slice(DW * h, DW * h + DW)
                    q = qT[j][r, t * P:(t + 1) * P]
                    pe.matmul(k.ps[j][:, 0, :], q, kT[j][r, 0:T], start=True, stop=True)
                    pe.matmul(k.ps[j][:, 1, 0:CTX], q, kT[j][r, T:KEYS], start=True, stop=False)
                    pe.matmul(k.ps[j][:, 1, 0:CTX], k.one16[:, :], mrow[j][:, :], start=False,
                              stop=True).then_inc(S["scores"], 1)

                def transposes(n):
                    j, u, t, h = unit(n)
                    pe.wait_ge(S["exp"], n + 1)
                    if n >= 2:
                        pe.wait_ge(S["pT"], n - 1)
                        pe.wait_ge(S["attn"], n - 1)
                    for b in range(NT):
                        pe.transpose(k.ps[j][:, 2, b * P:(b + 1) * P], prob[j][:, u % 2, b * P:(b + 1) * P], w["ident"])
                    pe.transpose(k.ps[j][0:CTX, 3, 0:P], prob[j][:, u % 2, T:KEYS], w["ident"]).then_inc(S["pT_ps"], 1)

                def values(n):
                    j, u, t, h = unit(n)
                    pe.wait_ge(S["pT"], n + 1)
                    pe.wait_ge(S["pTc"], n + 1)
                    out = k.ps[j][:, 3, 2 * P:2 * P + DW]
                    for b in range(NT):
                        pe.matmul(out, pT[j][:, b * P:(b + 1) * P], V[j][:, b, h * DW:(h + 1) * DW],
                                  start=(b == 0), stop=False)
                    pe.matmul(out, pTc[j][:, :], ckv[j][:, D + h * DW:D + (h + 1) * DW], start=False,
                              stop=True).then_inc(S["pv"], 1)

                for n in range(UNITS + 2):
                    if n < UNITS:
                        scores(n)
                    if 0 <= n - 1 < UNITS:
                        transposes(n - 1)
                    if 0 <= n - 2 < UNITS:
                        values(n - 2)
                for j in LANES:
                    pe.wait_ge(S["attn"], UNITS - 1 + j)
                    for t in range(NT):
                        ins = pe.transpose(k.ps[j][:, 2, t * P:(t + 1) * P], xn[j][:, t, :], w["ident"])
                    ins.then_inc(S["a_ps"], 1)
                for j in LANES:
                    pe.wait_ge(S["aT"], j + 1)
                    pe.matmul(k.ps[j][:, 1, :], w["xo2"], qT[j][:, :], start=True, stop=True).then_inc(S["y"], 1)
                tail.tensor(pe)

            @block.scalar
            def _(act):
                k.have(act, "vec")
                for j in LANES:
                    act.wait_ge(S["cn_ps"], j + 1)
                    act.activation(cnT[j][:, :], k.ps[j][0:CD, 0, 0:CTX], ACT.Identity, bias=w["ln_x_b"][0:CD, :],
                                   scale=w["ln_x_g"][0:CD, :]).then_inc(S["cnT"], 1)
                for j in LANES:
                    act.wait_ge(S["n_ps"], j + 1)
                    act.activation(xnT[j][:, :], k.ps[j][:, 1, :], ACT.Identity, bias=w["ln_l_b"],
                                   scale=w["ln_l_g"]).then_inc(S["nT"], 1)
                for j in LANES:
                    act.wait_ge(S["qkv_ps"], j + 1)
                    act.activation(qk[j][:, :, :], k.ps[j][:, :, 0:2 * D], ACT.Copy).then_inc(S["qkv"], 1)
                act.wait_ge(S["scl"], 1)
                for j in LANES:
                    act.wait_ge(S["q_ps"], j + 1)
                    act.activation(qT[j][:, :], k.ps[j][:, 0, :], ACT.Copy, scale=qg[:, :])
                    act.activation(kT[j][:, 0:T], k.ps[j][:, 1, :], ACT.Copy, scale=w["kn_g"])
                    act.activation(kT[j][:, T:KEYS], k.ps[j][:, 2, 0:CTX], ACT.Copy,
                                   scale=w["kn_g"]).then_inc(S["q_sb"], 1)
                for n in range(UNITS + 1):
                    if n < UNITS:
                        j, u, t, h = unit(n)
                        act.wait_ge(S["max"], n + 1)
                        if n >= 4:
                            act.wait_ge(S["pT_ps"], n - 3)
                            act.wait_ge(S["attn"], n - 3)
                        act.activation(prob[j][:, u % 2, :], k.ps[j][:, 0:2, :].rearrange("p b n -> p (b n)")[:, 0:KEYS],
                                       ACT.Exp, bias=nmax[j][:, u % 2:u % 2 + 1],
                                       accum_out=rs[j][:, u % 2:u % 2 + 1]).then_inc(S["exp"], 1)
                    if n >= 1:
                        j, u, t, h = unit(n - 1)
                        act.wait_ge(S["pT_ps"], n)
                        if n - 1 >= 2:
                            act.wait_ge(S["pv"], n - 2)
                        act.activation(pT[j][:, :], k.ps[j][:, 2, :], ACT.Copy).then_inc(S["pT"], 1)
                for j in LANES:
                    act.wait_ge(S["a_ps"], j + 1)
                    act.activation(qT[j][:, :], k.ps[j][:, 2, :], ACT.Copy).then_inc(S["aT"], 1)
                tail.scalar(act)

            @block.vector
            def _(dve):
                k.have(dve, "vec")
                c = Chain(dve, S["step"])
                vector_layernorm(k, dve, c, S, lambda j, t: k.ctx[j][:, :], lambda j, t: cn[j][:, :], st, "cn",
                                 n_rows=CTX, tiles=1)
                vector_layernorm(k, dve, c, S, lambda j, t: k.X[j][:, t, :], lambda j, t: xn[j][:, t, :], st, "n",
                                 base=2)
                dve.tensor_scalar(qg[:, :], w["qn_g"], float(DW) ** -0.5, None, ALU.mult).then_inc(S["scl"], 1)
                for j in LANES:
                    dve.tensor_scalar(mrow[j][:, :], k.maskrow[0][j][:, :], FAR, -FAR, ALU.mult,
                                      ALU.add).then_inc(S["mask"], 1)
                n = {}
                for j in LANES:
                    dve.wait_ge(S["ckv_ps"], j + 1)
                    dve.tensor_copy(ckv[j][:, :], k.ps[j][0:CTX, 2, 0:2 * D]).then_inc(S["ckv"], 1)
                    dve.wait_ge(S["ckv"], j + 1)
                    c.link(dve.tensor_tensor(csq[j][:, :], ckv[j][:, 0:D], ckv[j][:, 0:D], ALU.mult))
                    c.link(dve.tensor_reduce(css[j][:, :], csq[j][:, :].rearrange("p (h d) -> p h d", d=DW), AX.X, ALU.add))
                    dve.tensor_scalar(css[j][:, :], css[j][:, :], 1.0 / DW, 1e-16, ALU.mult,
                                      ALU.max).then_inc(S["c_rms"], 1)
                for j in LANES:
                    dve.wait_ge(S["inv_c"], j + 1)
                    kc = ckv[j][:, 0:D].rearrange("p (h d) -> p h d", d=DW)
                    dve.tensor_tensor(kc, kc, rep(css[j][:, :], 2, DW), ALU.mult).then_inc(S["ck"], 1)
                for j in LANES:
                    dve.wait_ge(S["qkv"], j + 1)
                    n[j] = c.mark(dve.tensor_tensor(sq[j][:, :, :], qk[j][:, :, :], qk[j][:, :, :], ALU.mult))
                    dve.tensor_copy(V[j][:, :, :], k.ps[j][:, :, 2 * D:3 * D]).then_inc(S["v"], 1)
                for j in LANES:
                    c.wait(n[j])
                    n[j] = c.mark(dve.tensor_reduce(ss[j][:, :], sq[j][:, :, :].rearrange("p t (h d) -> p (t h) d", d=DW),
                                                    AX.X, ALU.add))
                for j in LANES:
                    c.wait(n[j])
                    dve.tensor_scalar(ss[j][:, :], ss[j][:, :], 1.0 / DW, 1e-16, ALU.mult,
                                      ALU.max).then_inc(S["rms"], 1)
                for j in LANES:
                    dve.wait_ge(S["inv"], j + 1)
                    both = qk[j][:, :, :].rearrange("p t (h d) -> p (t h) d", d=DW)
                    dve.tensor_tensor(both, both, rep(ss[j][:, :], 2, DW), ALU.mult).then_inc(S["qk"], 1)
                for n in range(UNITS + 2):
                    if n < UNITS:
                        j, u, t, h = unit(n)
                        dve.wait_ge(S["scores"], n + 1)
                        dve.tensor_reduce(nmax[j][:, u % 2:u % 2 + 1],
                                          k.ps[j][:, 0:2, :].rearrange("p b n -> p (b n)")[:, 0:KEYS], AX.X, ALU.max,
                                          negate=True).then_inc(S["max"], 1)
                    if 0 <= n - 1 < UNITS:
                        j, u, t, h = unit(n - 1)
                        dve.wait_ge(S["pT_ps"], n)
                        dve.tensor_copy(pTc[j][:, :], k.ps[j][0:CTX, 3, 0:P]).then_inc(S["pTc"], 1)
                    if n >= 2:
                        j, u, t, h = unit(n - 2)
                        dve.wait_ge(S["pv"], n - 1)
                        c.link(dve.reciprocal(rs[j][:, u % 2:u % 2 + 1], rs[j][:, u % 2:u % 2 + 1]))
                        dve.tensor_scalar(xn[j][:, t, h * DW:(h + 1) * DW], k.ps[j][:, 3, 2 * P:2 * P + DW],
                                          rs[j][:, u % 2:u % 2 + 1], None, ALU.mult).then_inc(S["attn"], 1)
                tail.vector(dve, c)

            @block.gpsimd
            def _(pool):
                pool_layernorm(k, pool, S, st, n_rows=CTX, tiles=1)
                pool_layernorm(k, pool, S, st, base=2)
                for j in LANES:
                    pool.wait_ge(S["c_rms"], j + 1)
                    pool.tensor_tensor(css[j][:, :], css[j][:, :], k.half[0:CTX, 0:2], ALU.pow).then_inc(S["inv_c"], 1)
                for j in LANES:
                    pool.wait_ge(S["rms"], j + 1)
                    pool.tensor_tensor(ss[j][:, :], ss[j][:, :], k.half[:, 0:4 * NT], ALU.pow).then_inc(S["inv"], 1)
                tail.gpsimd(pool)
        k.close()


def l2_switch(k):
    nc, w = k.nc, k.w
    UNITS = 2 * E
    S = k.signals("logits less exp onehot o_ps oT sel b2 picked xm h_ps h_act h_dve used step"
                  + LN_SIGNALS + TAIL_SIGNALS)
    with k.scratch():
        st = [k.tmp(f"stats{j}", [P, NT, 10]) for j in LANES]
        p = [k.tmp(f"p{j}", [P, NT, E]) for j in LANES]
        wk = [k.tmp(f"wk{j}", [P, NT, E]) for j in LANES]
        onehot = [k.tmp(f"onehot{j}", [P, NT, E]) for j in LANES]
        small = [k.tmp(f"small{j}", [P, 2, NT]) for j in LANES]
        oT = [k.tmp(f"oT{j}", [E, T], BF16) for j in LANES]
        sel = k.tmp("sel", [E, E, P], BF16)
        b2 = k.tmp("b2", [P, 1])
        xm = [k.tmp(f"xm{j}", [P, T]) for j in LANES]
        hT = [k.tmp(f"hT{j}", [P, FC, T]) for j in LANES]
        yT = [k.tmp(f"yT{j}", [P, T]) for j in LANES]
        tail = Tail(k, S, st, via=3, ready="used", ready_from=UNITS - 2, bias=b2[:, :], yT=yT, bank=0)
        W1 = w["W1"].rearrange("p (e f) -> p e f", e=E)
        W2 = w["W2"].rearrange("p (e c n) -> p e c n", e=E, c=FC)
        with nc.Block(no_gpsimd_drain=True) as block:

            @block.tensor
            def _(pe):
                k.have(pe, "L2", "L2w1", "L2w2", "const")
                for j in LANES:
                    for t in range(NT):
                        ins = pe.matmul(k.ps[j][:, 0, t * E:(t + 1) * E], k.XT[j][:, t * P:(t + 1) * P],
                                        w["router2"], start=True, stop=True)
                    ins.then_inc(S["logits"], 1)
                for j in LANES:
                    pe.wait_ge(S["onehot"], j + 1)
                    for t in range(NT):
                        ins = pe.transpose(k.ps[j][0:E, 1, t * P:(t + 1) * P], onehot[j][:, t, :], w["ident"])
                    ins.then_inc(S["o_ps"], 1)
                pe.wait_ge(S["oT"], 2)
                pe.wait_ge(S["sel"], 1)

                def pick(n):
                    if n >= 2:
                        pe.wait_ge(S["xm"], n - 1)
                    pe.matmul(k.ps[n % 2][:, 0, :], sel[:, n // 2, :], oT[n % 2][:, :], start=True,
                              stop=True).then_inc(S["picked"], 1)

                def up(n):
                    e, j = n // 2, n % 2
                    pe.wait_ge(S["xm"], n + 1)
                    for f in range(FC):
                        out_before = 2 * n - 2 if f < 2 else 2 * n + 1
                        if out_before > 0:
                            pe.wait_ge(S["h_act" if f % 2 == 0 else "h_dve"], out_before)
                        pe.matmul(k.ps[j][:, 1 + f % 2, :], W1[:, e, f * P:(f + 1) * P], xm[j][:, :],
                                  start=True, stop=True).then_inc(S["h_ps"], 1)

                def down(n):
                    e, j = n // 2, n % 2
                    pe.wait_ge(S["h_act"], 2 * n + 2)
                    pe.wait_ge(S["h_dve"], 2 * n + 2)
                    for f in range(FC):
                        ins = pe.matmul(k.ps[j][:, 3, :], W2[:, e, f, :], hT[j][:, f, :],
                                        start=(e == 0 and f == 0), stop=(e == E - 1 and f == FC - 1))
                    ins.then_inc(S["used"], 1)

                pick(0)
                pick(1)
                for n in range(UNITS + 1):
                    if n < UNITS:
                        up(n)
                    if n + 2 < UNITS:
                        pick(n + 2)
                    if n >= 1:
                        down(n - 1)
                tail.tensor(pe)

            @block.scalar
            def _(act):
                k.have(act, "vec")
                for j in LANES:
                    act.wait_ge(S["less"], j + 1)
                    act.activation(p[j][:, :, :], p[j][:, :, :], ACT.Exp).then_inc(S["exp"], 1)
                for j in LANES:
                    act.wait_ge(S["o_ps"], j + 1)
                    act.activation(oT[j][:, :], k.ps[j][0:E, 1, :], ACT.Copy).then_inc(S["oT"], 1)
                for n in range(UNITS):
                    e, j = n // 2, n % 2
                    for f in range(0, FC, 2):
                        act.wait_ge(S["h_ps"], FC * n + f + 1)
                        if n >= 2:
                            act.wait_ge(S["used"], n - 1)
                        act.activation(hT[j][:, f, :], k.ps[j][:, 1, :], ACT.Relu,
                                       bias=w["b1"][:, e * FC + f:e * FC + f + 1]).then_inc(S["h_act"], 1)
                act.wait_ge(S["b2"], 1)
                tail.scalar(act)

            @block.vector
            def _(dve):
                k.have(dve, "rows", "vec", "const")
                c = Chain(dve, S["step"])
                dve.tensor_copy(sel[:, :, :], rep(w["ident"][0:E, 0:E], 2, P)).then_inc(S["sel"], 1)
                dve.tensor_reduce(b2[:, :], w["b2"], AX.X, ALU.add).then_inc(S["b2"], 1)
                for j in LANES:
                    dve.wait_ge(S["logits"], j + 1)
                    lg = k.ps[j][:, 0, 0:NT * E].rearrange("p (t e) -> p t e", e=E)
                    c.link(dve.tensor_tensor(p[j][:, :, :], lg, rep(w["br"], 1, NT), ALU.add))
                    c.link(dve.tensor_reduce(small[j][:, 0, :], p[j][:, :, :], AX.X, ALU.max))
                    dve.tensor_tensor(p[j][:, :, :], p[j][:, :, :], rep(small[j][:, 0, :], 2, E),
                                      ALU.subtract).then_inc(S["less"], 1)
                for j in LANES:
                    dve.wait_ge(S["exp"], j + 1)
                    c.link(dve.tensor_reduce(small[j][:, 0, :], p[j][:, :, :], AX.X, ALU.add))
                    c.link(dve.reciprocal(small[j][:, 1, :], small[j][:, 0, :]))
                    c.link(dve.tensor_tensor(p[j][:, :, :], p[j][:, :, :], rep(small[j][:, 1, :], 2, E), ALU.mult))
                    first_largest(dve, c, p[j][:, :, :], small[j][:, 0, :], wk[j][:, :, :], small[j][:, 1, :],
                                  onehot[j][:, :, :], w["down8"])
                    dve.tensor_copy(small[j][:, 0, :], small[j][:, 1, :]).then_inc(S["onehot"], 1)

                def masked(n):
                    j = n % 2
                    dve.wait_ge(S["picked"], n + 1)
                    if n >= 2:
                        dve.wait_ge(S["h_ps"], FC * (n - 1))
                    dve.tensor_tensor(xm[j][:, :], k.XT[j][:, :], k.ps[j][:, 0, :], ALU.mult).then_inc(S["xm"], 1)

                masked(0)
                masked(1)
                for n in range(UNITS):
                    e, j = n // 2, n % 2
                    for f in range(1, FC, 2):
                        dve.wait_ge(S["h_ps"], FC * n + f + 1)
                        if n >= 2:
                            dve.wait_ge(S["used"], n - 1)
                        dve.tensor_scalar(hT[j][:, f, :], k.ps[j][:, 2, :], w["b1"][:, e * FC + f:e * FC + f + 1],
                                          0.0, ALU.add, ALU.max).then_inc(S["h_dve"], 1)
                    if n + 2 < UNITS:
                        masked(n + 2)
                tail.vector(dve, c)

            @block.gpsimd
            def _(pool):
                tail.gpsimd(pool)
        k.close()



def l3_attention(k):
    nc, w = k.nc, k.w
    UNITS = 2 * NT * H
    CH = 4
    BLOCKS, BLOCK = 8, 64
    S = k.signals("q_ps q k_ps k v_ps v blk r1 h1 r2 keep scores max exp pT_ps pT pv attn a_ps aT y step astep"
                  + LN_SIGNALS + TAIL_SIGNALS)
    with k.scratch():
        st = [k.tmp(f"stats{j}", [P, NT, 10]) for j in LANES]
        qT = [k.tmp(f"qT{j}", [P, CH, T]) for j in LANES]
        kT = [k.tmp(f"kT{j}", [P, CH, T]) for j in LANES]
        V = [k.tmp(f"V{j}", [P, NT, D]) for j in LANES]
        blk = k.tmp("blk", [P, CH, BLOCKS]); h1 = k.tmp("h1", [P, BLOCKS]); new8 = k.tmp("new8", [P, BLOCKS])
        kq = k.tmp("kq", [P, 2, NT]); pair = k.tmp("pair", [P, NT, BLOCKS])
        mask = k.tmp("mask", [P, NT, T], BF16)
        prob = [k.tmp(f"prob{j}", [P, 2, T]) for j in LANES]
        nmax = [k.tmp(f"nmax{j}", [P, 2]) for j in LANES]
        rs = [k.tmp(f"rs{j}", [P, 2, H]) for j in LANES]
        pT = [k.tmp(f"pT{j}", [P, T]) for j in LANES]
        attn = [k.tmp(f"attn{j}", [P, NT, D]) for j in LANES]
        aT = [k.tmp(f"aT{j}", [P, T]) for j in LANES]
        tail = Tail(k, S, st, via=1, ready="y", bias=w["b_out"], yT=pT)

        def unit(n):
            j, u = n % 2, n // 2
            return j, u, u // H, u % H

        with nc.Block(no_gpsimd_drain=True) as block:

            @block.tensor
            def _(pe):
                k.have(pe, "L3", "const")
                for which, wt in (("q", w["q3"]), ("k", w["k3"])):
                    for c in range(CH):
                        for j in LANES:
                            i = 2 * c + j + (2 * CH if which == "k" else 0)
                            if i >= 4:
                                before = i - 4
                                pe.wait_ge(S["q"], before + 1) if before < 2 * CH else \
                                    pe.wait_ge(S["k"], before - 2 * CH + 1)
                            pe.matmul(k.ps[j][:, c % 2, :], wt[:, c * P:(c + 1) * P], k.XT[j][:, :],
                                      start=True, stop=True).then_inc(S[which + "_ps"], 1)
                for j in LANES:
                    for t in range(NT):
                        ins = pe.matmul(k.ps[j][:, 3, t * P:(t + 1) * P], k.XT[j][:, t * P:(t + 1) * P], w["v3"],
                                        start=True, stop=True)
                    ins.then_inc(S["v_ps"], 1)
                pe.wait_ge(S["blk"], 1)
                for c in range(CH):
                    ins = pe.matmul(k.ps[0][:, 2, 0:BLOCKS], w["r1"][:, c * P:(c + 1) * P], blk[:, c, :],
                                    start=(c == 0), stop=(c == CH - 1))
                ins.then_inc(S["r1"], 1)
                pe.wait_ge(S["h1"], 1)
                pe.matmul(k.ps[1][:, 2, 0:BLOCKS], w["r2"], h1[:, :], start=True, stop=True).then_inc(S["r2"], 1)
                pe.wait_ge(S["keep"], 1)
                pe.wait_ge(S["k"], 2 * CH)
                pe.wait_ge(S["v"], 2)

                def scores(n):
                    j, u, t, h = unit(n)
                    if n >= 4:
                        pe.wait_ge(S["exp"], n - 3)
                    c, r, nk = h // 4, 32 * (h % 4), (t + 1) * P
                    pe.matmul(k.ps[j][:, u % 2, 0:nk], qT[j][r:r + DH, c, t * P:(t + 1) * P],
                              kT[j][r:r + DH, c, 0:nk], start=True, stop=False)
                    pe.matmul(k.ps[j][:, u % 2, 0:nk], k.ident16[:, :], mask[:, t, 0:nk], start=False,
                              stop=True).then_inc(S["scores"], 1)

                def transposes(n):
                    j, u, t, h = unit(n)
                    pe.wait_ge(S["exp"], n + 1)
                    if n >= 2:
                        pe.wait_ge(S["pT"], n - 1)
                    for b in range(t + 1):
                        ins = pe.transpose(k.ps[j][:, 2, b * P:(b + 1) * P], prob[j][:, u % 2, b * P:(b + 1) * P],
                                           w["ident"])
                    ins.then_inc(S["pT_ps"], 1)

                def values(n):
                    j, u, t, h = unit(n)
                    pe.wait_ge(S["pT"], n + 1)
                    if h == 0 and t > 0:
                        pe.wait_ge(S["attn"], 2 * (t - 1) + j + 1)
                    for b in range(t + 1):
                        ins = pe.matmul(k.ps[j][:, 3, h * DH:(h + 1) * DH], pT[j][:, b * P:(b + 1) * P],
                                        V[j][:, b, h * DH:(h + 1) * DH], start=(b == 0), stop=(b == t))
                    ins.then_inc(S["pv"], 1)

                for n in range(UNITS + 3):
                    if n < UNITS:
                        scores(n)
                    if 0 <= n - 2 < UNITS:
                        transposes(n - 2)
                    if 0 <= n - 3 < UNITS:
                        values(n - 3)
                for j in LANES:
                    pe.wait_ge(S["attn"], 2 * (NT - 1) + j + 1)
                    for t in range(NT):
                        ins = pe.transpose(k.ps[j][:, 2, t * P:(t + 1) * P], attn[j][:, t, :], w["ident"])
                    ins.then_inc(S["a_ps"], 1)
                for j in LANES:
                    pe.wait_ge(S["aT"], j + 1)
                    pe.matmul(k.ps[j][:, 1, :], w["o3"], aT[j][:, :], start=True, stop=True).then_inc(S["y"], 1)
                tail.tensor(pe)

            @block.scalar
            def _(act):
                k.have(act, "vec")
                for which, dst, scale in (("q", qT, float(D) ** -0.5), ("k", kT, 1.0)):
                    for c in range(CH):
                        for j in LANES:
                            act.wait_ge(S[which + "_ps"], 2 * c + j + 1)
                            act.activation(dst[j][:, c, :], k.ps[j][:, c % 2, :], ACT.Copy,
                                           scale=scale).then_inc(S[which], 1)
                act.wait_ge(S["r1"], 1)
                act.activation(h1[:, :], k.ps[0][:, 2, 0:BLOCKS], ACT.Relu, bias=w["b_r1"],
                               scale=1.0 / BLOCK).then_inc(S["h1"], 1)
                for n in range(UNITS + 2):
                    if n < UNITS:
                        j, u, t, h = unit(n)
                        nk = (t + 1) * P
                        act.wait_ge(S["max"], n + 1)
                        if n >= 4:
                            act.wait_ge(S["pT_ps"], n - 3)
                        if h == 0 and t >= 2:
                            act.wait_ge(S["attn"], 2 * (t - 2) + j + 1)
                        act.activation(prob[j][:, u % 2, 0:nk], k.ps[j][:, u % 2, 0:nk], ACT.Exp,
                                       bias=nmax[j][:, u % 2:u % 2 + 1],
                                       accum_out=rs[j][:, t % 2, h:h + 1]).then_inc(S["exp"], 1)
                    if n >= 2:
                        j, u, t, h = unit(n - 2)
                        nk = (t + 1) * P
                        act.wait_ge(S["pT_ps"], n - 1)
                        if n - 2 >= 2:
                            act.wait_ge(S["pv"], n - 3)
                        act.activation(pT[j][:, 0:nk], k.ps[j][:, 2, 0:nk], ACT.Copy).then_inc(S["pT"], 1)
                for j in LANES:
                    act.wait_ge(S["a_ps"], j + 1)
                    act.activation(aT[j][:, :], k.ps[j][:, 2, :], ACT.Copy).then_inc(S["aT"], 1)
                tail.scalar(act)

            @block.vector
            def _(dve):
                k.have(dve, "vec", "const")
                c = Chain(dve, S["step"])
                dve.wait_ge(S["k"], 2 * (CH - 1) + 1)
                dve.tensor_reduce(blk[:, :, :], kT[0][:, :, :].rearrange("p c (b n) -> p c b n", n=BLOCK), AX.X,
                                  ALU.add).then_inc(S["blk"], 1)
                for j in LANES:
                    dve.wait_ge(S["v_ps"], j + 1)
                    dve.tensor_copy(V[j][:, :, :].rearrange("p t n -> p (t n)"), k.ps[j][:, 3, :]).then_inc(S["v"], 1)
                dve.wait_ge(S["r2"], 1)
                c.link(dve.tensor_scalar(new8[:, :], k.ps[1][:, 2, 0:BLOCKS], w["b_r2"], 0.0, ALU.add, ALU.is_gt))
                c.link(dve.tensor_scalar(new8[:, :], new8[:, :], k.first_pair[:, :], None, ALU.mult))
                c.link(dve.tensor_tensor(k.keep8[:, :], k.keep8[:, :], new8[:, :], ALU.max))
                both = k.keep8[:, :].rearrange("p (t two) -> p two t", two=2)
                dve.tensor_scalar(kq[:, 0, :], both[:, 0, :], w["low"], None, ALU.mult)
                c.link(dve.tensor_scalar(kq[:, 1, :], both[:, 1, :], w["high"], None, ALU.mult))
                c.link(dve.tensor_tensor(kq[:, 0, :], kq[:, 0, :], kq[:, 1, :], ALU.add))
                c.link(dve.tensor_tensor(pair[:, :, :], rep(k.keep8[:, :], 1, NT), rep(kq[:, 0, :], 2, BLOCKS),
                                         ALU.mult))
                c.link(dve.tensor_scalar(pair[:, :, :], pair[:, :, :], FAR, -FAR, ALU.mult, ALU.add))
                for t in range(NT):
                    if t > 0:
                        dve.tensor_copy(mask[:, t, 0:t * P].rearrange("p (b n) -> p b n", n=BLOCK),
                                        rep(pair[:, t, 0:2 * t], 2, BLOCK))
                    ins = dve.tensor_tensor(mask[:, t, t * P:(t + 1) * P].rearrange("p (b n) -> p b n", n=BLOCK),
                                            rep(pair[:, t, 2 * t:2 * t + 2], 2, BLOCK),
                                            w["causal"].rearrange("p (b n) -> p b n", n=BLOCK), ALU.add)
                ins.then_inc(S["keep"], 1)
                for n in range(UNITS + 3):
                    if n < UNITS:
                        j, u, t, h = unit(n)
                        dve.wait_ge(S["scores"], n + 1)
                        if n >= 4:
                            dve.wait_ge(S["exp"], n - 3)
                        dve.tensor_reduce(nmax[j][:, u % 2:u % 2 + 1], k.ps[j][:, u % 2, 0:(t + 1) * P], AX.X,
                                          ALU.max, negate=True).then_inc(S["max"], 1)
                    if n >= 3:
                        j, u, t, h = unit(n - 3)
                        if h == H - 1:
                            dve.wait_ge(S["pv"], n - 2)
                            c.link(dve.reciprocal(rs[j][:, t % 2, :], rs[j][:, t % 2, :]))
                            dve.tensor_tensor(attn[j][:, t, :].rearrange("p (h d) -> p h d", d=DH),
                                              k.ps[j][:, 3, 0:D].rearrange("p (h d) -> p h d", d=DH),
                                              rep(rs[j][:, t % 2, :], 2, DH), ALU.mult).then_inc(S["attn"], 1)
                tail.vector(dve, c)

            @block.gpsimd
            def _(pool):
                tail.gpsimd(pool)
        k.close()


def l3_bitnet(k):
    nc, w = k.nc, k.w
    S = k.signals("absum total unround tern quant x_ps xqT gu_ps silu hid hscale hq hq_ps hqT y_tile step"
                  + LN_SIGNALS + TAIL_SIGNALS)
    UNITS = 2 * NT
    with k.scratch():
        st = [k.tmp(f"stats{j}", [P, NT, 10]) for j in LANES]
        w3 = k.group["L3"][:, -3 * FF:].rearrange("p (a n) -> p a n", a=3)
        absum = k.tmp("absum", [P, 3]); mean = k.tmp("mean", [P, 3]); inv = k.tmp("inv", [P, 3])
        scaled = k.tmp("scaled", [P, 3, FF]); tern = k.tmp("tern", [P, 3, FF], BF16)
        unround = k.tmp("unround", [P, 1])
        am = [k.tmp(f"am{j}", [P, NT]) for j in LANES]; qs = [k.tmp(f"qs{j}", [P, NT]) for j in LANES]
        sg = [k.tmp(f"sg{j}", [P, NT]) for j in LANES]; su = [k.tmp(f"su{j}", [P, NT]) for j in LANES]
        xq = [k.tmp(f"xq{j}", [P, NT, D]) for j in LANES]
        xqT = [k.tmp(f"xqT{j}", [P, T], BF16) for j in LANES]
        g = [k.tmp(f"g{j}", [P, FF]) for j in LANES]
        hid = [k.tmp(f"hid{j}", [P, FF]) for j in LANES]
        hm = [k.tmp(f"hm{j}", [P, NT]) for j in LANES]; hs = [k.tmp(f"hs{j}", [P, NT]) for j in LANES]
        sd = [k.tmp(f"sd{j}", [P, NT]) for j in LANES]
        hqT = [k.tmp(f"hqT{j}", [P, FC, P], BF16) for j in LANES]
        tail = Tail(k, S, st, y_at=("y_tile", 1, UNITS - 2), tile_scale=sd)
        with nc.Block(no_gpsimd_drain=True) as block:

            @block.tensor
            def _(pe):
                k.have(pe, "const")
                pe.wait_ge(S["absum"], 1)
                pe.matmul(k.ps[0][:, 0, 0:3], w["ones"], absum[:, :], start=True, stop=True).then_inc(S["total"], 1)
                for j in LANES:
                    pe.wait_ge(S["quant"], j + 1)
                    for t in range(NT):
                        ins = pe.transpose(k.ps[j][:, 2, t * P:(t + 1) * P], xq[j][:, t, :], w["ident"])
                    ins.then_inc(S["x_ps"], 1)
                pe.wait_ge(S["tern"], 1)
                pe.wait_ge(S["xqT"], 2)

                def gate_up(n):
                    j, t = n % 2, n // 2
                    if n >= 2:
                        pe.wait_ge(S["hid"], n - 1)
                    for a in range(2):
                        ins = pe.matmul(k.ps[j][:, a, :], xqT[j][:, t * P:(t + 1) * P], tern[:, a, :],
                                        start=True, stop=True)
                    ins.then_inc(S["gu_ps"], 1)

                def turn(n):
                    j, t = n % 2, n // 2
                    pe.wait_ge(S["hq"], n + 1)
                    if n >= 2:
                        pe.wait_ge(S["hqT"], n - 1)
                    for f in range(FC):
                        ins = pe.transpose(k.ps[j][:, 2, f * P:(f + 1) * P], hid[j][:, f * P:(f + 1) * P], w["ident"])
                    ins.then_inc(S["hq_ps"], 1)

                def down(n):
                    j, t = n % 2, n // 2
                    pe.wait_ge(S["hqT"], n + 1)
                    for f in range(FC):
                        ins = pe.matmul(k.ps[j][:, 3, t * P:(t + 1) * P], hqT[j][:, f, :],
                                        tern[:, 2, f * P:(f + 1) * P], start=(f == 0), stop=(f == FC - 1))
                    ins.then_inc(S["y_tile"], 1)

                for n in range(UNITS + 2):
                    if n < UNITS:
                        gate_up(n)
                    if 0 <= n - 1 < UNITS:
                        turn(n - 1)
                    if 0 <= n - 2 < UNITS:
                        down(n - 2)
                tail.tensor(pe)

            @block.scalar
            def _(act):
                for j in LANES:
                    act.wait_ge(S["x_ps"], j + 1)
                    act.wait_ge(S["unround"], 1)
                    act.activation(xqT[j][:, :], k.ps[j][:, 2, :], ACT.Identity, bias=unround[:, :],
                                   scale=1.0).then_inc(S["xqT"], 1)
                act.wait_ge(S["hscale"], 1)
                for n in range(UNITS + 1):
                    if n < UNITS:
                        j, t = n % 2, n // 2
                        act.wait_ge(S["gu_ps"], n + 1)
                        act.activation(g[j][:, :], k.ps[j][:, 0, :], ACT.Silu,
                                       scale=sg[j][:, t:t + 1]).then_inc(S["silu"], 1)
                    if n >= 1:
                        j, t = (n - 1) % 2, (n - 1) // 2
                        act.wait_ge(S["hq_ps"], n)
                        if n - 1 >= 2:
                            act.wait_ge(S["y_tile"], n - 2)
                        act.activation(hqT[j][:, :, :].rearrange("p f n -> p (f n)"), k.ps[j][:, 2, :], ACT.Identity,
                                       bias=unround[:, :], scale=1.0).then_inc(S["hqT"], 1)
                tail.scalar(act)

            @block.vector
            def _(dve):
                k.have(dve, "L3")
                c = Chain(dve, S["step"])
                dve.tensor_reduce(absum[:, :], w3, AX.X, ALU.add, apply_absolute_value=True).then_inc(S["absum"], 1)
                n = {}
                for j in LANES:
                    n[j] = c.mark(dve.tensor_reduce(am[j][:, :], k.X[j][:, :, :], AX.X, ALU.max,
                                                    apply_absolute_value=True))
                dve.wait_ge(S["total"], 1)
                c.link(dve.tensor_scalar(mean[:, :], k.ps[0][:, 0, 0:3], 1.0 / (D * FF), 1e-5, ALU.mult, ALU.max))
                c.link(dve.reciprocal(inv[:, :], mean[:, :]))
                for j in LANES:
                    c.link(dve.tensor_scalar(am[j][:, :], am[j][:, :], 1e-5, None, ALU.max))
                    c.link(dve.reciprocal(qs[j][:, :], am[j][:, :]))
                    c.link(dve.tensor_scalar(qs[j][:, :], qs[j][:, :], 127.0, None, ALU.mult))
                    for t in range(NT):
                        ins = dve.tensor_scalar(xq[j][:, t, :], k.X[j][:, t, :], qs[j][:, t:t + 1], 127.0,
                                                ALU.mult, ALU.min)
                    c.link(ins)
                    dve.tensor_scalar(xq[j][:, :, :], xq[j][:, :, :], -128.0, ROUND, ALU.max,
                                      ALU.add).then_inc(S["quant"], 1)
                for a in range(3):
                    ins = dve.tensor_scalar(scaled[:, a, :], w3[:, a, :], inv[:, a:a + 1], ROUND, ALU.mult, ALU.add)
                c.link(ins)
                c.link(dve.tensor_scalar(scaled[:, :, :], scaled[:, :, :], ROUND, 1.0, ALU.subtract, ALU.min))
                dve.tensor_scalar(tern[:, :, :], scaled[:, :, :], -1.0, None, ALU.max).then_inc(S["tern"], 1)
                for j in LANES:
                    for dst, a in ((sg, 0), (su, 1)):
                        ins = dve.tensor_scalar(dst[j][:, :], am[j][:, :], mean[:, a:a + 1], 1.0 / 127.0,
                                                ALU.mult, ALU.mult)
                ins.then_inc(S["hscale"], 1)
                dve.wait_ge(S["hscale"], 1)
                for n in range(UNITS):
                    j, t = n % 2, n // 2
                    dve.wait_ge(S["silu"], n + 1)
                    if n >= 2:
                        dve.wait_ge(S["hq_ps"], n - 1)
                    ins = dve.scalar_tensor_tensor(out=hid[j][:, :], in0=k.ps[j][:, 1, :], scalar=su[j][:, t:t + 1],
                                                   in1=g[j][:, :], op0=ALU.mult, op1=ALU.mult)
                    ins.then_inc(S["hid"], 1)
                    dve.wait_ge(S["hid"], n + 1)
                    one = slice(t, t + 1)
                    c.link(dve.tensor_reduce(hm[j][:, one], hid[j][:, :], AX.X, ALU.max, apply_absolute_value=True))
                    c.link(dve.tensor_scalar(hm[j][:, one], hm[j][:, one], 1e-5, None, ALU.max))
                    dve.tensor_scalar(sd[j][:, one], hm[j][:, one], mean[:, 2:3], 1.0 / 127.0, ALU.mult, ALU.mult)
                    c.link(dve.reciprocal(hs[j][:, one], hm[j][:, one]))
                    c.link(dve.tensor_scalar(hs[j][:, one], hs[j][:, one], 127.0, None, ALU.mult))
                    c.link(dve.tensor_scalar(hid[j][:, :], hid[j][:, :], hs[j][:, one], 127.0, ALU.mult, ALU.min))
                    dve.tensor_scalar(hid[j][:, :], hid[j][:, :], -128.0, ROUND, ALU.max,
                                      ALU.add).then_inc(S["hq"], 1)
                tail.vector(dve, c)

            @block.gpsimd
            def _(pool):
                pool.memset(unround[:, :], -ROUND).then_inc(S["unround"], 1)
                tail.gpsimd(pool)
        k.close()



def build(nc, dram):
    with ExitStack() as stack:
        k = Net(nc, stack, dram)
        w = k.w
        setup(k)
        with nc.Fori(0, B // 2) as g:
            load_pair(k, g)
            l0_state_space(k)
            cross_attention(k, w["q0"], w["k0"], w["v0"], w["o0"], "L0", wide=False, bias=0.0)
            l0_signs(k)
            l1_quaternion(k)
            cross_attention(k, w["xq1"], w["xk1"], w["xv1"], w["xo1"], "L1", wide=True, bias=w["xbo1"])
            l1_mixture(k)
            l2_linear_attention(k)
            l2_perceiver(k)
            l2_switch(k)
            l3_attention(k)
            cross_attention(k, w["xq3"], w["xk3"], w["xv3"], w["xo3"], "L3", wide=False, bias=0.0, mask=1)
            l3_bitnet(k)
            store_pair(k, g)


def layout(i):
    import numpy as np

    f32 = np.float32

    def chunks(a):
        c = a.shape[0] // P
        return np.ascontiguousarray(a.reshape(c, P, -1).transpose(1, 0, 2).reshape(P, -1))

    def column(v):
        return np.asarray(v).reshape(-1, P).T

    def padded(v):
        out = np.zeros((P, 1), f32)
        out[:v.shape[0], 0] = v
        return out

    def every(v):
        return np.broadcast_to(np.asarray(v).reshape(1, -1), (P, np.asarray(v).size))

    def spread(wt):
        out = np.zeros((D, H, 32), f32)
        out[:, :, 0:DH] = wt.reshape(D, H, DH)
        return out.reshape(D, H * 32)

    qkv = i["L3_attn_w_qkv"]
    r1 = np.zeros((H, 32, P), f32)
    r1[:, 0:DH] = i["L3_attn_w_r1"].T.reshape(H, DH, P)
    part = {
        "gate": i["L0_attn_Wg"].T, "inB": i["L0_attn_WB"].T, "Wout": i["L0_attn_Wout"].T,
        "q0": i["L0_xattn_Wq"], "o0": i["L0_xattn_Wo"],
        "k1": i["L1_attn_Wk"].T, "v1": i["L1_attn_Wv"].T, "o1": i["L1_attn_Wo"].T,
        "xq1": i["L1_xattn_Wq"], "xo1": chunks(i["L1_xattn_Wo"]), "router1": i["L1_ffn_w_router"],
        "wi": i["L1_ffn_wi"].transpose(1, 0, 2).reshape(D, E * FF),
        "wo": i["L1_ffn_wo"].reshape(E, FC, P, D).transpose(2, 0, 1, 3).reshape(P, E * FF),
        "qkv2": np.concatenate([i["L2_attn_q_w"].T, i["L2_attn_k_w"].T, i["L2_attn_v_w"].T], 1),
        "o2": i["L2_attn_o_w"].T, "fc": i["L2_attn_fc_w"].T, "proj": chunks(i["L2_attn_proj_w"].T),
        "xqkv2": np.concatenate([i["L2_xattn_Wq"].T, i["L2_xattn_Wlkv"].T], 1),
        "xo2": i["L2_xattn_Wo"].T, "router2": i["L2_ffn_Wr"],
        "W1": i["L2_ffn_W1"].transpose(1, 0, 2).reshape(D, E * FF),
        "W2": i["L2_ffn_W2"].reshape(E, FC, P, D).transpose(2, 0, 1, 3).reshape(P, E * FF),
        "q3": spread(qkv[0:D].T), "k3": spread(qkv[D:2 * D].T), "v3": qkv[2 * D:].T,
        "r1": chunks(r1.reshape(H * 32, P)), "r2": np.broadcast_to(i["L3_attn_w_r2"].T, (P, P)),
        "o3": i["L3_attn_w_out"].T, "xq3": i["L3_xattn_Wq"], "xo3": i["L3_xattn_Wo"],
        "wgate": i["L3_ffn_w_gate"].T, "wup": i["L3_ffn_w_up"].T, "wdown": chunks(i["L3_ffn_w_down"].T),
        "k0": i["L0_xattn_Wk"], "v0": i["L0_xattn_Wv"], "xk1": i["L1_xattn_Wk"], "xv1": i["L1_xattn_Wv"],
        "xkv2": i["L2_xattn_Wkv"].T, "xk3": i["L3_xattn_Wk"], "xv3": i["L3_xattn_Wv"],
        "bg": padded(i["L0_attn_bg"]), "A_log": padded(i["L0_attn_A_log"]), "D": column(i["L0_attn_D"]),
        "gamma": column(i["L0_attn_gamma"]), "beta": column(i["L0_attn_beta"]),
        "bout": column(i["L0_attn_bout"]),
        "s0": every(i["L0_ffn_s0"]), "s1": every(i["L0_ffn_s1"]), "s2": every(i["L0_ffn_s2"]),
        "ln_g": column(i["L1_attn_ln_g"]), "ln_b": column(i["L1_attn_ln_b"]), "bo1": column(i["L1_attn_bo"]),
        "xbo1": column(i["L1_xattn_bo"]),
        "ln1_w": column(i["L2_attn_ln1_w"]), "ln1_b": column(i["L2_attn_ln1_b"]),
        "o_b": column(i["L2_attn_o_b"]), "ln2_w": column(i["L2_attn_ln2_w"]),
        "ln2_b": column(i["L2_attn_ln2_b"]), "fc_b": column(i["L2_attn_fc_b"]),
        "proj_b": column(i["L2_attn_proj_b"]),
        "ln_x_g": padded(i["L2_xattn_ln_x_g"]), "ln_x_b": padded(i["L2_xattn_ln_x_b"]),
        "ln_l_g": column(i["L2_xattn_ln_l_g"]), "ln_l_b": column(i["L2_xattn_ln_l_b"]),
        "qn_g": column(np.concatenate([i["L2_xattn_qn_g"]] * 2)),
        "kn_g": column(np.concatenate([i["L2_xattn_kn_g"]] * 2)), "xbo2": column(i["L2_xattn_bo"]),
        "b1": column(i["L2_ffn_b1"].reshape(-1)), "b2": i["L2_ffn_b2"].T,
        "b_r1": column(i["L3_attn_b_r1"]), "b_r2": every(i["L3_attn_b_r2"]), "b_out": column(i["L3_attn_b_out"]),
        "bk1": every(i["L1_attn_bk"]), "bv1": every(i["L1_attn_bv"]),
        "bqkv2": every(np.concatenate([i["L2_attn_q_b"], i["L2_attn_k_b"], i["L2_attn_v_b"]])),
        "br": every(i["L2_ffn_br"]), "WC": i["L0_attn_WC"].T,
    }
    row, col = np.arange(P)[:, None], np.arange(P)[None, :]
    restart = np.ones((P, E, 16), f32)
    restart[:, :, 0] = 0.0
    part.update({
        "ident": (row == col), "tri": (row <= col), "ones": np.ones((P, P)),
        "headmask": row // DH == np.arange(H)[None, :],
        "rpos": (np.arange(NT)[None, :] * P + row + 1.0) ** -0.5,
        "slot": np.broadcast_to(np.arange(CAP), (P, CAP)), "down8": np.broadcast_to(E - np.arange(E), (P, E)),
        "causal": np.where(col <= row, 0.0, -NEVER), "low": row < 64, "high": row >= 64,
        "restart": restart.reshape(P, -1),
    })

    def pack(columns):
        arrays = [np.asarray(part[name]).astype(f32) if name in dict(CONSTS) else part[name] for name, _ in columns]
        for (name, n), a in zip(columns, arrays):
            assert a.shape[1] == n, (name, a.shape, n)
        return np.ascontiguousarray(np.concatenate(arrays, 1))

    out = {group: pack(columns) for group, columns in WEIGHTS.items()}
    out.update({"ctxw": pack(CTX_WEIGHTS), "vec": pack(VECTORS), "rows": pack(ROWS),
                "const": pack(CONSTS), "WC": pack([("WC", D)])})
    out.update({"x": i["x"], "ctx": i["ctx_768"],
                "ctxT": np.ascontiguousarray(i["ctx_768"].transpose(0, 2, 1)),
                "mask0": i["mask_BxS2_bk0"], "mask1": i["mask_BxS2_bf1"],
                "k0": i["L0_ffn_k0"], "k1": i["L0_ffn_k1"], "k2": i["L0_ffn_k2"]})
    return out


def kernel(**inputs):
    import numpy as np
    import concourse.bacc as bacc
    from concourse.bass_utils import run_bass_kernel_spmd as run

    arrays = layout({name: np.asarray(a) for name, a in inputs.items()})
    nc = bacc.Bacc("TRN2", target_bir_lowering=False, num_devices=1)
    dram, sent = {}, {}
    for name, a in arrays.items():
        a = np.ascontiguousarray(a)
        sent["in_" + name + "_dram"] = a
        dram[name] = nc.dram_tensor("in_" + name + "_dram", a.shape, mybir.dt.from_np(a.dtype),
                                    kind="ExternalInput").ap()
    dram["out"] = nc.dram_tensor("out_dram", (B, T, D), F32, kind="ExternalOutput").ap()
    build(nc, dram)
    return run(nc, [sent], core_ids=[0]).results[0]["out_dram"]
```

```python
from contextlib import ExitStack

import concourse.bass as bass
from concourse import mybir

F32 = mybir.dt.float32
BF16 = mybir.dt.bfloat16
U8 = mybir.dt.uint8
ALU = mybir.AluOpType
ACT = mybir.ActivationFunctionType
AX = mybir.AxisListType

B, T, D = 4, 512, 128
LANES = (0, 1)
P = 128
SIGNALS = 50
NT = T // P
CTX, CD = 77, 96
H = 16
DH = D // H
DW = 64
EPS = 1e-5
E = 8
FF = 512
FC = FF // P
CAP = 80
FAR = 1e30
NEVER = 3e38
ROUND = 12582912.0

WEIGHTS = {
    "L0": [("gate", 64), ("inB", 64), ("Wout", 128), ("q0", 128), ("o0", 128)],
    "L1": [("k1", 128), ("v1", 128), ("o1", 128), ("xq1", 1024), ("xo1", 1024), ("router1", 8)],
    "L1wi": [("wi", E * FF)],
    "L1wo": [("wo", E * FF)],
    "L2": [("qkv2", 384), ("o2", 128), ("fc", 512), ("proj", 512),
           ("xqkv2", 384), ("xo2", 128), ("router2", 8)],
    "L2w1": [("W1", E * FF)],
    "L2w2": [("W2", E * FF)],
    "L3": [("q3", 128), ("k3", 128), ("v3", 128), ("r1", 128), ("r2", 128), ("o3", 128),
           ("xq3", 128), ("xo3", 128), ("wgate", 512), ("wup", 512), ("wdown", 512)],
}
CTX_WEIGHTS = [("k0", 128), ("v0", 128), ("xk1", 1024), ("xv1", 1024), ("xkv2", 256),
               ("xk3", 128), ("xv3", 128)]
VECTORS = [("bg", 1), ("A_log", 1), ("D", 1), ("gamma", 1), ("beta", 1), ("bout", 1),
           ("s0", 1), ("s1", 1), ("s2", 1), ("ln_g", 1), ("ln_b", 1), ("bo1", 1), ("xbo1", 1),
           ("ln1_w", 1), ("ln1_b", 1), ("o_b", 1), ("ln2_w", 1), ("ln2_b", 1), ("fc_b", FC),
           ("proj_b", 1), ("ln_x_g", 1), ("ln_x_b", 1), ("ln_l_g", 1), ("ln_l_b", 1),
           ("qn_g", 1), ("kn_g", 1), ("xbo2", 1), ("b1", E * FC), ("b2", E),
           ("b_r1", 1), ("b_r2", 1), ("b_out", 1)]
ROWS = [("bk1", 128), ("bv1", 128), ("bqkv2", 384), ("br", 8)]
CONSTS = [("ident", P), ("tri", P), ("ones", P), ("headmask", H), ("rpos", NT), ("slot", CAP),
          ("down8", E), ("low", 1), ("high", 1), ("restart", 16 * E)]
CONSTS16 = [("pick", 2 * 4 * 3 * P), ("extra", P), ("ones_of", 4 * P)]
PARTS_Q = (0, 0, 1, 0, 2, 1)
PARTS_K = (0, 1, 0, 2, 0, 1)
KEEP_ROW = 6 * DH


def places(columns):
    at, out = 0, {}
    for name, n in columns:
        out[name] = (at, at + n)
        at += n
    return out, at


class Chain:

    def __init__(self, eng, sem):
        self.eng, self.sem, self.n = eng, sem, 0

    def mark(self, ins):
        self.n += 1
        ins.then_inc(self.sem, 1)
        return self.n

    def wait(self, n):
        self.eng.wait_ge(self.sem, n)

    def link(self, ins):
        self.wait(self.mark(ins))


def rep(ap, axis, n):
    ap = ap.unsqueeze(axis)
    shape = list(ap.shape)
    shape[axis] = n
    return ap.broadcast_to(shape)


class Net:

    def __init__(self, nc, stack, dram):
        self.nc, self.stack, self.dram = nc, stack, dram
        self.w, self.loaded, self.group = {}, {}, {}
        self.layer_no = 0
        for group, columns in WEIGHTS.items():
            self.hold(group, columns, P)
        self.hold("ctxw", CTX_WEIGHTS, CD)
        self.hold("vec", VECTORS, P)
        self.hold("rows", ROWS, P)
        self.hold("const", CONSTS, P)
        self.hold("WC", [("WC", D)], 64)
        self.signs0 = self.sb("signs0", [P, FF], BF16)
        self.signs1 = self.sb("signs1", [P, FC, FF], BF16)
        self.signs2 = self.sb("signs2", [P, FC, D], BF16)
        self.signs_loaded = self.sem("signs_loaded")
        self.ps = [stack.enter_context(nc.psum_tensor(f"psum_lane{j}", [P, 4, 512], F32)) for j in LANES]
        self.X = [self.sb(f"X{j}", [P, NT, D]) for j in LANES]
        self.XT = [self.sb(f"XT{j}", [P, T]) for j in LANES]
        self.ctxT = [self.sb(f"ctxT{j}", [CD, CTX]) for j in LANES]
        self.ctx = [self.sb(f"ctx{j}", [CTX, CD]) for j in LANES]
        self.maskrow = [[self.sb(f"mask_row{m}{j}", [1, CTX], U8) for j in LANES] for m in (0, 1)]
        self.half = self.sb("minus_half", [P, 4 * NT])
        self.one16 = self.sb("ones_bf16", [1, P], BF16)
        self.ident16 = self.sb("ident_bf16", [P, P], BF16)
        self.tri16 = self.sb("tri_bf16", [P, P], BF16)
        self.ones16 = self.sb("all_ones_bf16", [P, P], BF16)
        self.c16 = self.sb("const_bf16", [P, places(CONSTS16)[1]], BF16)
        for name, (a, b) in places(CONSTS16)[0].items():
            self.w[name] = self.c16[:, a:b]
        self.w["causal"] = self.sb("causal_bf16", [P, P], BF16)[:, :]
        self.first_pair = self.sb("first_pair", [P, 1])
        self.keep8 = self.sb("keep_block", [P, 8])
        self.sets = [[stack.enter_context(nc.semaphore(f"step{a}_{i}")) for i in range(SIGNALS)] for a in range(2)]
        self.turn = 0

    def sb(self, name, shape, dtype=F32):
        return self.stack.enter_context(self.nc.sbuf_tensor(name, shape, dtype))

    def sem(self, name):
        return self.stack.enter_context(self.nc.semaphore(name))

    def hold(self, group, columns, rows):
        where, n = places(columns)
        tile = self.sb("in_" + group, [rows, n])
        self.loaded[group] = self.sem("loaded_" + group)
        self.group[group] = tile
        for name, (a, b) in where.items():
            self.w[name] = tile[:, a:b]

    def signals(self, names):
        names = names.split()
        assert len(names) <= SIGNALS and len(set(names)) == len(names)
        self.turn = 1 - self.turn
        nums = sorted(s.num for s in self.sets[1 - self.turn])
        assert nums[-1] - nums[0] == len(nums) - 1
        self.nc.sync.sem_clear(range(nums[0], nums[-1] + 1))
        return dict(zip(names, self.sets[self.turn]))

    def have(self, eng, *groups):
        for group in groups:
            eng.wait_ge(self.loaded[group], 16)

    def scratch(self):
        self.layer = ExitStack()
        self.layer_no = self.layer_no + 1
        return self.layer

    def tmp(self, name, shape, dtype=F32):
        return self.layer.enter_context(self.nc.sbuf_tensor(f"{name}_{self.layer_no}", shape, dtype))



LN_SIGNALS = " ln_var ln_rs"


def variances(dve, c, S, src, st, n_rows, tiles):
    def stats(j, ts):
        for t in ts:
            ins = dve.bn_stats(st[j][0:n_rows, t, 0:6], src(j, t))
        return c.mark(ins)

    def aggregate(j):
        for t in range(tiles):
            ins = dve.bn_aggr(st[j][0:n_rows, t, 6:8], st[j][0:n_rows, t, 0:6])
        return c.mark(ins)

    def announce(j):
        dve.tensor_scalar(st[j][0:n_rows, 0:tiles, 8], st[j][0:n_rows, 0:tiles, 7], EPS, None,
                          ALU.add).then_inc(S["ln_var"], 1)

    early = (tiles + 1) // 2
    first = stats(0, range(tiles))
    second = stats(1, range(early))
    c.wait(first)
    first = aggregate(0)
    if tiles > early:
        second = stats(1, range(early, tiles))
    c.wait(first)
    announce(0)
    c.wait(second)
    c.wait(aggregate(1))
    announce(1)


def vector_layernorm(k, dve, c, S, src, out, st, done, n_rows=P, tiles=NT, base=0):
    variances(dve, c, S, src, st, n_rows, tiles)
    for j in LANES:
        dve.wait_ge(S["ln_rs"], base + j + 1)
        for t in range(tiles):
            ins = dve.tensor_scalar(out(j, t), src(j, t), st[j][0:n_rows, t, 6:7],
                                    st[j][0:n_rows, t, 9:10], ALU.subtract, ALU.mult)
        ins.then_inc(S[done], 1)


def pool_layernorm(k, pool, S, st, n_rows=P, tiles=NT, base=0):
    for j in LANES:
        pool.wait_ge(S["ln_var"], base + j + 1)
        pool.tensor_tensor(st[j][0:n_rows, 0:tiles, 9], st[j][0:n_rows, 0:tiles, 8],
                           k.half[0:n_rows, 0:tiles], ALU.pow).then_inc(S["ln_rs"], 1)


TAIL_SIGNALS = " tail_yT_sb tail_y tail_x tail_xT"


class Tail:

    def __init__(self, k, S, st, base=0, via=None, ready=None, bias=None, bank=3, yT=None,
                 bank_x=2, x_factor=1.0, y_scale=None, y_at=("tail_y", 1, 0), tile_scale=None, ready_from=0):
        self.k, self.S, self.st, self.base, self.via = k, S, st, base, via
        self.ready, self.bias, self.bank, self.yT = ready, bias, bank, yT
        self.bank_x, self.x_factor, self.y_scale = bank_x, x_factor, y_scale
        self.ready_from = ready_from
        self.tile_scale = tile_scale
        self.y_at = y_at
        self.Y = ([v[:, 0:T].rearrange("p (t n) -> p t n", t=NT) for v in yT] if yT is not None else
                  [k.tmp(f"tail_y{j}", [P, NT, D])[:, :, :] for j in LANES])

    def scalar(self, act):
        k, S = self.k, self.S
        if self.via is not None:
            for j in LANES:
                act.wait_ge(S[self.ready], self.ready_from + j + 1)
                act.activation(self.yT[j][:, 0:T], k.ps[j][:, self.via, :], ACT.Identity,
                               bias=self.bias, scale=1.0).then_inc(S["tail_yT_sb"], 1)
        for j in LANES:
            act.wait_ge(S["tail_xT"], j + 1)
            act.activation(k.XT[j][:, :], k.ps[j][:, self.bank_x, :], ACT.Copy)

    def tensor(self, pe):
        k, S = self.k, self.S
        if self.via is not None:
            for j in LANES:
                pe.wait_ge(S["tail_yT_sb"], j + 1)
                for t in range(NT):
                    ins = pe.transpose(k.ps[j][:, self.bank, t * P:(t + 1) * P],
                                       self.yT[j][:, t * P:(t + 1) * P], k.w["ident"])
                ins.then_inc(S["tail_y"], 1)
        for j in LANES:
            pe.wait_ge(S["tail_x"], j + 1)
            for t in range(NT):
                ins = pe.transpose(k.ps[j][:, self.bank_x, t * P:(t + 1) * P], k.X[j][:, t, :],
                                   k.w["ident"])
            ins.then_inc(S["tail_xT"], 1)

    def vector(self, dve, c):
        k, S = self.k, self.S
        last = {}
        for j in LANES:
            name, each, before = self.y_at
            dve.wait_ge(S[name], before + (j + 1) * each)
            y = k.ps[j][:, self.bank, :]
            x = k.X[j][:, :, :].rearrange("p t n -> p (t n)")
            out = self.Y[j][:, :, :].rearrange("p t n -> p (t n)")
            if self.tile_scale is not None:
                for t in range(NT):
                    ins = dve.scalar_tensor_tensor(out=self.Y[j][:, t, :], in0=y[:, t * P:(t + 1) * P],
                                                   scalar=self.tile_scale[j][:, t:t + 1], in1=k.X[j][:, t, :],
                                                   op0=ALU.mult, op1=ALU.add)
            elif self.y_scale is not None:
                ins = dve.scalar_tensor_tensor(out=out, in0=y, scalar=self.y_scale, in1=x,
                                               op0=ALU.mult, op1=ALU.add)
            else:
                ins = dve.scalar_tensor_tensor(out=out, in0=x, scalar=self.x_factor, in1=y,
                                               op0=ALU.mult, op1=ALU.add)
            last[j] = c.mark(ins)
        for j in LANES:
            c.wait(last[j])
        self.normalise(dve, c)

    def normalise(self, dve, c):
        k, S = self.k, self.S
        variances(dve, c, S, lambda j, t: self.Y[j][:, t, :], self.st, P, NT)
        for j in LANES:
            dve.wait_ge(S["ln_rs"], self.base + j + 1)
            for t in range(NT):
                ins = dve.tensor_scalar(k.X[j][:, t, :], self.Y[j][:, t, :],
                                        self.st[j][:, t, 6:7], self.st[j][:, t, 9:10],
                                        ALU.subtract, ALU.mult)
            ins.then_inc(S["tail_x"], 1)

    def gpsimd(self, pool):
        pool_layernorm(self.k, pool, self.S, self.st, base=self.base)



def setup(k):
    nc = k.nc
    S = k.signals("filled c16_in above arrived")
    with k.scratch(), nc.Block(no_gpsimd_drain=True) as block:
        raw0 = k.tmp("signs0_raw", [P, 2, FF], U8)
        raw1 = k.tmp("signs1_raw", [P, FC, FF], U8)
        raw2 = k.tmp("signs2_raw", [P, FC, D], U8)
        bytes16 = k.tmp("const16_bytes", [P, places(CONSTS16)[1]], U8)
        above = k.tmp("above_diagonal", [P, P])

        @block.sync
        def _(sp):
            for group in ("const", "vec"):
                sp.dma_start(k.group[group][:, :], k.dram[group]).then_inc(k.loaded[group], 16)
            sp.dma_start(raw0[:, :, :], k.dram["k0"].rearrange("(a p) n -> p a n", p=P)).then_inc(k.signs_loaded, 16)
            sp.dma_start(raw1[:, :, :], k.dram["k1"].rearrange("(a p) n -> p a n", p=P)).then_inc(k.signs_loaded, 16)
            sp.dma_start(raw2[:, :, :], k.dram["k2"].rearrange("(a p) n -> p a n", p=P)).then_inc(k.signs_loaded, 16)
            sp.dma_start(bytes16[:, :], k.dram["const16"]).then_inc(S["c16_in"], 16)
            for group in ("L0", "WC", "ctxw"):
                sp.dma_start(k.group[group][:, :], k.dram[group]).then_inc(k.loaded[group], 16)
            load_pair(k, sp, 0, S["arrived"])
            for group in ("L1", "rows", "L1wi", "L1wo", "L2", "L2w1", "L2w2", "L3"):
                sp.dma_start(k.group[group][:, :], k.dram[group]).then_inc(k.loaded[group], 16)

        @block.gpsimd
        def _(pool):
            c = Chain(pool, S["filled"])
            c.mark(pool.memset(k.half[:, :], -0.5))
            c.mark(pool.memset(k.one16[:, :], 1.0))
            c.mark(pool.memset(k.first_pair[:, :], 1.0))
            c.mark(pool.memset(k.keep8[:, :], 0.0))
            pool.wait_ge(k.signs_loaded, 48)
            c.mark(pool.tensor_scalar(k.signs1[:, 0, :], raw1[:, 0, :], 2.0, -1.0, ALU.mult, ALU.add))
            c.wait(c.n)

        @block.vector
        def _(dve):
            k.have(dve, "const", "vec")
            dve.tensor_copy(k.ident16[:, :], k.w["ident"])
            dve.tensor_copy(k.tri16[:, :], k.w["tri"])
            dve.tensor_copy(k.ones16[:, :], k.w["ones"])
            dve.tensor_tensor(above[:, :], k.w["tri"], k.w["ident"], ALU.subtract).then_inc(S["above"], 1)
            dve.wait_ge(S["above"], 1)
            dve.tensor_scalar(k.w["causal"], above[:, :], -NEVER, None, ALU.mult)
            dve.wait_ge(k.signs_loaded, 48)
            dve.tensor_scalar(k.signs1[:, 1:FC, :], raw1[:, 1:FC, :], 2.0, -1.0, ALU.mult, ALU.add)
            dve.tensor_tensor(k.signs0[:, :], raw0[:, 0, :], raw0[:, 1, :], ALU.subtract)
            dve.tensor_scalar(k.signs2[:, :, :], raw2[:, :, :], 2.0, -1.0, ALU.mult, ALU.add)
            dve.wait_ge(S["c16_in"], 16)
            dve.tensor_copy(k.c16[:, :], bytes16[:, :])


def load_pair(k, sp, pair, arrived):
    for j in LANES:
        one = bass.ds(2 * pair + j, 1)
        sp.dma_start(k.X[j][:, :, :],
                     k.dram["x"][one, :, :].rearrange("a (t p) n -> p (a t) n", p=P)).then_inc(arrived, 16)
        sp.dma_start(k.ctxT[j][:, :], k.dram["ctxT"][one, :, :].rearrange("a p n -> p (a n)")).then_inc(arrived, 16)
        sp.dma_start(k.ctx[j][:, :], k.dram["ctx"][one, :, :].rearrange("a p n -> p (a n)")).then_inc(arrived, 16)
        for m in (0, 1):
            sp.dma_start(k.maskrow[m][j][:, :], k.dram[f"mask{m}"][one, :]).then_inc(arrived, 16)
    sp.wait_ge(arrived, 16 * 10)


def turn_pair(k):
    nc = k.nc
    S = k.signals("xT")
    with nc.Block(no_gpsimd_drain=True) as block:

        @block.tensor
        def _(pe):
            k.have(pe, "const")
            for j in LANES:
                for t in range(NT):
                    ins = pe.transpose(k.ps[j][:, 2, t * P:(t + 1) * P], k.X[j][:, t, :], k.w["ident"])
                ins.then_inc(S["xT"], 1)

        @block.scalar
        def _(act):
            for j in LANES:
                act.wait_ge(S["xT"], j + 1)
                act.activation(k.XT[j][:, :], k.ps[j][:, 2, :], ACT.Copy)


def store_pair(k, g):
    nc = k.nc
    assert B == 4
    S = k.signals("stored arrived cleared")
    with nc.Block(no_gpsimd_drain=True) as block:

        @block.sync
        def _(sp):
            for j in LANES:
                out = k.dram["out"][bass.ds(2 * g + j, 1), :, :].rearrange("a (t p) n -> p (a t) n", p=P)
                sp.dma_start(out, k.X[j][:, :, :]).then_inc(S["stored"], 16)
            sp.wait_ge(S["stored"], 32)
            load_pair(k, sp, 1, S["arrived"])

        @block.gpsimd
        def _(pool):
            pool.memset(k.first_pair[:, :], 0.0).then_inc(S["cleared"], 1)
            pool.wait_ge(S["cleared"], 1)



def l0_state_space(k):
    nc, w = k.nc, k.w
    S = k.signals("pre gate scanned hT_ps hT h_tok hn hnT_ps hnT y step act_step"
                  + LN_SIGNALS + TAIL_SIGNALS)
    with k.scratch():
        st = [k.tmp(f"stats{j}", [P, NT, 10]) for j in LANES]
        A = k.tmp("A", [64, 1]); negbg = k.tmp("negbg", [64, 1]); D1 = k.tmp("D1", [P, 1])
        u = [k.tmp(f"u{j}", [64, T]) for j in LANES]
        gate = [k.tmp(f"gate{j}", [64, T]) for j in LANES]
        states = [k.tmp(f"states{j}", [64, T]) for j in LANES]
        hT = [k.tmp(f"hT{j}", [P, T]) for j in LANES]
        hn = [k.tmp(f"hn{j}", [P, NT, D]) for j in LANES]
        hnT = [k.tmp(f"hnT{j}", [P, T]) for j in LANES]
        tail = Tail(k, S, st, base=2, via=1, ready="y", bias=w["bout"], yT=hT)
        with nc.Block(no_gpsimd_drain=True) as block:

            @block.tensor
            def _(pe):
                k.have(pe, "L0", "WC", "const")
                for j in LANES:
                    pe.matmul(k.ps[j][0:64, 0, :], w["gate"], k.XT[j][:, :], start=True, stop=True)
                    pe.matmul(k.ps[j][0:64, 1, :], w["inB"], k.XT[j][:, :], start=True,
                              stop=True).then_inc(S["pre"], 1)
                for j in LANES:
                    pe.wait_ge(S["scanned"], j + 1)
                    pe.matmul(k.ps[j][:, 2, :], w["WC"], states[j][:, :], start=True,
                              stop=True).then_inc(S["hT_ps"], 1)
                for j in LANES:
                    pe.wait_ge(S["hT"], j + 1)
                    for t in range(NT):
                        ins = pe.transpose(k.ps[j][:, 0, t * P:(t + 1) * P], hT[j][:, t * P:(t + 1) * P], w["ident"])
                    ins.then_inc(S["h_tok"], 1)
                for j in LANES:
                    pe.wait_ge(S["hn"], j + 1)
                    for t in range(NT):
                        ins = pe.transpose(k.ps[j][:, 2, t * P:(t + 1) * P], hn[j][:, t, :], w["ident"])
                    ins.then_inc(S["hnT_ps"], 1)
                for j in LANES:
                    pe.wait_ge(S["hnT"], j + 1)
                    pe.matmul(k.ps[j][:, 1, :], w["Wout"], hnT[j][:, :], start=True,
                              stop=True).then_inc(S["y"], 1)
                tail.tensor(pe)

            @block.scalar
            def _(act):
                k.have(act, "vec")
                c = Chain(act, S["act_step"])
                act.activation(A[:, :], w["A_log"][0:64, :], ACT.Exp)
                c.link(act.activation(negbg[:, :], w["bg"][0:64, :], ACT.Copy, scale=-1.0))
                for j in LANES:
                    act.wait_ge(S["pre"], j + 1)
                    act.activation(gate[j][:, :], k.ps[j][0:64, 0, :], ACT.Exp, bias=negbg[:, :],
                                   scale=-1.0).then_inc(S["gate"], 1)
                for j in LANES:
                    act.wait_ge(S["hnT_ps"], j + 1)
                    act.activation(hnT[j][:, :], k.ps[j][:, 2, :], ACT.Identity, bias=w["beta"],
                                   scale=w["gamma"]).then_inc(S["hnT"], 1)
                tail.scalar(act)

            @block.vector
            def _(dve):
                k.have(dve, "vec")
                c = Chain(dve, S["step"])
                dve.tensor_scalar(D1[:, :], w["D"], 1.0, None, ALU.add)
                n = {}
                for j in LANES:
                    dve.wait_ge(S["gate"], j + 1)
                    n[j] = c.mark(dve.tensor_scalar(gate[j][:, :], gate[j][:, :], 1.0, None, ALU.add))
                for j in LANES:
                    c.wait(n[j])
                    n[j] = c.mark(dve.reciprocal(gate[j][:, :], gate[j][:, :]))
                for j in LANES:
                    c.wait(n[j])
                    n[j] = c.mark(dve.tensor_tensor(u[j][:, :], gate[j][:, :], k.ps[j][0:64, 1, :], ALU.mult))
                for j in LANES:
                    c.wait(n[j])
                    dve.tensor_tensor_scan(states[j][:, :], A[:, 0:1].broadcast_to([64, T]), u[j][:, :], 0.0,
                                           ALU.mult, ALU.add).then_inc(S["scanned"], 1)
                for j in LANES:
                    dve.wait_ge(S["hT_ps"], j + 1)
                    dve.scalar_tensor_tensor(out=hT[j][:, :], in0=k.XT[j][:, :], scalar=D1[:, :],
                                             in1=k.ps[j][:, 2, :], op0=ALU.mult,
                                             op1=ALU.add).then_inc(S["hT"], 1)
                for j in LANES:
                    dve.wait_ge(S["h_tok"], j + 1)
                vector_layernorm(k, dve, c, S, lambda j, t: k.ps[j][:, 0, t * P:(t + 1) * P],
                                 lambda j, t: hn[j][:, t, :], st, "hn")
                tail.vector(dve, c)

            @block.gpsimd
            def _(pool):
                pool_layernorm(k, pool, S, st)
                tail.gpsimd(pool)
    


def cross_attention(k, wq, wk, wv, wo, group, wide, bias=None, mask=None):
    nc, w = k.nc, k.w
    HG = 4
    GROUPS = H // HG
    UNITS = 2 * NT * GROUPS
    dh = DW if wide else DH
    inner = H * dh
    KC = inner // P
    VW = dh + 1
    SC = HG * CTX
    scale = float(dh) ** -0.5
    S = k.signals("zeros kT_ps kT kblock v_ps v vones qT_ps qT mask scores less exp pT_ps pT pv attn aT_ps aT y "
                  "step" + LN_SIGNALS + TAIL_SIGNALS)
    with k.scratch():
        st = [k.tmp(f"stats{j}", [P, NT, 10]) for j in LANES]
        kT = [k.tmp(f"kT{j}", [P, H if wide else KC, CTX]) for j in LANES]
        V = [k.tmp(f"V{j}", [CTX, H, VW]) for j in LANES]
        qT = [k.tmp(f"qT{j}", [P, KC, T]) for j in LANES]
        prob = [k.tmp(f"prob{j}", [P, 2, SC]) for j in LANES]
        pT = [k.tmp(f"pT{j}", [CTX, HG * P]) for j in LANES]
        nmax = [k.tmp(f"nmax{j}", [P, 2, HG]) for j in LANES]
        rsum = [k.tmp(f"rsum{j}", [P, H]) for j in LANES]
        attn = [k.tmp(f"attn{j}", [P, (1 if wide else NT), inner]) for j in LANES]
        aT = qT
        if not wide:
            kblock = [k.tmp(f"kblock{j}", [P, H, CTX]) for j in LANES]
        if mask is not None:
            mrow = [k.tmp(f"mrow{j}", [1, HG, CTX], BF16) for j in LANES]
        yT = [prob[j][:, :, :].rearrange("p a n -> p (a n)") for j in LANES]
        tail = Tail(k, S, st, via=1, ready="y", bias=bias, yT=yT)
        VN = min(512, inner)
        TURN, WEIGH, DIVIDE = 3, 4, 5
        LATE = 6

        def heads(hg):
            return [HG * hg + i for i in range(HG)]

        def unit(n):
            j, u = n % 2, n // 2
            return j, u, u // GROUPS, u % GROUPS

        with nc.Block(no_gpsimd_drain=True) as block:

            @block.tensor
            def _(pe):
                k.have(pe, group, "ctxw", "const")
                for j in LANES:
                    for c in range(KC):
                        ins = pe.matmul(k.ps[j][:, c // 4, (c % 4) * CTX:(c % 4 + 1) * CTX],
                                        wk[:, c * P:(c + 1) * P], k.ctxT[j][:, :], start=True, stop=True)
                    ins.then_inc(S["kT_ps"], 1)
                    for c in range(inner // VN):
                        ins = pe.matmul(k.ps[j][0:CTX, 2 + c, 0:VN], k.ctxT[j][:, :],
                                        wv[:, c * VN:(c + 1) * VN], start=True, stop=True)
                    ins.then_inc(S["v_ps"], 1)
                for c in range(KC):
                    for j in LANES:
                        if c < 2:
                            pe.wait_ge(S["kT"], j + 1)
                        else:
                            pe.wait_ge(S["qT"], 2 * (c - 2) + j + 1)
                        pe.matmul(k.ps[j][:, c % 2, :], wq[:, c * P:(c + 1) * P], k.XT[j][:, :],
                                  start=True, stop=True).then_inc(S["qT_ps"], 1)
                if not wide:
                    pe.wait_ge(S["kblock"], 2)
                pe.wait_ge(S["qT"], 2 * KC)
                pe.wait_ge(S["v"], 2)
                pe.wait_ge(S["vones"], 2)
                if mask is not None:
                    pe.wait_ge(S["mask"], 2)

                def scores(n):
                    j, u, t, hg = unit(n)
                    if n >= 4:
                        pe.wait_ge(S["less"], n - 3)
                    bank = k.ps[j][:, u % 2, :]
                    if wide:
                        for i in range(0, HG, 2):
                            h = HG * hg + i
                            ins = pe.matmul(bank[:, i * CTX:(i + 2) * CTX], qT[j][:, h // 2, t * P:(t + 1) * P],
                                            kT[j][:, h:h + 2, :].rearrange("p h n -> p (h n)"),
                                            start=True, stop=True)
                    else:
                        ins = pe.matmul(bank[:, 0:SC], qT[j][:, 0, t * P:(t + 1) * P],
                                        kblock[j][:, HG * hg:HG * hg + HG, :].rearrange("p h n -> p (h n)"),
                                        start=True, stop=mask is None)
                        if mask is not None:
                            ins = pe.matmul(bank[:, 0:SC], k.one16[:, :],
                                            mrow[j][:, :, :].rearrange("p h n -> p (h n)"),
                                            start=False, stop=True)
                    ins.then_inc(S["scores"], 1)

                def transposes(n):
                    j, u, t, hg = unit(n)
                    pe.wait_ge(S["exp"], n + 1)
                    if n >= 2:
                        pe.wait_ge(S["pT"], n - 1)
                    for h in range(HG):
                        ins = pe.transpose(k.ps[j][0:CTX, 2, h * P:(h + 1) * P],
                                           prob[j][:, u % 2, h * CTX:(h + 1) * CTX], w["ident"])
                    ins.then_inc(S["pT_ps"], 1)

                def values(n):
                    j, u, t, hg = unit(n)
                    pe.wait_ge(S["pT"], n + 1)
                    if wide and n >= 2:
                        pe.wait_ge(S["attn"], n - 1)
                    if not wide and hg == 0 and t > 0:
                        pe.wait_ge(S["attn"], 2 * (t - 1) + j + 1)
                    for i, h in enumerate(heads(hg)):
                        at = (0 if wide else hg * HG * VW) + i * VW
                        ins = pe.matmul(k.ps[j][:, 3, at:at + VW], pT[j][:, i * P:(i + 1) * P],
                                        V[j][:, h, :], start=True, stop=True)
                    ins.then_inc(S["pv"], 1)

                for n in range(UNITS + LATE):
                    if n < UNITS:
                        scores(n)
                    if 0 <= n - TURN < UNITS:
                        transposes(n - TURN)
                    if 0 <= n - WEIGH < UNITS:
                        values(n - WEIGH)
                    if wide and n >= LATE:
                        j, u, t, hg = unit(n - LATE)
                        if hg == GROUPS - 1 and j == 1:
                            pe.wait_ge(S["attn"], n - LATE + 1)
                            pe.wait_ge(S["pT"], min(n - TURN + 1, UNITS))
                            for half in range(2):
                                for jj in LANES:
                                    if half == 1:
                                        pe.wait_ge(S["aT"], 4 * t + jj + 1)
                                    for c in range(4):
                                        f = 4 * half + c
                                        ins = pe.transpose(k.ps[jj][:, 2, c * P:(c + 1) * P],
                                                           attn[jj][:, 0, f * P:(f + 1) * P], w["ident"])
                                    ins.then_inc(S["aT_ps"], 1)
                            pe.wait_ge(S["aT"], 4 * t + 4)
                if not wide:
                    for j in LANES:
                        pe.wait_ge(S["attn"], 2 * (NT - 1) + j + 1)
                        for t in range(NT):
                            ins = pe.transpose(k.ps[j][:, 2, t * P:(t + 1) * P], attn[j][:, t, :], w["ident"])
                        ins.then_inc(S["aT_ps"], 1)
                n_aT = 4 * NT if wide else 2
                for j in LANES:
                    pe.wait_ge(S["aT"], n_aT)
                    for c in range(KC):
                        ins = pe.matmul(k.ps[j][:, 1, :], wo[:, c * P:(c + 1) * P], aT[j][:, c, :],
                                        start=(c == 0), stop=(c == KC - 1))
                    ins.then_inc(S["y"], 1)
                tail.tensor(pe)

            @block.scalar
            def _(act):
                k.have(act, "vec")
                for j in LANES:
                    act.wait_ge(S["kT_ps"], j + 1)
                    if wide:
                        act.wait_ge(S["zeros"], j + 1)
                        by_half = kT[j][:, :, :].rearrange("p (c two) n -> p two c n", two=2)
                        for half in range(2):
                            chunks = k.ps[j][:, half, 0:4 * CTX].rearrange("p (c n) -> p c n", c=4)
                            for odd in range(2):
                                r = slice(DW * odd, DW * odd + DW)
                                ins = act.activation(by_half[r, odd, 4 * half:4 * half + 4, :], chunks[r], ACT.Copy)
                    else:
                        ins = act.activation(kT[j][:, 0, :], k.ps[j][:, 0, 0:CTX], ACT.Copy)
                    ins.then_inc(S["kT"], 1)
                for c in range(KC):
                    for j in LANES:
                        act.wait_ge(S["qT_ps"], 2 * c + j + 1)
                        act.activation(qT[j][:, c, :], k.ps[j][:, c % 2, :], ACT.Copy,
                                       scale=scale).then_inc(S["qT"], 1)
                for n in range(UNITS + LATE):
                    m = n - TURN
                    if 0 <= m < UNITS:
                        j, u, t, hg = unit(m)
                        act.wait_ge(S["pT_ps"], m + 1)
                        if m >= 2:
                            act.wait_ge(S["pv"], m - 1)
                        act.activation(pT[j][:, :], k.ps[j][0:CTX, 2, :], ACT.Copy).then_inc(S["pT"], 1)
                    if wide and n >= LATE:
                        j, u, t, hg = unit(n - LATE)
                        if hg == GROUPS - 1 and j == 1:
                            for half in range(2):
                                for jj in LANES:
                                    act.wait_ge(S["aT_ps"], 4 * t + 2 * half + jj + 1)
                                    act.activation(aT[jj][:, 4 * half:4 * half + 4, t * P:(t + 1) * P],
                                                   k.ps[jj][:, 2, :].rearrange("p (c n) -> p c n", c=4),
                                                   ACT.Copy).then_inc(S["aT"], 1)
                    if n < UNITS:
                        j, u, t, hg = unit(n)
                        act.wait_ge(S["less"], n + 1)
                        act.activation(prob[j][:, u % 2, :], prob[j][:, u % 2, :], ACT.Exp).then_inc(S["exp"], 1)
                if not wide:
                    for j in LANES:
                        act.wait_ge(S["aT_ps"], j + 1)
                        act.activation(aT[j][:, 0, :], k.ps[j][:, 2, :], ACT.Copy).then_inc(S["aT"], 1)
                tail.scalar(act)

            @block.vector
            def _(dve):
                k.have(dve, "const")
                c = Chain(dve, S["step"])
                for j in LANES:
                    dve.wait_ge(S["v_ps"], j + 1)
                    for a in range(inner // VN):
                        hh = VN // dh
                        ins = dve.tensor_copy(V[j][:, a * hh:(a + 1) * hh, 0:dh],
                                              k.ps[j][0:CTX, 2 + a, 0:VN].rearrange("p (h d) -> p h d", d=dh))
                    ins.then_inc(S["v"], 1)
                if not wide:
                    for j in LANES:
                        dve.wait_ge(S["kT"], j + 1)
                        dve.tensor_tensor(kblock[j][:, :, :], rep(kT[j][:, 0, :], 1, H),
                                          rep(w["headmask"], 2, CTX), ALU.mult).then_inc(S["kblock"], 1)
                if mask is not None:
                    for j in LANES:
                        dve.tensor_scalar(mrow[j][:, :, :], rep(k.maskrow[mask][j][:, :], 1, HG), FAR, -FAR,
                                          ALU.mult, ALU.add).then_inc(S["mask"], 1)

                def normalise(n):
                    j, u, t, hg = unit(n)
                    if wide:
                        dve.wait_ge(S["pv"], n + 1)
                        if hg == 0 and t > 0:
                            dve.wait_ge(S["aT_ps"], 4 * (t - 1) + 2 + j + 1)
                        count = HG
                        a = attn[j][:, 0, HG * hg * dh:HG * (hg + 1) * dh].rearrange("p (h d) -> p h d", d=dh)
                    else:
                        if hg != GROUPS - 1:
                            return
                        dve.wait_ge(S["pv"], n + 1)
                        count = H
                        a = attn[j][:, t, :].rearrange("p (h d) -> p h d", d=dh)
                    o = k.ps[j][:, 3, 0:count * VW].rearrange("p (h d) -> p h d", d=VW)
                    c.link(dve.reciprocal(rsum[j][:, 0:count], o[:, :, dh]))
                    dve.tensor_tensor(a, o[:, :, 0:dh], rep(rsum[j][:, 0:count], 2, dh),
                                      ALU.mult).then_inc(S["attn"], 1)

                for n in range(UNITS + DIVIDE):
                    if n >= DIVIDE:
                        normalise(n - DIVIDE)
                    if n < UNITS:
                        j, u, t, hg = unit(n)
                        dve.wait_ge(S["scores"], n + 1)
                        s3 = k.ps[j][:, u % 2, 0:SC].rearrange("p (h n) -> p h n", n=CTX)
                        c.link(dve.tensor_reduce(nmax[j][:, u % 2, :], s3, AX.X, ALU.max, negate=True))
                        if n >= 4:
                            dve.wait_ge(S["pT_ps"], n - 3)
                        dve.tensor_tensor(prob[j][:, u % 2, :].rearrange("p (h n) -> p h n", n=CTX), s3,
                                          rep(nmax[j][:, u % 2, :], 2, CTX), ALU.add).then_inc(S["less"], 1)
                tail.vector(dve, c)

            @block.gpsimd
            def _(pool):
                if wide:
                    for j in LANES:
                        pool.memset(kT[j][:, :, :], 0.0).then_inc(S["zeros"], 1)
                for j in LANES:
                    pool.memset(V[j][:, :, dh:VW], 1.0).then_inc(S["vones"], 1)
                tail.gpsimd(pool)
    

def l0_signs(k):
    nc, w = k.nc, k.w
    S = k.signals("signs signs1 scales h1_ps h1 h2_ps h2 yT_ps step" + LN_SIGNALS + TAIL_SIGNALS)
    with k.scratch():
        st = [k.tmp(f"stats{j}", [P, NT, 10]) for j in LANES]
        w0 = k.tmp("w0", [P, FF]); w1 = k.tmp("w1", [P, FC, FF]); w2 = k.tmp("w2", [P, FC, D])
        sc = k.tmp("scales", [P, 2])
        h1 = [k.tmp(f"h1{j}", [P, FC, T]) for j in LANES]
        h2 = [k.tmp(f"h2{j}", [P, FC, T]) for j in LANES]
        yT = [k.tmp(f"yT{j}", [P, T]) for j in LANES]
        tail = Tail(k, S, st, via=2, ready="yT_ps", bias=0.0, yT=yT, y_scale=w["s2"])
        with nc.Block(no_gpsimd_drain=True) as block:

            @block.gpsimd
            def _(pool):
                for c in (2, 3):
                    pool.tensor_copy(w1[:, c, :], k.signs1[:, c, :]).then_inc(S["signs1"], 1)
                tail.gpsimd(pool)

            @block.tensor
            def _(pe):
                k.have(pe, "const")
                pe.wait_ge(S["signs"], 1)
                for f in range(FC):
                    for j in LANES:
                        n = 2 * f + j
                        if f >= 2:
                            pe.wait_ge(S["h1"], n - 3)
                        pe.matmul(k.ps[j][:, f % 2, :], w0[:, f * P:(f + 1) * P], k.XT[j][:, :],
                                  start=True, stop=True).then_inc(S["h1_ps"], 1)
                pe.wait_ge(S["signs"], 2)
                pe.wait_ge(S["signs1"], 2)
                for f in range(FC):
                    for j in LANES:
                        n = 2 * f + j
                        pe.wait_ge(S["h1"], 2 * (FC - 1) + j + 1)
                        if f >= 2:
                            pe.wait_ge(S["h2"], n - 3)
                        for c in range(FC):
                            ins = pe.matmul(k.ps[j][:, f % 2, :], w1[:, c, f * P:(f + 1) * P],
                                            h1[j][:, c, :], start=(c == 0), stop=(c == FC - 1))
                        ins.then_inc(S["h2_ps"], 1)
                for j in LANES:
                    pe.wait_ge(S["h2"], 2 * (FC - 1) + j + 1)
                    for c in range(FC):
                        ins = pe.matmul(k.ps[j][:, 2, :], w2[:, c, :], h2[j][:, c, :],
                                        start=(c == 0), stop=(c == FC - 1))
                    ins.then_inc(S["yT_ps"], 1)
                tail.tensor(pe)

            @block.scalar
            def _(act):
                act.wait_ge(S["scales"], 1)
                for f in range(FC):
                    for j in LANES:
                        act.wait_ge(S["h1_ps"], 2 * f + j + 1)
                        act.activation(h1[j][:, f, :], k.ps[j][:, f % 2, :], ACT.Relu,
                                       scale=sc[:, 0:1]).then_inc(S["h1"], 1)
                for f in range(FC):
                    for j in LANES:
                        act.wait_ge(S["h2_ps"], 2 * f + j + 1)
                        act.activation(h2[j][:, f, :], k.ps[j][:, f % 2, :], ACT.Relu,
                                       scale=sc[:, 1:2]).then_inc(S["h2"], 1)
                tail.scalar(act)

            @block.vector
            def _(dve):
                k.have(dve, "vec")
                c = Chain(dve, S["step"])
                dve.tensor_scalar(sc[:, 0:1], w["s0"], 4.0, None, ALU.mult)
                dve.tensor_scalar(sc[:, 1:2], w["s1"], 2.0, None, ALU.mult).then_inc(S["scales"], 1)
                dve.tensor_copy(w0[:, :], k.signs0[:, :]).then_inc(S["signs"], 1)
                dve.tensor_copy(w1[:, 0:2, :], k.signs1[:, 0:2, :])
                dve.tensor_copy(w2[:, :, :], k.signs2[:, :, :]).then_inc(S["signs"], 1)
                tail.vector(dve, c)
    


SIGN = [[1, 1, 1, 1], [-1, 1, -1, 1], [-1, 1, 1, -1], [-1, -1, 1, 1]]


def quaternion_product(dve, c, q1, q2, prod, out, conjugate, done=None):
    n = {}
    for j in LANES:
        for a in range(4):
            ins = dve.tensor_tensor(prod[j][:, a, :, :], rep(q1[j][:, :, a], 2, 4), q2[j], ALU.mult)
        n[j] = c.mark(ins)

    def sign(a, r):
        return SIGN[a][r] * (-1 if conjugate and r ^ a else 1)

    order = {}
    for r in range(4):
        terms = sorted(range(4), key=lambda a: -sign(a, r))
        assert sign(terms[0], r) > 0
        order[r] = terms
    for step in range(3):
        for j in LANES:
            c.wait(n[j])
            for r in range(4):
                a = order[r][step + 1]
                first = prod[j][:, order[r][0], :, r ^ order[r][0]] if step == 0 else out[j][:, :, r]
                ins = dve.tensor_tensor(out[j][:, :, r], first, prod[j][:, a, :, r ^ a],
                                        ALU.add if sign(a, r) > 0 else ALU.subtract)
            if step == 2 and done is not None:
                ins.then_inc(done, 1)
            else:
                n[j] = c.mark(ins)
    return n


def l1_quaternion(k):
    nc, w = k.nc, k.w
    NQ = NT * D // 4
    S = k.signals("kv_ps norm2 root bound memory n n_ps nT y step" + LN_SIGNALS + TAIL_SIGNALS)
    with k.scratch():
        st = [k.tmp(f"stats{j}", [P, NT, 10]) for j in LANES]
        key = [k.tmp(f"key{j}", [P, NQ, 4]) for j in LANES]
        val = [k.tmp(f"val{j}", [P, NQ, 4]) for j in LANES]
        sq = [k.tmp(f"sq{j}", [P, NQ, 4]) for j in LANES]
        n2 = [k.tmp(f"n2{j}", [P, NQ]) for j in LANES]
        root = [k.tmp(f"root{j}", [P, NQ]) for j in LANES]
        inv = [k.tmp(f"inv{j}", [P, NQ]) for j in LANES]
        prod = [k.tmp(f"prod{j}", [P, 4, NQ, 4]) for j in LANES]
        bound = [k.tmp(f"bound{j}", [P, NQ, 4]) for j in LANES]
        nT = [k.tmp(f"nT{j}", [P, T]) for j in LANES]
        yT = [k.tmp(f"yT{j}", [P, T]) for j in LANES]
        tail = Tail(k, S, st, base=2, via=1, ready="y", bias=w["bo1"], yT=yT, x_factor=2.0)

        def tiles(ap):
            return ap.rearrange("p (t q) c -> p t (q c)", t=NT)

        with nc.Block(no_gpsimd_drain=True) as block:

            @block.tensor
            def _(pe):
                k.have(pe, "L1", "const")
                wkv = k.group["L1"][:, 0:2 * D]
                for j in LANES:
                    for t in range(NT):
                        ins = pe.matmul(k.ps[j][:, t // 2, (t % 2) * 256:(t % 2) * 256 + 256],
                                        k.XT[j][:, t * P:(t + 1) * P], wkv, start=True, stop=True)
                    ins.then_inc(S["kv_ps"], 1)
                for j in LANES:
                    pe.wait_ge(S["bound"], j + 1)
                    b = tiles(bound[j][:, :, :])
                    pe.matmul(k.ps[j][:, 2, :], w["tri"], b.rearrange("p t n -> p (t n)"), start=True, stop=False)
                    for t in range(NT - 1):
                        ins = pe.matmul(k.ps[j][:, 2, (t + 1) * P:], w["ones"], rep(b[:, t, :], 1, NT - 1 - t),
                                        start=False, stop=(t == NT - 2))
                    ins.then_inc(S["memory"], 1)
                for j in LANES:
                    pe.wait_ge(S["n"], j + 1)
                    for t in range(NT):
                        ins = pe.transpose(k.ps[j][:, 0, t * P:(t + 1) * P], tiles(bound[j][:, :, :])[:, t, :],
                                           w["ident"])
                    ins.then_inc(S["n_ps"], 1)
                for j in LANES:
                    pe.wait_ge(S["nT"], j + 1)
                    pe.matmul(k.ps[j][:, 1, :], w["o1"], nT[j][:, :], start=True, stop=True).then_inc(S["y"], 1)
                tail.tensor(pe)

            @block.scalar
            def _(act):
                k.have(act, "vec")
                for j in LANES:
                    act.wait_ge(S["norm2"], j + 1)
                    act.activation(root[j][:, :], n2[j][:, :], ACT.Sqrt).then_inc(S["root"], 1)
                for j in LANES:
                    act.wait_ge(S["n_ps"], j + 1)
                    act.activation(nT[j][:, :], k.ps[j][:, 0, :], ACT.Identity, bias=w["ln_b"],
                                   scale=w["ln_g"]).then_inc(S["nT"], 1)
                tail.scalar(act)

            @block.vector
            def _(dve):
                k.have(dve, "rows", "const")
                c = Chain(dve, S["step"])
                n = {}
                for j in LANES:
                    dve.wait_ge(S["kv_ps"], j + 1)
                    kv = k.ps[j][:, 0:2, :].rearrange("p b (s kv n) -> p (b s) kv n", s=2, kv=2)
                    dve.tensor_tensor(tiles(key[j][:, :, :]), kv[:, :, 0, :], rep(w["bk1"], 1, NT),
                                      ALU.add)
                    n[j] = c.mark(dve.tensor_tensor(tiles(val[j][:, :, :]), kv[:, :, 1, :], rep(w["bv1"], 1, NT),
                                                    ALU.add))
                for j in LANES:
                    c.wait(n[j])
                    n[j] = c.mark(dve.tensor_tensor(sq[j][:, :, :], key[j][:, :, :], key[j][:, :, :], ALU.mult))
                for j in LANES:
                    c.wait(n[j])
                    n[j] = c.mark(dve.tensor_reduce(n2[j][:, :], sq[j][:, :, :], AX.X, ALU.add))
                for j in LANES:
                    c.wait(n[j])
                    dve.tensor_scalar(n2[j][:, :], n2[j][:, :], 1e-24, None, ALU.max).then_inc(S["norm2"], 1)
                for j in LANES:
                    dve.wait_ge(S["root"], j + 1)
                    n[j] = c.mark(dve.reciprocal(inv[j][:, :], root[j][:, :]))
                for a, b in ((inv, inv), (root, n2)):
                    for j in LANES:
                        c.wait(n[j])
                        n[j] = c.mark(dve.tensor_tensor(root[j][:, :], a[j][:, :], b[j][:, :], ALU.mult))
                for j in LANES:
                    c.wait(n[j])
                    n[j] = c.mark(dve.tensor_scalar(root[j][:, :], root[j][:, :], -0.5, 1.5, ALU.mult, ALU.add))
                for j in LANES:
                    c.wait(n[j])
                    n[j] = c.mark(dve.tensor_tensor(n2[j][:, :], root[j][:, :], inv[j][:, :], ALU.mult))
                for j in LANES:
                    c.wait(n[j])
                    n[j] = c.mark(dve.tensor_tensor(key[j][:, :, :], key[j][:, :, :], rep(n2[j][:, :], 2, 4),
                                                    ALU.mult))
                for j in LANES:
                    c.wait(n[j])
                kq = [key[j][:, :, :] for j in LANES]
                quaternion_product(dve, c, [val[j][:, :, :] for j in LANES], kq, prod, bound, False, done=S["bound"])
                for j in LANES:
                    dve.wait_ge(S["memory"], j + 1)
                memory = [k.ps[j][:, 2, :].rearrange("p (q c) -> p q c", c=4) for j in LANES]
                n = quaternion_product(dve, c, memory, kq, prod, bound, True)
                for j in LANES:
                    c.wait(n[j])
                    n[j] = c.mark(dve.tensor_tensor(tiles(sq[j][:, :, :]), tiles(bound[j][:, :, :]),
                                                    rep(w["rpos"], 2, D), ALU.mult))
                for j in LANES:
                    c.wait(n[j])
                vector_layernorm(k, dve, c, S, lambda j, t: tiles(sq[j][:, :, :])[:, t, :],
                                 lambda j, t: tiles(bound[j][:, :, :])[:, t, :], st, "n")
                tail.vector(dve, c)

            @block.gpsimd
            def _(pool):
                pool_layernorm(k, pool, S, st)
                tail.gpsimd(pool)
    

def first_largest(dve, c, p, m, wk, mw, onehot, down8):
    c.link(dve.tensor_reduce(m, p, AX.X, ALU.max))
    c.link(dve.tensor_tensor(wk, p, rep(m, 2, E), ALU.is_equal))
    c.link(dve.tensor_tensor(wk, wk, rep(down8, 1, 2 * NT), ALU.mult))
    c.link(dve.tensor_reduce(mw, wk, AX.X, ALU.max))
    return dve.tensor_tensor(onehot, wk, rep(mw, 2, E), ALU.is_equal)


def l1_mixture(k):
    nc, w = k.nc, k.w
    NB = 2 * NT
    SL = E * CAP
    S = k.signals("logits less exp masks cum disp taken xin h_ps h eo_ps eo gates gd gd2 ct_ps ct y_tile step"
                  + LN_SIGNALS + TAIL_SIGNALS)
    with k.scratch():
        st = [k.tmp(f"stats{j}", [P, NT, 10]) for j in LANES]
        p = k.tmp("p", [P, NB, E]); wk = k.tmp("wk", [P, NB, E])
        small = k.tmp("small", [P, 4, NB])
        mask = k.tmp("mask", [P, 2, NB, E]); mask16 = k.tmp("mask16", [P, 2, NB, E], BF16)
        gate = k.tmp("gate", [P, NB, E])
        total = k.tmp("total", [P, E, 2 * NB]); upto = k.tmp("upto", [P, E, 2 * NB])
        cum = k.tmp("cum", [P, 2, NB, E]); pos = k.tmp("pos", [P, NB, E])
        disp = k.tmp("disp", [P, 2, SL])
        gd = k.tmp("gd", [P, NB, SL])
        xin = k.tmp("xin", [P, SL])
        hid = k.tmp("hid", [P, E, FC * CAP])
        eo = k.tmp("eo", [CAP, E, D])
        ct = k.tmp("ct", [CAP, 2, E * P])
        tail = Tail(k, S, st, y_at=("y_tile", NT, 0))
        wi = w["wi"].rearrange("p (e f) -> p e f", e=E)
        wo = w["wo"].rearrange("p (e c n) -> p e c n", e=E, c=FC)
        with nc.Block(no_gpsimd_drain=True) as block:

            @block.tensor
            def _(pe):
                k.have(pe, "L1", "L1wi", "L1wo", "const")
                for j in LANES:
                    for t in range(NT):
                        ins = pe.matmul(k.ps[j][:, 0, t * E:(t + 1) * E], k.XT[j][:, t * P:(t + 1) * P],
                                        w["router1"], start=True, stop=True)
                    ins.then_inc(S["logits"], 1)
                pe.wait_ge(S["masks"], 1)
                flat = mask16[:, :, :, :].rearrange("p a b e -> p (a b e)")
                pe.matmul(k.ps[0][:, 0, 0:P], k.tri16[:, :], flat, start=True, stop=True)
                pe.matmul(k.ps[0][:, 1, 0:P], k.ones16[:, :], flat, start=True, stop=True).then_inc(S["cum"], 1)
                for i in range(NB):
                    pe.wait_ge(S["disp"], i + 1)
                    for half in range(2):
                        ins = pe.matmul(k.ps[0][:, 2 + half, 0:SL // 2], k.X[i // NT][:, i % NT, :],
                                        disp[:, i % 2, half * SL // 2:(half + 1) * SL // 2],
                                        start=(i == 0), stop=(i == NB - 1))
                    ins.then_inc(S["taken"], 1)
                pe.wait_ge(S["xin"], 1)

                def up(e):
                    if e >= 2:
                        pe.wait_ge(S["h"], e - 1)
                    for c in range(FC):
                        ins = pe.matmul(k.ps[1][:, e % 2, c * CAP:(c + 1) * CAP], wi[:, e, c * P:(c + 1) * P],
                                        xin[:, e * CAP:(e + 1) * CAP], start=True, stop=True)
                    ins.then_inc(S["h_ps"], 1)

                up(0)
                for e in range(E):
                    if e + 1 < E:
                        up(e + 1)
                    pe.wait_ge(S["h"], e + 1)
                    for c in range(FC):
                        ins = pe.matmul(k.ps[1][0:CAP, 2 + e // 4, (e % 4) * D:(e % 4 + 1) * D],
                                        hid[:, e, c * CAP:(c + 1) * CAP], wo[:, e, c, :],
                                        start=(c == 0), stop=(c == FC - 1))
                    if e % 4 == 3:
                        ins.then_inc(S["eo_ps"], 1)

                def turn(i):
                    pe.wait_ge(S[("gd", "gd2")[i // NT]], i % NT + 1)
                    if i >= 2:
                        pe.wait_ge(S["ct"], i - 1)
                    for e in range(E):
                        ins = pe.transpose(k.ps[i % 2][0:CAP, e // 4, (e % 4) * P:(e % 4 + 1) * P],
                                           gd[:, i, e * CAP:(e + 1) * CAP], w["ident"])
                    ins.then_inc(S["ct_ps"], 1)

                turn(0)
                for i in range(NB):
                    if i + 1 < NB:
                        turn(i + 1)
                    if i == 0:
                        pe.wait_ge(S["eo"], 2)
                    pe.wait_ge(S["ct"], i + 1)
                    for e in range(E):
                        ins = pe.matmul(k.ps[i // NT][:, 3, (i % NT) * P:(i % NT + 1) * P],
                                        ct[:, i % 2, e * P:(e + 1) * P], eo[:, e, :],
                                        start=(e == 0), stop=(e == E - 1))
                    ins.then_inc(S["y_tile"], 1)
                tail.tensor(pe)

            @block.scalar
            def _(act):
                act.wait_ge(S["less"], 2)
                act.activation(p[:, :, :], p[:, :, :], ACT.Exp).then_inc(S["exp"], 1)
                act.wait_ge(S["taken"], NB)
                act.activation(xin[:, :].rearrange("p (a n) -> p a n", a=2), k.ps[0][:, 2:4, 0:SL // 2],
                               ACT.Copy).then_inc(S["xin"], 1)
                for e in range(E):
                    act.wait_ge(S["h_ps"], e + 1)
                    act.activation(hid[:, e, :], k.ps[1][:, e % 2, 0:FC * CAP], ACT.Relu).then_inc(S["h"], 1)
                for i in range(NB):
                    act.wait_ge(S["ct_ps"], i + 1)
                    if i >= 2:
                        act.wait_ge(S["y_tile"], i - 1)
                    act.activation(ct[:, i % 2, :].rearrange("p (a n) -> p a n", a=2), k.ps[i % 2][0:CAP, 0:2, :],
                                   ACT.Copy).then_inc(S["ct"], 1)
                tail.scalar(act)

            @block.vector
            def _(dve):
                k.have(dve, "const")
                c = Chain(dve, S["step"])
                for j in LANES:
                    at = slice(NT * j, NT * j + NT)
                    dve.wait_ge(S["logits"], j + 1)
                    lg = k.ps[j][:, 0, 0:NT * E].rearrange("p (t e) -> p t e", e=E)
                    c.link(dve.tensor_reduce(small[:, 0, at], lg, AX.X, ALU.max))
                    dve.tensor_tensor(p[:, at, :], lg, rep(small[:, 0, at], 2, E), ALU.subtract).then_inc(S["less"], 1)
                dve.wait_ge(S["exp"], 1)
                c.link(dve.tensor_reduce(small[:, 0, :], p[:, :, :], AX.X, ALU.add))
                c.link(dve.reciprocal(small[:, 1, :], small[:, 0, :]))
                c.link(dve.tensor_tensor(p[:, :, :], p[:, :, :], rep(small[:, 1, :], 2, E), ALU.mult))
                c.link(first_largest(dve, c, p[:, :, :], small[:, 2, :], wk[:, :, :], small[:, 0, :],
                                     mask[:, 0, :, :], w["down8"]))
                dve.tensor_tensor(gate[:, :, :], mask[:, 0, :, :], rep(small[:, 2, :], 2, E), ALU.mult)
                c.link(dve.scalar_tensor_tensor(out=p[:, :, :], in0=mask[:, 0, :, :], scalar=-2.0, in1=p[:, :, :],
                                                op0=ALU.mult, op1=ALU.add))
                c.link(first_largest(dve, c, p[:, :, :], small[:, 3, :], wk[:, :, :], small[:, 0, :],
                                     mask[:, 1, :, :], w["down8"]))
                dve.tensor_copy(mask16[:, :, :, :], mask[:, :, :, :]).then_inc(S["masks"], 1)
                c.link(dve.tensor_tensor(wk[:, :, :], mask[:, 1, :, :], rep(small[:, 3, :], 2, E), ALU.mult))
                dve.tensor_tensor(gate[:, :, :], gate[:, :, :], wk[:, :, :], ALU.add)
                dve.wait_ge(S["cum"], 1)
                c.link(dve.tensor_copy(total[:, :, :], k.ps[0][:, 1, 0:P].rearrange("p (b e) -> p e b", e=E)))
                c.link(dve.tensor_tensor_scan(upto[:, :, :].rearrange("p e b -> p (e b)"), w["restart"],
                                              total[:, :, :].rearrange("p e b -> p (e b)"), 0.0, ALU.mult, ALU.add))
                c.link(dve.tensor_tensor(upto[:, :, :], upto[:, :, :], total[:, :, :], ALU.subtract))
                cumf = cum[:, :, :, :].rearrange("p a b e -> p (a b) e")
                c.link(dve.tensor_tensor(cumf, k.ps[0][:, 0, 0:P].rearrange("p (b e) -> p b e", e=E),
                                         upto[:, :, :].rearrange("p e b -> p b e"), ALU.add))
                c.link(dve.tensor_tensor(cumf, cumf, mask[:, :, :, :].rearrange("p a b e -> p (a b) e"), ALU.mult))
                ins = dve.scalar_tensor_tensor(out=pos[:, :, :], in0=cum[:, 0, :, :], scalar=-1.0,
                                               in1=cum[:, 1, :, :], op0=ALU.add, op1=ALU.add)
                ins.then_inc(S["gates"], 1)
                dve.wait_ge(S["gates"], 1)
                for i in range(NB):
                    if i >= 2:
                        dve.wait_ge(S["taken"], i - 1)
                    dve.tensor_tensor(disp[:, i % 2, :].rearrange("p (e s) -> p e s", s=CAP), rep(w["slot"], 1, E),
                                      rep(pos[:, i, :], 2, CAP), ALU.is_equal).then_inc(S["disp"], 1)
                for i in range(NT, NB):
                    for e in range(E):
                        ins = dve.tensor_scalar(gd[:, i, e * CAP:(e + 1) * CAP], w["slot"], pos[:, i, e:e + 1],
                                                gate[:, i, e:e + 1], ALU.is_equal, ALU.mult)
                    ins.then_inc(S["gd2"], 1)
                for half in range(2):
                    dve.wait_ge(S["eo_ps"], half + 1)
                    dve.tensor_copy(eo[:, 4 * half:4 * half + 4, :].rearrange("p e n -> p (e n)"),
                                    k.ps[1][0:CAP, 2 + half, :]).then_inc(S["eo"], 1)
                tail.vector(dve, c)

            @block.gpsimd
            def _(pool):
                k.have(pool, "const")
                pool.wait_ge(S["gates"], 1)
                for i in range(NT):
                    for e in range(E):
                        ins = pool.tensor_scalar(gd[:, i, e * CAP:(e + 1) * CAP], w["slot"], pos[:, i, e:e + 1],
                                                 gate[:, i, e:e + 1], ALU.is_equal, ALU.mult)
                    ins.then_inc(S["gd"], 1)
                tail.gpsimd(pool)
    


def l2_linear_attention(k):
    nc, w = k.nc, k.w
    VW = DH + 1
    S = k.signals("n1 n1_ps n1T qkv_ps z expz qk vones kv_in kv_prod attn a_ps aT o_ps oT o_tok n2 n2_ps n2T fc_ps h "
                  "y step" + LN_SIGNALS + TAIL_SIGNALS)
    with k.scratch():
        st = [k.tmp(f"stats{j}", [P, NT, 10]) for j in LANES]
        xn = [k.tmp(f"xn{j}", [P, NT, D]) for j in LANES]
        xnT = [k.tmp(f"xnT{j}", [P, T]) for j in LANES]
        z = [k.tmp(f"z{j}", [P, NT, 2 * D]) for j in LANES]
        ez = [k.tmp(f"ez{j}", [P, NT, 2 * D]) for j in LANES]
        V = [k.tmp(f"V{j}", [P, NT, H, VW]) for j in LANES]
        outer = [k.tmp(f"outer{j}", [P, DH, VW, H]) for j in LANES]
        inner = k.tmp("inner", [P, H, VW, DH])
        kv = [k.tmp(f"kv{j}", [P, DH, VW]) for j in LANES]
        o = [k.tmp(f"o{j}", [P, H, VW]) for j in LANES]
        rs = [k.tmp(f"rs{j}", [P, H]) for j in LANES]
        attn = [k.tmp(f"attn{j}", [P, NT, D]) for j in LANES]
        hT = [k.tmp(f"hT{j}", [P, FC, T]) for j in LANES]
        tail = Tail(k, S, st, base=4, via=2, ready="y", bias=w["proj_b"], yT=xnT)
        with nc.Block(no_gpsimd_drain=True) as block:

            @block.tensor
            def _(pe):
                k.have(pe, "L2", "const")
                for j in LANES:
                    pe.wait_ge(S["n1"], j + 1)
                    for t in range(NT):
                        ins = pe.transpose(k.ps[j][:, 0, t * P:(t + 1) * P], xn[j][:, t, :], w["ident"])
                    ins.then_inc(S["n1_ps"], 1)
                for j in LANES:
                    pe.wait_ge(S["n1T"], j + 1)
                    for t in range(NT):
                        ins = pe.matmul(k.ps[j][:, t, 0:3 * D], xnT[j][:, t * P:(t + 1) * P], w["qkv2"],
                                        start=True, stop=True)
                    ins.then_inc(S["qkv_ps"], 1)
                for j in LANES:
                    pe.wait_ge(S["attn"], (NT - 1) * 2 + j + 1)
                    for t in range(NT):
                        ins = pe.transpose(k.ps[j][:, 0, t * P:(t + 1) * P], attn[j][:, t, :], w["ident"])
                    ins.then_inc(S["a_ps"], 1)
                for j in LANES:
                    pe.wait_ge(S["aT"], j + 1)
                    pe.matmul(k.ps[j][:, 1, :], w["o2"], xnT[j][:, :], start=True, stop=True).then_inc(S["o_ps"], 1)
                for j in LANES:
                    pe.wait_ge(S["oT"], j + 1)
                    for t in range(NT):
                        ins = pe.transpose(k.ps[j][:, 2, t * P:(t + 1) * P], hT[j][:, 0, t * P:(t + 1) * P], w["ident"])
                    ins.then_inc(S["o_tok"], 1)
                for j in LANES:
                    pe.wait_ge(S["n2"], j + 1)
                    for t in range(NT):
                        ins = pe.transpose(k.ps[j][:, 0, t * P:(t + 1) * P], xn[j][:, t, :], w["ident"])
                    ins.then_inc(S["n2_ps"], 1)
                for f in range(FC):
                    for j in LANES:
                        pe.wait_ge(S["n2T"], j + 1)
                        if f >= 2:
                            pe.wait_ge(S["h"], 2 * (f - 2) + j + 1)
                        pe.matmul(k.ps[j][:, f % 2, :], w["fc"][:, f * P:(f + 1) * P], xnT[j][:, :],
                                  start=True, stop=True).then_inc(S["fc_ps"], 1)
                for j in LANES:
                    pe.wait_ge(S["h"], 2 * (FC - 1) + j + 1)
                    for f in range(FC):
                        ins = pe.matmul(k.ps[j][:, 2, :], w["proj"][:, f * P:(f + 1) * P], hT[j][:, f, :],
                                        start=(f == 0), stop=(f == FC - 1))
                    ins.then_inc(S["y"], 1)
                tail.tensor(pe)

            @block.scalar
            def _(act):
                k.have(act, "vec")
                for j in LANES:
                    act.wait_ge(S["n1_ps"], j + 1)
                    act.activation(xnT[j][:, :], k.ps[j][:, 0, :], ACT.Identity, bias=w["ln1_b"],
                                   scale=w["ln1_w"]).then_inc(S["n1T"], 1)
                for j in LANES:
                    act.wait_ge(S["z"], j + 1)
                    act.activation(ez[j][:, :, :], ez[j][:, :, :], ACT.Exp).then_inc(S["expz"], 1)
                for j in LANES:
                    act.wait_ge(S["a_ps"], j + 1)
                    act.activation(xnT[j][:, :], k.ps[j][:, 0, :], ACT.Copy).then_inc(S["aT"], 1)
                for j in LANES:
                    act.wait_ge(S["o_ps"], j + 1)
                    act.activation(hT[j][:, 0, :], k.ps[j][:, 1, :], ACT.Identity, bias=w["o_b"],
                                   scale=1.0).then_inc(S["oT"], 1)
                for j in LANES:
                    act.wait_ge(S["n2_ps"], j + 1)
                    act.activation(xnT[j][:, :], k.ps[j][:, 0, :], ACT.Identity, bias=w["ln2_b"],
                                   scale=w["ln2_w"]).then_inc(S["n2T"], 1)
                for f in range(FC):
                    for j in LANES:
                        act.wait_ge(S["fc_ps"], 2 * f + j + 1)
                        act.activation(hT[j][:, f, :], k.ps[j][:, f % 2, :], ACT.Gelu,
                                       bias=w["fc_b"][:, f:f + 1]).then_inc(S["h"], 1)
                tail.scalar(act)

            @block.vector
            def _(dve):
                k.have(dve, "rows", "const")
                c = Chain(dve, S["step"])
                vector_layernorm(k, dve, c, S, lambda j, t: k.X[j][:, t, :], lambda j, t: xn[j][:, t, :], st, "n1")
                n = {}
                for j in LANES:
                    dve.wait_ge(S["qkv_ps"], j + 1)
                    n[j] = c.mark(dve.tensor_tensor(z[j][:, :, :], k.ps[j][:, :, 0:2 * D],
                                                    rep(w["bqkv2"][:, 0:2 * D], 1, NT), ALU.add))
                    if j == 0:
                        dve.wait_ge(S["vones"], 2)
                    for t in range(NT):
                        dve.tensor_tensor(V[j][:, t, :, 0:DH],
                                          k.ps[j][:, t, 2 * D:3 * D].rearrange("p (h d) -> p h d", d=DH),
                                          w["bqkv2"][:, 2 * D:3 * D].rearrange("p (h d) -> p h d", d=DH), ALU.add)
                    c.wait(n[j])
                    dve.tensor_scalar(ez[j][:, :, :], z[j][:, :, :], 0.0, None, ALU.min).then_inc(S["z"], 1)
                for j in LANES:
                    dve.wait_ge(S["expz"], j + 1)
                    dve.scalar_tensor_tensor(out=z[j][:, :, :], in0=z[j][:, :, :], scalar=0.0,
                                             in1=ez[j][:, :, :], op0=ALU.max, op1=ALU.add).then_inc(S["qk"], 1)
                for i in range(2 * NT):
                    t, j = i // 2, i % 2
                    dve.wait_ge(S["kv_prod"], i + 1)
                    ins = dve.tensor_reduce(kv[j][:, :, :].rearrange("p d e -> p (d e)"),
                                            outer[j][:, :, :, :].rearrange("p d e h -> p (d e) h"), AX.X, ALU.add)
                    ins.then_inc(S["kv_in"], 1)
                    dve.wait_ge(S["kv_in"], i + 1)
                    q = z[j][:, t, 0:D].rearrange("p (h d) -> p h d", d=DH)
                    c.link(dve.tensor_tensor(inner[:, :, :, :], rep(q, 2, VW),
                                             rep(kv[j][:, :, :].rearrange("p d e -> p e d"), 1, H), ALU.mult))
                    c.link(dve.tensor_reduce(o[j][:, :, :].rearrange("p h e -> p (h e)"),
                                             inner[:, :, :, :].rearrange("p h e d -> p (h e) d"), AX.X, ALU.add))
                    c.link(dve.reciprocal(rs[j][:, :], o[j][:, :, DH]))
                    dve.tensor_tensor(attn[j][:, t, :].rearrange("p (h d) -> p h d", d=DH), o[j][:, :, 0:DH],
                                      rep(rs[j][:, :], 2, DH), ALU.mult).then_inc(S["attn"], 1)
                n = {}
                for j in LANES:
                    dve.wait_ge(S["o_tok"], j + 1)
                    n[j] = c.mark(dve.tensor_tensor(attn[j][:, :, :].rearrange("p t n -> p (t n)"),
                                                    k.X[j][:, :, :].rearrange("p t n -> p (t n)"),
                                                    k.ps[j][:, 2, :], ALU.add))
                for j in LANES:
                    c.wait(n[j])
                vector_layernorm(k, dve, c, S, lambda j, t: attn[j][:, t, :], lambda j, t: xn[j][:, t, :], st, "n2",
                                 base=2)
                for j in LANES:
                    n[j] = c.mark(dve.tensor_tensor(k.X[j][:, :, :], k.X[j][:, :, :], attn[j][:, :, :], ALU.add))
                for j in LANES:
                    c.wait(n[j])
                tail.vector(dve, c)

            @block.gpsimd
            def _(pool):
                for j in LANES:
                    pool.memset(V[j][:, :, :, DH:VW], 1.0).then_inc(S["vones"], 1)
                pool_layernorm(k, pool, S, st)
                for i in range(2 * NT):
                    t, j = i // 2, i % 2
                    pool.wait_ge(S["qk"], j + 1)
                    if i >= 2:
                        pool.wait_ge(S["kv_in"], i - 1)
                    key = z[j][:, t, D:2 * D].rearrange("p (h d) -> p d h", d=DH)
                    val = V[j][:, t, :, :].rearrange("p h e -> p e h")
                    pool.tensor_tensor(outer[j][:, :, :, :], rep(key, 2, VW), rep(val, 1, DH),
                                       ALU.mult).then_inc(S["kv_prod"], 1)
                pool_layernorm(k, pool, S, st, base=2)
                tail.gpsimd(pool)
    

def l2_perceiver(k):
    nc, w = k.nc, k.w
    KEYS = T + CTX
    UNITS = 2 * NT * 2
    S = k.signals("zeros cn n cn_ps cnT n_ps nT ckv_ps ckv qkv_ps qkv v rms inv inv_c c_rms qk ck q_ps q_sb scl mask scores max "
                  "exp pT_ps pT pTc pv attn a_ps aT y step" + LN_SIGNALS + TAIL_SIGNALS)
    with k.scratch():
        st = [k.tmp(f"stats{j}", [P, NT, 10]) for j in LANES]
        cn = [k.tmp(f"cn{j}", [CTX, CD]) for j in LANES]
        cnT = [k.tmp(f"cnT{j}", [CD, CTX]) for j in LANES]
        xn = [k.tmp(f"xn{j}", [P, NT, D]) for j in LANES]
        xnT = [k.tmp(f"xnT{j}", [P, T]) for j in LANES]
        ckv = [k.tmp(f"ckv{j}", [CTX, 2 * D]) for j in LANES]
        qk = [k.tmp(f"qk{j}", [P, NT, 2 * D]) for j in LANES]
        V = [k.tmp(f"V{j}", [P, NT, D]) for j in LANES]
        sq = [k.tmp(f"sq{j}", [P, NT, 2 * D]) for j in LANES]
        csq = [k.tmp(f"csq{j}", [CTX, D]) for j in LANES]
        ss = [k.tmp(f"ss{j}", [P, 4 * NT]) for j in LANES]
        css = [k.tmp(f"css{j}", [CTX, 2]) for j in LANES]
        qT = [k.tmp(f"qT{j}", [P, T]) for j in LANES]
        kT = [k.tmp(f"kT{j}", [P, 2, KEYS]) for j in LANES]
        mrow = [k.tmp(f"mrow{j}", [1, CTX], BF16) for j in LANES]
        qg = k.tmp("qg", [P, 1])
        prob = [k.tmp(f"prob{j}", [P, 2, KEYS]) for j in LANES]
        nmax = [k.tmp(f"nmax{j}", [P, 2]) for j in LANES]
        rs = [k.tmp(f"rs{j}", [P, 2]) for j in LANES]
        pT = [k.tmp(f"pT{j}", [P, T]) for j in LANES]
        pTc = [k.tmp(f"pTc{j}", [CTX, P]) for j in LANES]
        tail = Tail(k, S, st, base=4, via=1, ready="y", bias=w["xbo2"], yT=xnT)

        TURN, WEIGH, DIVIDE = 2, 3, 4

        def unit(n):
            j, u = n % 2, n // 2
            return j, u, u // 2, u % 2

        with nc.Block(no_gpsimd_drain=True) as block:

            @block.tensor
            def _(pe):
                k.have(pe, "L2", "ctxw", "const")
                for j in LANES:
                    pe.wait_ge(S["cn"], j + 1)
                    pe.transpose(k.ps[j][0:CD, 0, 0:CTX], cn[j][:, :], w["ident"][0:CTX, 0:CTX]).then_inc(S["cn_ps"], 1)
                for j in LANES:
                    pe.wait_ge(S["n"], j + 1)
                    for t in range(NT):
                        ins = pe.transpose(k.ps[j][:, 1, t * P:(t + 1) * P], xn[j][:, t, :], w["ident"])
                    ins.then_inc(S["n_ps"], 1)
                for j in LANES:
                    pe.wait_ge(S["cnT"], j + 1)
                    pe.matmul(k.ps[j][0:CTX, 2, 0:2 * D], cnT[j][:, :], w["xkv2"], start=True,
                              stop=True).then_inc(S["ckv_ps"], 1)
                for j in LANES:
                    pe.wait_ge(S["nT"], j + 1)
                    pe.wait_ge(S["ckv"], j + 1)
                    for t in range(NT):
                        ins = pe.matmul(k.ps[j][:, t, 0:3 * D], xnT[j][:, t * P:(t + 1) * P], w["xqkv2"],
                                        start=True, stop=True)
                    ins.then_inc(S["qkv_ps"], 1)
                for j in LANES:
                    pe.wait_ge(S["qk"], j + 1)
                    pe.wait_ge(S["ck"], j + 1)
                    pe.wait_ge(S["v"], j + 1)
                    for a in range(2):
                        for t in range(NT):
                            pe.transpose(k.ps[j][:, a, t * P:(t + 1) * P], qk[j][:, t, a * D:(a + 1) * D], w["ident"])
                    pe.transpose(k.ps[j][:, 2, 0:CTX], ckv[j][:, 0:D], w["ident"][0:CTX, 0:CTX]).then_inc(S["q_ps"], 1)
                pe.wait_ge(S["q_sb"], 2)
                pe.wait_ge(S["mask"], 2)

                def scores(n):
                    j, u, t, h = unit(n)
                    if n >= 2:
                        pe.wait_ge(S["exp"], n - 1)
                    q = qT[j][:, t * P:(t + 1) * P]
                    pe.matmul(k.ps[j][:, 0, :], q, kT[j][:, h, 0:T], start=True, stop=True)
                    pe.matmul(k.ps[j][:, 1, 0:CTX], q, kT[j][:, h, T:KEYS], start=True, stop=False)
                    pe.matmul(k.ps[j][:, 1, 0:CTX], k.one16[:, :], mrow[j][:, :], start=False,
                              stop=True).then_inc(S["scores"], 1)

                def transposes(n):
                    j, u, t, h = unit(n)
                    pe.wait_ge(S["exp"], n + 1)
                    if n >= 2:
                        pe.wait_ge(S["pT"], n - 1)
                        pe.wait_ge(S["attn"], n - 1)
                    for b in range(NT):
                        pe.transpose(k.ps[j][:, 2, b * P:(b + 1) * P], prob[j][:, u % 2, b * P:(b + 1) * P], w["ident"])
                    pe.transpose(k.ps[j][0:CTX, 3, 0:P], prob[j][:, u % 2, T:KEYS], w["ident"]).then_inc(S["pT_ps"], 1)

                def values(n):
                    j, u, t, h = unit(n)
                    pe.wait_ge(S["pT"], n + 1)
                    pe.wait_ge(S["pTc"], n + 1)
                    out = k.ps[j][:, 3, 2 * P:2 * P + DW]
                    for b in range(NT):
                        pe.matmul(out, pT[j][:, b * P:(b + 1) * P], V[j][:, b, h * DW:(h + 1) * DW],
                                  start=(b == 0), stop=False)
                    pe.matmul(out, pTc[j][:, :], ckv[j][:, D + h * DW:D + (h + 1) * DW], start=False,
                              stop=True).then_inc(S["pv"], 1)

                for n in range(UNITS + WEIGH):
                    if n < UNITS:
                        scores(n)
                    if 0 <= n - TURN < UNITS:
                        transposes(n - TURN)
                    if n >= WEIGH:
                        values(n - WEIGH)
                for j in LANES:
                    pe.wait_ge(S["attn"], UNITS - 1 + j)
                    for t in range(NT):
                        ins = pe.transpose(k.ps[j][:, 2, t * P:(t + 1) * P], xn[j][:, t, :], w["ident"])
                    ins.then_inc(S["a_ps"], 1)
                for j in LANES:
                    pe.wait_ge(S["aT"], j + 1)
                    pe.matmul(k.ps[j][:, 1, :], w["xo2"], qT[j][:, :], start=True, stop=True).then_inc(S["y"], 1)
                tail.tensor(pe)

            @block.scalar
            def _(act):
                k.have(act, "vec")
                for j in LANES:
                    act.wait_ge(S["cn_ps"], j + 1)
                    act.activation(cnT[j][:, :], k.ps[j][0:CD, 0, 0:CTX], ACT.Identity, bias=w["ln_x_b"][0:CD, :],
                                   scale=w["ln_x_g"][0:CD, :]).then_inc(S["cnT"], 1)
                for j in LANES:
                    act.wait_ge(S["n_ps"], j + 1)
                    act.activation(xnT[j][:, :], k.ps[j][:, 1, :], ACT.Identity, bias=w["ln_l_b"],
                                   scale=w["ln_l_g"]).then_inc(S["nT"], 1)
                for j in LANES:
                    act.wait_ge(S["qkv_ps"], j + 1)
                    act.activation(qk[j][:, :, :], k.ps[j][:, :, 0:2 * D], ACT.Copy).then_inc(S["qkv"], 1)
                act.wait_ge(S["scl"], 1)
                for j in LANES:
                    act.wait_ge(S["q_ps"], j + 1)
                    act.activation(qT[j][:, :], k.ps[j][:, 0, :], ACT.Copy, scale=qg[:, :])
                    act.wait_ge(S["zeros"], j + 1)
                    for h in range(2):
                        r = slice(DW * h, DW * h + DW)
                        act.activation(kT[j][r, h, 0:T], k.ps[j][r, 1, :], ACT.Copy, scale=w["kn_g"][r])
                        ins = act.activation(kT[j][r, h, T:KEYS], k.ps[j][r, 2, 0:CTX], ACT.Copy, scale=w["kn_g"][r])
                    ins.then_inc(S["q_sb"], 1)
                for n in range(UNITS + TURN):
                    m = n - TURN
                    if m >= 0:
                        j, u, t, h = unit(m)
                        act.wait_ge(S["pT_ps"], m + 1)
                        if m >= 2:
                            act.wait_ge(S["pv"], m - 1)
                        act.activation(pT[j][:, :], k.ps[j][:, 2, :], ACT.Copy).then_inc(S["pT"], 1)
                    if n < UNITS:
                        j, u, t, h = unit(n)
                        act.wait_ge(S["max"], n + 1)
                        if n >= 4:
                            act.wait_ge(S["pT_ps"], n - 3)
                            act.wait_ge(S["attn"], n - 3)
                        act.activation(prob[j][:, u % 2, :], k.ps[j][:, 0:2, :].rearrange("p b n -> p (b n)")[:, 0:KEYS],
                                       ACT.Exp, bias=nmax[j][:, u % 2:u % 2 + 1],
                                       accum_out=rs[j][:, u % 2:u % 2 + 1]).then_inc(S["exp"], 1)
                for j in LANES:
                    act.wait_ge(S["a_ps"], j + 1)
                    act.activation(qT[j][:, :], k.ps[j][:, 2, :], ACT.Copy).then_inc(S["aT"], 1)
                tail.scalar(act)

            @block.vector
            def _(dve):
                k.have(dve, "vec")
                c = Chain(dve, S["step"])
                vector_layernorm(k, dve, c, S, lambda j, t: k.ctx[j][:, :], lambda j, t: cn[j][:, :], st, "cn",
                                 n_rows=CTX, tiles=1)
                vector_layernorm(k, dve, c, S, lambda j, t: k.X[j][:, t, :], lambda j, t: xn[j][:, t, :], st, "n",
                                 base=2)
                dve.tensor_scalar(qg[:, :], w["qn_g"], float(DW) ** -0.5, None, ALU.mult).then_inc(S["scl"], 1)
                for j in LANES:
                    dve.tensor_scalar(mrow[j][:, :], k.maskrow[0][j][:, :], FAR, -FAR, ALU.mult,
                                      ALU.add).then_inc(S["mask"], 1)
                n = {}
                for j in LANES:
                    dve.wait_ge(S["ckv_ps"], j + 1)
                    dve.tensor_copy(ckv[j][:, :], k.ps[j][0:CTX, 2, 0:2 * D]).then_inc(S["ckv"], 1)
                    dve.wait_ge(S["ckv"], j + 1)
                    c.link(dve.tensor_tensor(csq[j][:, :], ckv[j][:, 0:D], ckv[j][:, 0:D], ALU.mult))
                    c.link(dve.tensor_reduce(css[j][:, :], csq[j][:, :].rearrange("p (h d) -> p h d", d=DW), AX.X, ALU.add))
                    dve.tensor_scalar(css[j][:, :], css[j][:, :], 1.0 / DW, 1e-16, ALU.mult,
                                      ALU.max).then_inc(S["c_rms"], 1)
                for j in LANES:
                    dve.wait_ge(S["inv_c"], j + 1)
                    kc = ckv[j][:, 0:D].rearrange("p (h d) -> p h d", d=DW)
                    dve.tensor_tensor(kc, kc, rep(css[j][:, :], 2, DW), ALU.mult).then_inc(S["ck"], 1)
                for j in LANES:
                    dve.wait_ge(S["qkv"], j + 1)
                    n[j] = c.mark(dve.tensor_tensor(sq[j][:, :, :], qk[j][:, :, :], qk[j][:, :, :], ALU.mult))
                    dve.tensor_copy(V[j][:, :, :], k.ps[j][:, :, 2 * D:3 * D]).then_inc(S["v"], 1)
                for j in LANES:
                    c.wait(n[j])
                    n[j] = c.mark(dve.tensor_reduce(ss[j][:, :], sq[j][:, :, :].rearrange("p t (h d) -> p (t h) d", d=DW),
                                                    AX.X, ALU.add))
                for j in LANES:
                    c.wait(n[j])
                    dve.tensor_scalar(ss[j][:, :], ss[j][:, :], 1.0 / DW, 1e-16, ALU.mult,
                                      ALU.max).then_inc(S["rms"], 1)
                for j in LANES:
                    dve.wait_ge(S["inv"], j + 1)
                    both = qk[j][:, :, :].rearrange("p t (h d) -> p (t h) d", d=DW)
                    dve.tensor_tensor(both, both, rep(ss[j][:, :], 2, DW), ALU.mult).then_inc(S["qk"], 1)
                for n in range(UNITS + DIVIDE):
                    m = n - DIVIDE
                    if m >= 0:
                        j, u, t, h = unit(m)
                        dve.wait_ge(S["pv"], m + 1)
                        c.link(dve.reciprocal(rs[j][:, u % 2:u % 2 + 1], rs[j][:, u % 2:u % 2 + 1]))
                        dve.tensor_scalar(xn[j][:, t, h * DW:(h + 1) * DW], k.ps[j][:, 3, 2 * P:2 * P + DW],
                                          rs[j][:, u % 2:u % 2 + 1], None, ALU.mult).then_inc(S["attn"], 1)
                    if n < UNITS:
                        j, u, t, h = unit(n)
                        dve.wait_ge(S["scores"], n + 1)
                        dve.tensor_reduce(nmax[j][:, u % 2:u % 2 + 1],
                                          k.ps[j][:, 0:2, :].rearrange("p b n -> p (b n)")[:, 0:KEYS], AX.X, ALU.max,
                                          negate=True).then_inc(S["max"], 1)
                    m = n - TURN
                    if 0 <= m < UNITS:
                        j, u, t, h = unit(m)
                        dve.wait_ge(S["pT_ps"], m + 1)
                        if m >= 2:
                            dve.wait_ge(S["pv"], m - 1)
                        dve.tensor_copy(pTc[j][:, :], k.ps[j][0:CTX, 3, 0:P]).then_inc(S["pTc"], 1)
                tail.vector(dve, c)

            @block.gpsimd
            def _(pool):
                for j in LANES:
                    pool.memset(kT[j][:, :, :], 0.0).then_inc(S["zeros"], 1)
                pool_layernorm(k, pool, S, st, n_rows=CTX, tiles=1)
                pool_layernorm(k, pool, S, st, base=2)
                for j in LANES:
                    pool.wait_ge(S["c_rms"], j + 1)
                    pool.tensor_tensor(css[j][:, :], css[j][:, :], k.half[0:CTX, 0:2], ALU.pow).then_inc(S["inv_c"], 1)
                for j in LANES:
                    pool.wait_ge(S["rms"], j + 1)
                    pool.tensor_tensor(ss[j][:, :], ss[j][:, :], k.half[:, 0:4 * NT], ALU.pow).then_inc(S["inv"], 1)
                tail.gpsimd(pool)
    

def l2_switch(k):
    nc, w = k.nc, k.w
    UNITS = 2 * E
    S = k.signals("logits less exp onehot o_ps oT sel b2 picked xm h_ps h_act h_dve used step"
                  + LN_SIGNALS + TAIL_SIGNALS)
    with k.scratch():
        st = [k.tmp(f"stats{j}", [P, NT, 10]) for j in LANES]
        NB = 2 * NT
        p = k.tmp("p", [P, NB, E]); wk = k.tmp("wk", [P, NB, E]); onehot = k.tmp("onehot", [P, NB, E])
        small = k.tmp("small", [P, 2, NB])
        oT = [k.tmp(f"oT{j}", [E, T], BF16) for j in LANES]
        sel = k.tmp("sel", [E, E, P], BF16)
        b2 = k.tmp("b2", [P, 1])
        xm = [k.tmp(f"xm{j}", [P, T]) for j in LANES]
        hT = [k.tmp(f"hT{j}", [P, FC, T]) for j in LANES]
        yT = [k.tmp(f"yT{j}", [P, T]) for j in LANES]
        tail = Tail(k, S, st, via=3, ready="used", ready_from=UNITS - 2, bias=b2[:, :], yT=yT, bank=0)
        W1 = w["W1"].rearrange("p (e f) -> p e f", e=E)
        W2 = w["W2"].rearrange("p (e c n) -> p e c n", e=E, c=FC)
        with nc.Block(no_gpsimd_drain=True) as block:

            @block.tensor
            def _(pe):
                k.have(pe, "L2", "L2w1", "L2w2", "const")
                for j in LANES:
                    for t in range(NT):
                        ins = pe.matmul(k.ps[j][:, 0, t * E:(t + 1) * E], k.XT[j][:, t * P:(t + 1) * P],
                                        w["router2"], start=True, stop=True)
                    ins.then_inc(S["logits"], 1)
                pe.wait_ge(S["onehot"], 1)
                for j in LANES:
                    for t in range(NT):
                        ins = pe.transpose(k.ps[j][0:E, 1, t * P:(t + 1) * P], onehot[:, NT * j + t, :], w["ident"])
                    ins.then_inc(S["o_ps"], 1)
                pe.wait_ge(S["oT"], 2)
                pe.wait_ge(S["sel"], 1)

                def pick(n):
                    if n >= 2:
                        pe.wait_ge(S["xm"], n - 1)
                    pe.matmul(k.ps[n % 2][:, 0, :], sel[:, n // 2, :], oT[n % 2][:, :], start=True,
                              stop=True).then_inc(S["picked"], 1)

                def up(n):
                    e, j = n // 2, n % 2
                    pe.wait_ge(S["xm"], n + 1)
                    for f in range(FC):
                        out_before = 2 * n - 2 if f < 2 else 2 * n + 1
                        if out_before > 0:
                            pe.wait_ge(S["h_act" if f % 2 == 0 else "h_dve"], out_before)
                        pe.matmul(k.ps[j][:, 1 + f % 2, :], W1[:, e, f * P:(f + 1) * P], xm[j][:, :],
                                  start=True, stop=True).then_inc(S["h_ps"], 1)

                def down(n):
                    e, j = n // 2, n % 2
                    pe.wait_ge(S["h_act"], 2 * n + 2)
                    pe.wait_ge(S["h_dve"], 2 * n + 2)
                    for f in range(FC):
                        ins = pe.matmul(k.ps[j][:, 3, :], W2[:, e, f, :], hT[j][:, f, :],
                                        start=(e == 0 and f == 0), stop=(e == E - 1 and f == FC - 1))
                    ins.then_inc(S["used"], 1)

                pick(0)
                pick(1)
                for n in range(UNITS + 1):
                    if n < UNITS:
                        up(n)
                    if n + 2 < UNITS:
                        pick(n + 2)
                    if n >= 1:
                        down(n - 1)
                tail.tensor(pe)

            @block.scalar
            def _(act):
                k.have(act, "vec")
                act.wait_ge(S["less"], 2)
                act.activation(p[:, :, :], p[:, :, :], ACT.Exp).then_inc(S["exp"], 1)
                for j in LANES:
                    act.wait_ge(S["o_ps"], j + 1)
                    act.activation(oT[j][:, :], k.ps[j][0:E, 1, :], ACT.Copy).then_inc(S["oT"], 1)
                for n in range(UNITS):
                    e, j = n // 2, n % 2
                    for f in range(0, FC, 2):
                        act.wait_ge(S["h_ps"], FC * n + f + 1)
                        if n >= 2:
                            act.wait_ge(S["used"], n - 1)
                        act.activation(hT[j][:, f, :], k.ps[j][:, 1, :], ACT.Relu,
                                       bias=w["b1"][:, e * FC + f:e * FC + f + 1]).then_inc(S["h_act"], 1)
                act.wait_ge(S["b2"], 1)
                tail.scalar(act)

            @block.vector
            def _(dve):
                k.have(dve, "rows", "vec", "const")
                c = Chain(dve, S["step"])
                dve.tensor_copy(sel[:, :, :], rep(w["ident"][0:E, 0:E], 2, P)).then_inc(S["sel"], 1)
                dve.tensor_reduce(b2[:, :], w["b2"], AX.X, ALU.add).then_inc(S["b2"], 1)
                for j in LANES:
                    at = slice(NT * j, NT * j + NT)
                    dve.wait_ge(S["logits"], j + 1)
                    lg = k.ps[j][:, 0, 0:NT * E].rearrange("p (t e) -> p t e", e=E)
                    c.link(dve.tensor_tensor(p[:, at, :], lg, rep(w["br"], 1, NT), ALU.add))
                    c.link(dve.tensor_reduce(small[:, 0, at], p[:, at, :], AX.X, ALU.max))
                    dve.tensor_tensor(p[:, at, :], p[:, at, :], rep(small[:, 0, at], 2, E),
                                      ALU.subtract).then_inc(S["less"], 1)
                dve.wait_ge(S["exp"], 1)
                c.link(dve.tensor_reduce(small[:, 0, :], p[:, :, :], AX.X, ALU.add))
                c.link(dve.reciprocal(small[:, 1, :], small[:, 0, :]))
                c.link(dve.tensor_tensor(p[:, :, :], p[:, :, :], rep(small[:, 1, :], 2, E), ALU.mult))
                first_largest(dve, c, p[:, :, :], small[:, 0, :], wk[:, :, :], small[:, 1, :], onehot[:, :, :],
                              w["down8"]).then_inc(S["onehot"], 1)

                def masked(n):
                    j = n % 2
                    dve.wait_ge(S["picked"], n + 1)
                    if n >= 2:
                        dve.wait_ge(S["h_ps"], FC * (n - 1))
                    dve.tensor_tensor(xm[j][:, :], k.XT[j][:, :], k.ps[j][:, 0, :], ALU.mult).then_inc(S["xm"], 1)

                masked(0)
                masked(1)
                for n in range(UNITS):
                    e, j = n // 2, n % 2
                    for f in range(1, FC, 2):
                        dve.wait_ge(S["h_ps"], FC * n + f + 1)
                        if n >= 2:
                            dve.wait_ge(S["used"], n - 1)
                        dve.tensor_scalar(hT[j][:, f, :], k.ps[j][:, 2, :], w["b1"][:, e * FC + f:e * FC + f + 1],
                                          0.0, ALU.add, ALU.max).then_inc(S["h_dve"], 1)
                    if n + 2 < UNITS:
                        masked(n + 2)
                tail.vector(dve, c)

            @block.gpsimd
            def _(pool):
                tail.gpsimd(pool)
    


def l3_attention(k):
    nc, w = k.nc, k.w
    GROUPS, GH = 4, 4
    TILES = [(t, b) for t in range(NT) for b in range(t + 1)]
    UNITS = [(g, t, b) for g in range(GROUPS) for t, b in TILES]
    PER = len(TILES)
    BLOCKS, BLOCK = 8, 64
    HALF = 64
    S = k.signals("q_ps k_ps zeros pick v_ps v_ones v blk r1 h1 r2 rows kf kr km ksplit qf qk qh qr qm qsplit"
                  " picked in_act in_dve s1 part_max nmax nmax_parts nmax_ps nmaxT s2 exp pv outT o_ps attn"
                  " a_ps aT y step astep" + LN_SIGNALS + TAIL_SIGNALS)

    STEPS = []
    for g in range(GROUPS):
        STEPS.append(("maxima", g))
        for v in range(PER):
            if v == 3 and g > 0:
                STEPS.append(("results", g - 1))
            STEPS.append(("unit", g * PER + v))
        if g == 0:
            STEPS.append(None)
    STEPS += [None] * 4 + [("results", GROUPS - 1)]
    AHEAD = PER + 2
    LAG = 2
    SLOTS = AHEAD + len(STEPS)

    def step(s):
        return STEPS[s] if 0 <= s < len(STEPS) and STEPS[s] else (None, 0)

    with k.scratch():
        st = [k.tmp(f"stats{j}", [P, NT, 10]) for j in LANES]
        q16 = [k.tmp(f"q_operand{j}", [P, H // 2, T], BF16) for j in LANES]
        room = [k.group["L2w1"], k.group["L2w2"]]
        k16 = [r[:, :].bitcast(BF16).rearrange("p (h n) -> p h n", h=H) for r in room]
        pick = k.tmp("pick_all_rows", [P, 2, H // 2, 3 * P], BF16)
        row16 = {x: k.tmp(f"{x}_row", [P, T], BF16) for x in "qk"}
        VA = [k.tmp(f"values{j}", [P, NT, H * (DH + 1) + 32 - DH - 1]) for j in LANES]
        blk = k.tmp("blk", [P, BLOCKS]); h1 = k.tmp("h1", [P, BLOCKS]); new8 = k.tmp("new8", [P, BLOCKS])
        far8 = k.tmp("far8", [P, BLOCKS])
        pmax = [k.tmp(f"part_max{j}", [P, 2, NT, GH, NT]) for j in LANES]
        nmax = [k.tmp(f"nmax{j}", [P, NT, GH]) for j in LANES]
        nmax16 = [k.tmp(f"nmax_parts{j}", [P, NT, 3, GH], BF16) for j in LANES]
        nmaxT = [k.tmp(f"nmaxT{j}", [P, T], BF16) for j in LANES]
        pT = [k.tmp(f"pT{j}", [P, 3, T]) for j in LANES]
        outT = [k.tmp(f"outT{j}", [P, T]) for j in LANES]
        rs = [k.tmp(f"rs{j}", [P, NT, GH]) for j in LANES]
        attn = [k.tmp(f"attn{j}", [P, NT, D]) for j in LANES]
        part16 = {x: [p[:, :, :].rearrange("p a n -> p (a n)").bitcast(BF16).rearrange(
            "p (x a n) -> p x a n", x=2, a=3)[:, "qk".index(x)] for p in pT] for x in "qk"}
        whole = {"k": outT, "q": [a[:, :, :].rearrange("p t n -> p (t n)") for a in attn]}
        tail = Tail(k, S, st, via=1, ready="y", bias=w["b_out"], yT=outT)

        with nc.Block(no_gpsimd_drain=True) as block:

            @block.tensor
            def _(pe):
                k.have(pe, "L3", "const")
                for j in LANES:
                    pe.matmul(k.ps[j][:, 0, :], w["k3"], k.XT[j][:, :], start=True, stop=True).then_inc(S["k_ps"], 1)
                for j in LANES:
                    pe.matmul(k.ps[j][:, 1, :], w["q3"], k.XT[j][:, :], start=True, stop=True).then_inc(S["q_ps"], 1)
                for j in LANES:
                    for t in range(NT):
                        ins = pe.matmul(k.ps[j][:, 3, t * P:(t + 1) * P], k.XT[j][:, t * P:(t + 1) * P], w["v3"],
                                        start=True, stop=True)
                    ins.then_inc(S["v_ps"], 1)
                pe.wait_ge(S["blk"], 1)
                pe.matmul(k.ps[0][:, 2, 0:BLOCKS], w["r1"], blk[:, :], start=True, stop=True).then_inc(S["r1"], 1)
                pe.wait_ge(S["h1"], 1)
                pe.matmul(k.ps[1][:, 2, 0:BLOCKS], w["r2"], h1[:, :], start=True, stop=True).then_inc(S["r2"], 1)
                pe.wait_ge(S["rows"], 1)
                pe.wait_ge(S["qf"], 2)
                pe.wait_ge(S["pick"], 1)
                n = 0
                for x in "kq":
                    for c in range(H // 2):
                        for j in LANES:
                            if c == 0:
                                pe.wait_ge(S[x + "split"], j + 1)
                            if n >= 4:
                                pe.wait_ge(S[("in_act", "in_dve")[j]], (n - 4) // 2 + 1)
                            out = k.ps[j][:, c % 2, :]
                            for a in range(3):
                                pe.matmul(out, pick[:, "qk".index(x), c, a * P:(a + 1) * P], part16[x][j][:, a, :],
                                          start=(a == 0), stop=False)
                            pe.matmul(out, w["extra"], row16[x][:, :], start=False,
                                      stop=True).then_inc(S["picked"], 1)
                            n += 1
                for j in LANES:
                    pe.wait_ge(S[("in_act", "in_dve")[j]], n // 2)
                pe.wait_ge(S["zeros"], 4)

                def sweep1(i, j):
                    g, t, b = UNITS[i]
                    if i >= 1:
                        pe.wait_ge(S["part_max"], 2 * (i - 1) + j + 1)
                    for h in range(0, GH, 2):
                        out = k.ps[j][:, 0, h * P:(h + 2) * P]
                        ins = pe.matmul(out, q16[j][:, (GH * g + h) // 2, t * P:(t + 1) * P],
                                        k16[j][:, GH * g + h:GH * g + h + 2, b * P:(b + 1) * P],
                                        start=True, stop=(b < t))
                        if b == t:
                            ins = pe.matmul(out, k.ident16[:, :], rep(w["causal"], 1, 2), start=False, stop=True)
                    ins.then_inc(S["s1"], 1)

                def sweep2(s, j):
                    what, n = step(s)
                    if what is None:
                        return
                    bank = 1 + s % 2
                    before, m = step(s - 2)
                    if before == "unit":
                        pe.wait_ge(S["exp"], 2 * m + j + 1)
                    elif before == "maxima":
                        pe.wait_ge(S["nmaxT"], 2 * m + j + 1)
                    elif before == "results":
                        pe.wait_ge(S["attn"], 2 * m + j + 1)
                    if what == "maxima":
                        pe.wait_ge(S["nmax_parts"], 2 * n + j + 1)
                        for t in range(NT):
                            ins = pe.matmul(k.ps[j][0:3 * GH, bank, t * P:(t + 1) * P],
                                            nmax16[j][:, t, :, :].rearrange("p a h -> p (a h)"), k.ident16[:, :],
                                            start=True, stop=True)
                        ins.then_inc(S["nmax_ps"], 1)
                    elif what == "results":
                        pe.wait_ge(S["outT"], 2 * n + j + 1)
                        for t in range(NT):
                            ins = pe.transpose(k.ps[j][:, bank, t * P:(t + 1) * P], outT[j][:, t * P:(t + 1) * P],
                                               w["ident"])
                        ins.then_inc(S["o_ps"], 1)
                    else:
                        g, t, b = UNITS[n]
                        ones = w["ones_of"].rearrange("p (h n) -> p h n", h=GH)
                        pe.wait_ge(S["nmaxT"], 2 * g + j + 1)
                        for h in range(GH):
                            out = k.ps[j][:, bank, h * P:(h + 1) * P]
                            pe.matmul(out, k16[j][:, GH * g + h, b * P:(b + 1) * P],
                                      q16[j][:, (GH * g + h) // 2, t * P:(t + 1) * P], start=True, stop=False)
                            ins = pe.matmul(out, ones[:, h, :], nmaxT[j][:, t * P:(t + 1) * P],
                                            start=False, stop=(b < t))
                            if b == t:
                                ins = pe.matmul(out, w["causal"], k.ident16[:, :], start=False, stop=True)
                        ins.then_inc(S["s2"], 1)

                def values(s, j):
                    what, u = step(s)
                    if what != "unit":
                        return
                    g, t, b = UNITS[u]
                    pe.wait_ge(S["exp"], 2 * u + j + 1)
                    if t == 0 and g > 0:
                        pe.wait_ge(S["outT"], 2 * (g - 1) + j + 1)
                    for h in range(GH):
                        v = (DH + 1) * (GH * g + h)
                        ins = pe.matmul(k.ps[j][32 * h:32 * h + 32, 3, t * P:(t + 1) * P], VA[j][:, b, v:v + 32],
                                        pT[j][:, u % 3, h * P:(h + 1) * P], start=(b == 0), stop=(b == t))
                    ins.then_inc(S["pv"], 1)

                for slot in range(SLOTS):
                    for j in LANES:
                        if slot < len(UNITS):
                            sweep1(slot, j)
                        sweep2(slot - AHEAD, j)
                        values(slot - AHEAD - LAG, j)
                for j in LANES:
                    pe.wait_ge(S["attn"], 2 * (GROUPS - 1) + j + 1)
                    for t in range(NT):
                        ins = pe.transpose(k.ps[j][:, 0, t * P:(t + 1) * P], attn[j][:, t, :], w["ident"])
                    ins.then_inc(S["a_ps"], 1)
                for j in LANES:
                    pe.wait_ge(S["aT"], j + 1)
                    pe.matmul(k.ps[j][:, 1, :], w["o3"], pT[j][:, 0, :], start=True, stop=True).then_inc(S["y"], 1)
                tail.tensor(pe)

            @block.scalar
            def _(act):
                k.have(act, "vec")
                for j in LANES:
                    act.wait_ge(S["k_ps"], j + 1)
                    act.activation(part16["k"][j][:, 0, :], k.ps[j][:, 0, :], ACT.Copy)
                    act.activation(whole["k"][j][:, :], k.ps[j][:, 0, :], ACT.Copy).then_inc(S["kf"], 1)
                for j in LANES:
                    act.wait_ge(S["q_ps"], j + 1)
                    act.activation(whole["q"][j], k.ps[j][:, 1, :], ACT.Copy, scale=float(D) ** -0.5).then_inc(S["qf"], 1)
                act.wait_ge(S["r1"], 1)
                act.activation(h1[:, :], k.ps[0][:, 2, 0:BLOCKS], ACT.Relu, bias=w["b_r1"],
                               scale=1.0 / BLOCK).then_inc(S["h1"], 1)
                for j in LANES:
                    act.wait_ge(S["kr"], j + 1)
                    act.activation(part16["k"][j][:, 1, :], whole["k"][j][:, :], ACT.Copy).then_inc(S["km"], 1)
                for j in LANES:
                    act.wait_ge(S["qk"], j + 1)
                    act.activation(part16["q"][j][:, 0, :], whole["q"][j], ACT.Copy).then_inc(S["qh"], 1)
                for j in LANES:
                    act.wait_ge(S["qr"], j + 1)
                    act.activation(part16["q"][j][:, 1, :], whole["q"][j], ACT.Copy).then_inc(S["qm"], 1)
                for n, (x, c) in enumerate((x, c) for x in "kq" for c in range(H // 2)):
                    act.wait_ge(S["picked"], 2 * n + 1)
                    if x == "q":
                        ins = act.activation(q16[0][:, c, :], k.ps[0][:, c % 2, :], ACT.Copy)
                    else:
                        act.activation(k16[0][0:HALF, 2 * c, :], k.ps[0][0:HALF, c % 2, :], ACT.Copy)
                        ins = act.activation(k16[0][HALF:P, 2 * c + 1, :], k.ps[0][HALF:P, c % 2, :], ACT.Copy)
                    ins.then_inc(S["in_act"], 1)
                act.wait_ge(S["astep"], 4)
                for slot in range(AHEAD, SLOTS):
                    for j in LANES:
                        s = slot - AHEAD
                        what, n = step(s)
                        bank = 1 + s % 2
                        if what == "maxima":
                            act.wait_ge(S["nmax_ps"], 2 * n + j + 1)
                            act.activation(nmaxT[j][0:3 * GH, :], k.ps[j][0:3 * GH, bank, :],
                                           ACT.Copy).then_inc(S["nmaxT"], 1)
                        elif what == "unit":
                            act.wait_ge(S["s2"], 2 * n + j + 1)
                            if n >= 3:
                                act.wait_ge(S["pv"], 2 * (n - 3) + j + 1)
                            act.activation(pT[j][:, n % 3, :], k.ps[j][:, bank, :], ACT.Exp).then_inc(S["exp"], 1)
                        ended, u = step(s - LAG - 1)
                        if ended == "unit" and u % PER == PER - 1:
                            g = u // PER
                            act.wait_ge(S["pv"], 2 * u + j + 1)
                            if g > 0:
                                act.wait_ge(S["o_ps"], 2 * (g - 1) + j + 1)
                            else:
                                act.wait_ge(S["in_dve"], H)
                            act.activation(outT[j][:, :], k.ps[j][:, 3, :], ACT.Copy).then_inc(S["outT"], 1)
                for j in LANES:
                    act.wait_ge(S["a_ps"], j + 1)
                    act.activation(pT[j][:, 0, :], k.ps[j][:, 0, :], ACT.Copy).then_inc(S["aT"], 1)
                tail.scalar(act)

            @block.vector
            def _(dve):
                k.have(dve, "vec", "const")
                c = Chain(dve, S["step"])
                four = w["pick"].rearrange("p (x v n) -> p x v n", x=2, v=4)
                dve.tensor_scalar(pick[:, :, 0:4, :], four, w["low"], None, ALU.mult)
                dve.tensor_scalar(pick[:, :, 4:8, :], four, w["high"], None, ALU.mult).then_inc(S["pick"], 1)
                dve.wait_ge(S["kf"], 1)
                dve.tensor_reduce(blk[:, :], whole["k"][0][:, :].rearrange("p (b n) -> p b n", n=BLOCK), AX.X,
                                  ALU.add).then_inc(S["blk"], 1)
                dve.wait_ge(S["blk"], 1)
                for j in LANES:
                    dve.wait_ge(S["kf"], j + 1)
                    dve.tensor_tensor(whole["k"][j][:, :], whole["k"][j][:, :], part16["k"][j][:, 0, :],
                                      ALU.subtract).then_inc(S["kr"], 1)
                dve.wait_ge(S["v_ones"], 1)
                for j in LANES:
                    dve.wait_ge(S["v_ps"], j + 1)
                    va = VA[j][:, :, 0:H * (DH + 1)].rearrange("p t (h d) -> p t h d", h=H)
                    ps = k.ps[j][:, 3, :].rearrange("p (t h d) -> p t h d", t=NT, h=H)
                    for t in range(NT):
                        ins = dve.tensor_copy(va[:, t, :, 0:DH], ps[:, t])
                    ins.then_inc(S["v"], 1)
                dve.wait_ge(S["r2"], 1)
                c.link(dve.tensor_scalar(new8[:, :], k.ps[1][:, 2, 0:BLOCKS], w["b_r2"], 0.0, ALU.add, ALU.is_gt))
                c.link(dve.tensor_scalar(new8[:, :], new8[:, :], k.first_pair[:, :], None, ALU.mult))
                c.link(dve.tensor_tensor(k.keep8[:, :], k.keep8[:, :], new8[:, :], ALU.max))
                c.link(dve.tensor_scalar(far8[:, :], k.keep8[:, :], FAR, -FAR, ALU.mult, ALU.add))
                by_block = {x: r[:, :].rearrange("p (b n) -> p b n", n=BLOCK) for x, r in row16.items()}
                dve.tensor_copy(by_block["q"], rep(k.keep8[:, :], 2, BLOCK))
                dve.tensor_copy(by_block["k"], rep(far8[:, :], 2, BLOCK)).then_inc(S["rows"], 1)
                for j in LANES:
                    dve.wait_ge(S["km"], j + 1)
                    dve.tensor_tensor(part16["k"][j][:, 2, :], whole["k"][j][:, :], part16["k"][j][:, 1, :],
                                      ALU.subtract).then_inc(S["ksplit"], 1)
                for j in LANES:
                    dve.wait_ge(S["qf"], j + 1)
                    q = whole["q"][j].rearrange("p (b n) -> p b n", n=BLOCK)
                    dve.tensor_tensor(q, q, rep(k.keep8[:, :], 2, BLOCK), ALU.mult).then_inc(S["qk"], 1)
                for j in LANES:
                    dve.wait_ge(S["qh"], j + 1)
                    dve.tensor_tensor(whole["q"][j], whole["q"][j], part16["q"][j][:, 0, :],
                                      ALU.subtract).then_inc(S["qr"], 1)
                for j in LANES:
                    dve.wait_ge(S["qm"], j + 1)
                    dve.tensor_tensor(part16["q"][j][:, 2, :], whole["q"][j], part16["q"][j][:, 1, :],
                                      ALU.subtract).then_inc(S["qsplit"], 1)
                for n, (x, ch) in enumerate((x, ch) for x in "kq" for ch in range(H // 2)):
                    dve.wait_ge(S["picked"], 2 * n + 2)
                    if x == "q":
                        ins = dve.tensor_copy(q16[1][:, ch, :], k.ps[1][:, ch % 2, :])
                    else:
                        dve.tensor_copy(k16[1][0:HALF, 2 * ch, :], k.ps[1][0:HALF, ch % 2, :])
                        ins = dve.tensor_copy(k16[1][HALF:P, 2 * ch + 1, :], k.ps[1][HALF:P, ch % 2, :])
                    ins.then_inc(S["in_dve"], 1)
                dve.wait_ge(S["astep"], 4)
                for slot in range(SLOTS):
                    for j in LANES:
                        if slot < len(UNITS):
                            g, t, b = UNITS[slot]
                            dve.wait_ge(S["s1"], 2 * slot + j + 1)
                            if slot % PER == 0 and g >= 2:
                                dve.wait_ge(S["nmax"], 2 * (g - 2) + j + 1)
                            dve.tensor_reduce(pmax[j][:, g % 2, t, :, b], k.ps[j][:, 0, :].rearrange("p (h n) -> p h n", h=GH),
                                              AX.X, ALU.max, negate=True).then_inc(S["part_max"], 1)
                        if slot % PER == 0 and 0 < slot <= len(UNITS):
                            g = slot // PER - 1
                            dve.wait_ge(S["part_max"], 2 * (slot - 1) + j + 1)
                            if g > 0:
                                dve.wait_ge(S["nmax_parts"], 2 * (g - 1) + j + 1)
                            dve.tensor_reduce(nmax[j][:, :, :], pmax[j][:, g % 2, :, :, :], AX.X,
                                              ALU.min).then_inc(S["nmax"], 1)
                        s = slot - AHEAD
                        what, g = step(s)
                        if what == "results":
                            dve.wait_ge(S["o_ps"], 2 * g + j + 1)
                            o = k.ps[j][:, 1 + s % 2, :].rearrange("p (t h n) -> p t h n", t=NT, h=GH)
                            c.link(dve.reciprocal(rs[j][:, :, :], o[:, :, :, DH]))
                            for t in range(NT):
                                heads = attn[j][:, t, GH * g * DH:GH * (g + 1) * DH]
                                ins = dve.tensor_tensor(heads.rearrange("p (h d) -> p h d", d=DH), o[:, t, :, 0:DH],
                                                        rep(rs[j][:, t, :], 2, DH), ALU.mult)
                            ins.then_inc(S["attn"], 1)
                tail.vector(dve, c)

            @block.gpsimd
            def _(pool):
                c = Chain(pool, S["astep"])
                c.mark(pool.memset(nmaxT[0][:, :], 0.0))
                c.mark(pool.memset(nmaxT[1][:, :], 0.0))
                c.mark(pool.memset(pmax[0][:, :, :, :, :], NEVER))
                c.mark(pool.memset(pmax[1][:, :, :, :, :], NEVER))
                pool.memset(VA[0][:, :, :], 1.0)
                pool.memset(VA[1][:, :, :], 1.0).then_inc(S["v_ones"], 1)
                pool.wait_ge(S["v_ones"], 1)
                for j in LANES:
                    pairs = room[j][:, :].rearrange("p (c two n) -> p c two n", c=H // 2, two=2)
                    pool.memset(pairs[HALF:P, :, 0, :], 0.0).then_inc(S["zeros"], 1)
                    pool.wait_ge(S["zeros"], 2 * j + 1)
                    pool.memset(pairs[0:HALF, :, 1, :], 0.0).then_inc(S["zeros"], 1)
                    pool.wait_ge(S["zeros"], 2 * j + 2)
                for g in range(GROUPS):
                    for j in LANES:
                        pool.wait_ge(S["nmax"], 2 * g + j + 1)
                        if g > 0:
                            pool.wait_ge(S["nmax_ps"], 2 * (g - 1) + j + 1)
                        c.link(pool.tensor_copy(nmax16[j][:, :, 0, :], nmax[j][:, :, :]))
                        c.link(pool.tensor_tensor(nmax[j][:, :, :], nmax[j][:, :, :], nmax16[j][:, :, 0, :], ALU.subtract))
                        c.link(pool.tensor_copy(nmax16[j][:, :, 1, :], nmax[j][:, :, :]))
                        pool.tensor_tensor(nmax16[j][:, :, 2, :], nmax[j][:, :, :], nmax16[j][:, :, 1, :],
                                           ALU.subtract).then_inc(S["nmax_parts"], 1)
                tail.gpsimd(pool)
    

def l3_bitnet(k):
    nc, w = k.nc, k.w
    S = k.signals("reloaded absum total unround tern quant x_ps xqT gu_ps silu hid hscale hq hq_ps hqT y_tile step"
                  + LN_SIGNALS + TAIL_SIGNALS)
    UNITS = 2 * NT
    with k.scratch():
        st = [k.tmp(f"stats{j}", [P, NT, 10]) for j in LANES]
        w3 = k.group["L3"][:, -3 * FF:].rearrange("p (a n) -> p a n", a=3)
        absum = k.tmp("absum", [P, 3]); mean = k.tmp("mean", [P, 3]); inv = k.tmp("inv", [P, 3])
        scaled = k.tmp("scaled", [P, 3, FF]); tern = k.tmp("tern", [P, 3, FF], BF16)
        unround = k.tmp("unround", [P, 1])
        am = [k.tmp(f"am{j}", [P, NT]) for j in LANES]; qs = [k.tmp(f"qs{j}", [P, NT]) for j in LANES]
        sg = [k.tmp(f"sg{j}", [P, NT]) for j in LANES]; su = [k.tmp(f"su{j}", [P, NT]) for j in LANES]
        xq = [k.tmp(f"xq{j}", [P, NT, D]) for j in LANES]
        xqT = [k.tmp(f"xqT{j}", [P, T], BF16) for j in LANES]
        g = [k.tmp(f"g{j}", [P, FF]) for j in LANES]
        hid = [k.tmp(f"hid{j}", [P, FF]) for j in LANES]
        hm = [k.tmp(f"hm{j}", [P, NT]) for j in LANES]; hs = [k.tmp(f"hs{j}", [P, NT]) for j in LANES]
        sd = [k.tmp(f"sd{j}", [P, NT]) for j in LANES]
        hqT = [k.tmp(f"hqT{j}", [P, FC, P], BF16) for j in LANES]
        tail = Tail(k, S, st, y_at=("y_tile", 1, UNITS - 2), tile_scale=sd)
        with nc.Block(no_gpsimd_drain=True) as block:

            @block.sync
            def _(sp):
                for group in ("L2w1", "L2w2"):
                    sp.dma_start(k.group[group][:, :], k.dram[group]).then_inc(S["reloaded"], 16)
                sp.wait_ge(S["reloaded"], 32)

            @block.tensor
            def _(pe):
                k.have(pe, "const")
                pe.wait_ge(S["absum"], 1)
                pe.matmul(k.ps[0][:, 0, 0:3], w["ones"], absum[:, :], start=True, stop=True).then_inc(S["total"], 1)
                for j in LANES:
                    pe.wait_ge(S["quant"], j + 1)
                    for t in range(NT):
                        ins = pe.transpose(k.ps[j][:, 2, t * P:(t + 1) * P], xq[j][:, t, :], w["ident"])
                    ins.then_inc(S["x_ps"], 1)
                pe.wait_ge(S["tern"], 1)
                pe.wait_ge(S["xqT"], 2)

                def gate_up(n):
                    j, t = n % 2, n // 2
                    if n >= 2:
                        pe.wait_ge(S["hid"], n - 1)
                    for a in range(2):
                        ins = pe.matmul(k.ps[j][:, a, :], xqT[j][:, t * P:(t + 1) * P], tern[:, a, :],
                                        start=True, stop=True)
                    ins.then_inc(S["gu_ps"], 1)

                def turn(n):
                    j, t = n % 2, n // 2
                    pe.wait_ge(S["hq"], n + 1)
                    if n >= 2:
                        pe.wait_ge(S["hqT"], n - 1)
                    for f in range(FC):
                        ins = pe.transpose(k.ps[j][:, 2, f * P:(f + 1) * P], hid[j][:, f * P:(f + 1) * P], w["ident"])
                    ins.then_inc(S["hq_ps"], 1)

                def down(n):
                    j, t = n % 2, n // 2
                    pe.wait_ge(S["hqT"], n + 1)
                    for f in range(FC):
                        ins = pe.matmul(k.ps[j][:, 3, t * P:(t + 1) * P], hqT[j][:, f, :],
                                        tern[:, 2, f * P:(f + 1) * P], start=(f == 0), stop=(f == FC - 1))
                    ins.then_inc(S["y_tile"], 1)

                for n in range(UNITS + 2):
                    if n < UNITS:
                        gate_up(n)
                    if 0 <= n - 1 < UNITS:
                        turn(n - 1)
                    if 0 <= n - 2 < UNITS:
                        down(n - 2)
                tail.tensor(pe)

            @block.scalar
            def _(act):
                for j in LANES:
                    act.wait_ge(S["x_ps"], j + 1)
                    act.wait_ge(S["unround"], 1)
                    act.activation(xqT[j][:, :], k.ps[j][:, 2, :], ACT.Identity, bias=unround[:, :],
                                   scale=1.0).then_inc(S["xqT"], 1)
                act.wait_ge(S["hscale"], 1)
                for n in range(UNITS + 1):
                    if n < UNITS:
                        j, t = n % 2, n // 2
                        act.wait_ge(S["gu_ps"], n + 1)
                        act.activation(g[j][:, :], k.ps[j][:, 0, :], ACT.Silu,
                                       scale=sg[j][:, t:t + 1]).then_inc(S["silu"], 1)
                    if n >= 1:
                        j, t = (n - 1) % 2, (n - 1) // 2
                        act.wait_ge(S["hq_ps"], n)
                        if n - 1 >= 2:
                            act.wait_ge(S["y_tile"], n - 2)
                        act.activation(hqT[j][:, :, :].rearrange("p f n -> p (f n)"), k.ps[j][:, 2, :], ACT.Identity,
                                       bias=unround[:, :], scale=1.0).then_inc(S["hqT"], 1)
                tail.scalar(act)

            @block.vector
            def _(dve):
                k.have(dve, "L3")
                c = Chain(dve, S["step"])
                dve.tensor_reduce(absum[:, :], w3, AX.X, ALU.add, apply_absolute_value=True).then_inc(S["absum"], 1)
                n = {}
                for j in LANES:
                    n[j] = c.mark(dve.tensor_reduce(am[j][:, :], k.X[j][:, :, :], AX.X, ALU.max,
                                                    apply_absolute_value=True))
                dve.wait_ge(S["total"], 1)
                c.link(dve.tensor_scalar(mean[:, :], k.ps[0][:, 0, 0:3], 1.0 / (D * FF), 1e-5, ALU.mult, ALU.max))
                c.link(dve.reciprocal(inv[:, :], mean[:, :]))
                for j in LANES:
                    c.link(dve.tensor_scalar(am[j][:, :], am[j][:, :], 1e-5, None, ALU.max))
                    c.link(dve.reciprocal(qs[j][:, :], am[j][:, :]))
                    c.link(dve.tensor_scalar(qs[j][:, :], qs[j][:, :], 127.0, None, ALU.mult))
                    for t in range(NT):
                        ins = dve.tensor_scalar(xq[j][:, t, :], k.X[j][:, t, :], qs[j][:, t:t + 1], 127.0,
                                                ALU.mult, ALU.min)
                    c.link(ins)
                    dve.tensor_scalar(xq[j][:, :, :], xq[j][:, :, :], -128.0, ROUND, ALU.max,
                                      ALU.add).then_inc(S["quant"], 1)
                for a in range(3):
                    ins = dve.tensor_scalar(scaled[:, a, :], w3[:, a, :], inv[:, a:a + 1], ROUND, ALU.mult, ALU.add)
                c.link(ins)
                c.link(dve.tensor_scalar(scaled[:, :, :], scaled[:, :, :], ROUND, 1.0, ALU.subtract, ALU.min))
                dve.tensor_scalar(tern[:, :, :], scaled[:, :, :], -1.0, None, ALU.max).then_inc(S["tern"], 1)
                for j in LANES:
                    for dst, a in ((sg, 0), (su, 1)):
                        ins = dve.tensor_scalar(dst[j][:, :], am[j][:, :], mean[:, a:a + 1], 1.0 / 127.0,
                                                ALU.mult, ALU.mult)
                ins.then_inc(S["hscale"], 1)
                dve.wait_ge(S["hscale"], 1)
                for n in range(UNITS):
                    j, t = n % 2, n // 2
                    dve.wait_ge(S["silu"], n + 1)
                    if n >= 2:
                        dve.wait_ge(S["hq_ps"], n - 1)
                    ins = dve.scalar_tensor_tensor(out=hid[j][:, :], in0=k.ps[j][:, 1, :], scalar=su[j][:, t:t + 1],
                                                   in1=g[j][:, :], op0=ALU.mult, op1=ALU.mult)
                    ins.then_inc(S["hid"], 1)
                    dve.wait_ge(S["hid"], n + 1)
                    one = slice(t, t + 1)
                    c.link(dve.tensor_reduce(hm[j][:, one], hid[j][:, :], AX.X, ALU.max, apply_absolute_value=True))
                    c.link(dve.tensor_scalar(hm[j][:, one], hm[j][:, one], 1e-5, None, ALU.max))
                    dve.tensor_scalar(sd[j][:, one], hm[j][:, one], mean[:, 2:3], 1.0 / 127.0, ALU.mult, ALU.mult)
                    c.link(dve.reciprocal(hs[j][:, one], hm[j][:, one]))
                    c.link(dve.tensor_scalar(hs[j][:, one], hs[j][:, one], 127.0, None, ALU.mult))
                    c.link(dve.tensor_scalar(hid[j][:, :], hid[j][:, :], hs[j][:, one], 127.0, ALU.mult, ALU.min))
                    dve.tensor_scalar(hid[j][:, :], hid[j][:, :], -128.0, ROUND, ALU.max,
                                      ALU.add).then_inc(S["hq"], 1)
                tail.vector(dve, c)

            @block.gpsimd
            def _(pool):
                pool.memset(unround[:, :], -ROUND).then_inc(S["unround"], 1)
                tail.gpsimd(pool)
    


def build(nc, dram):
    with ExitStack() as stack:
        k = Net(nc, stack, dram)
        w = k.w
        setup(k)
        with nc.Fori(0, B // 2) as g:
            turn_pair(k)
            l0_state_space(k)
            cross_attention(k, w["q0"], w["k0"], w["v0"], w["o0"], "L0", wide=False, bias=0.0)
            l0_signs(k)
            l1_quaternion(k)
            cross_attention(k, w["xq1"], w["xk1"], w["xv1"], w["xo1"], "L1", wide=True, bias=w["xbo1"])
            l1_mixture(k)
            l2_linear_attention(k)
            l2_perceiver(k)
            l2_switch(k)
            l3_attention(k)
            cross_attention(k, w["xq3"], w["xk3"], w["xv3"], w["xo3"], "L3", wide=False, bias=0.0, mask=1)
            l3_bitnet(k)
            store_pair(k, g)


def layout(i):
    import numpy as np

    f32 = np.float32

    def chunks(a):
        c = a.shape[0] // P
        return np.ascontiguousarray(a.reshape(c, P, -1).transpose(1, 0, 2).reshape(P, -1))

    def column(v):
        return np.asarray(v).reshape(-1, P).T

    def padded(v):
        out = np.zeros((P, 1), f32)
        out[:v.shape[0], 0] = v
        return out

    def every(v):
        return np.broadcast_to(np.asarray(v).reshape(1, -1), (P, np.asarray(v).size))

    qkv = i["L3_attn_w_qkv"]
    part = {
        "gate": i["L0_attn_Wg"].T, "inB": i["L0_attn_WB"].T, "Wout": i["L0_attn_Wout"].T,
        "q0": i["L0_xattn_Wq"], "o0": i["L0_xattn_Wo"],
        "k1": i["L1_attn_Wk"].T, "v1": i["L1_attn_Wv"].T, "o1": i["L1_attn_Wo"].T,
        "xq1": i["L1_xattn_Wq"], "xo1": chunks(i["L1_xattn_Wo"]), "router1": i["L1_ffn_w_router"],
        "wi": i["L1_ffn_wi"].transpose(1, 0, 2).reshape(D, E * FF),
        "wo": i["L1_ffn_wo"].reshape(E, FC, P, D).transpose(2, 0, 1, 3).reshape(P, E * FF),
        "qkv2": np.concatenate([i["L2_attn_q_w"].T, i["L2_attn_k_w"].T, i["L2_attn_v_w"].T], 1),
        "o2": i["L2_attn_o_w"].T, "fc": i["L2_attn_fc_w"].T, "proj": chunks(i["L2_attn_proj_w"].T),
        "xqkv2": np.concatenate([i["L2_xattn_Wq"].T, i["L2_xattn_Wlkv"].T], 1),
        "xo2": i["L2_xattn_Wo"].T, "router2": i["L2_ffn_Wr"],
        "W1": i["L2_ffn_W1"].transpose(1, 0, 2).reshape(D, E * FF),
        "W2": i["L2_ffn_W2"].reshape(E, FC, P, D).transpose(2, 0, 1, 3).reshape(P, E * FF),
        "q3": qkv[0:D].T, "k3": qkv[D:2 * D].T, "v3": qkv[2 * D:].T,
        "r1": i["L3_attn_w_r1"].T, "r2": np.broadcast_to(i["L3_attn_w_r2"].T, (P, P)),
        "o3": i["L3_attn_w_out"].T, "xq3": i["L3_xattn_Wq"], "xo3": i["L3_xattn_Wo"],
        "wgate": i["L3_ffn_w_gate"].T, "wup": i["L3_ffn_w_up"].T, "wdown": chunks(i["L3_ffn_w_down"].T),
        "k0": i["L0_xattn_Wk"], "v0": i["L0_xattn_Wv"], "xk1": i["L1_xattn_Wk"], "xv1": i["L1_xattn_Wv"],
        "xkv2": i["L2_xattn_Wkv"].T, "xk3": i["L3_xattn_Wk"], "xv3": i["L3_xattn_Wv"],
        "bg": padded(i["L0_attn_bg"]), "A_log": padded(i["L0_attn_A_log"]), "D": column(i["L0_attn_D"]),
        "gamma": column(i["L0_attn_gamma"]), "beta": column(i["L0_attn_beta"]),
        "bout": column(i["L0_attn_bout"]),
        "s0": every(i["L0_ffn_s0"]), "s1": every(i["L0_ffn_s1"]), "s2": every(i["L0_ffn_s2"]),
        "ln_g": column(i["L1_attn_ln_g"]), "ln_b": column(i["L1_attn_ln_b"]), "bo1": column(i["L1_attn_bo"]),
        "xbo1": column(i["L1_xattn_bo"]),
        "ln1_w": column(i["L2_attn_ln1_w"]), "ln1_b": column(i["L2_attn_ln1_b"]),
        "o_b": column(i["L2_attn_o_b"]), "ln2_w": column(i["L2_attn_ln2_w"]),
        "ln2_b": column(i["L2_attn_ln2_b"]), "fc_b": column(i["L2_attn_fc_b"]),
        "proj_b": column(i["L2_attn_proj_b"]),
        "ln_x_g": padded(i["L2_xattn_ln_x_g"]), "ln_x_b": padded(i["L2_xattn_ln_x_b"]),
        "ln_l_g": column(i["L2_xattn_ln_l_g"]), "ln_l_b": column(i["L2_xattn_ln_l_b"]),
        "qn_g": column(np.concatenate([i["L2_xattn_qn_g"]] * 2)),
        "kn_g": column(np.concatenate([i["L2_xattn_kn_g"]] * 2)), "xbo2": column(i["L2_xattn_bo"]),
        "b1": column(i["L2_ffn_b1"].reshape(-1)), "b2": i["L2_ffn_b2"].T,
        "b_r1": column(i["L3_attn_b_r1"]), "b_r2": every(i["L3_attn_b_r2"]), "b_out": column(i["L3_attn_b_out"]),
        "bk1": every(i["L1_attn_bk"]), "bv1": every(i["L1_attn_bv"]),
        "bqkv2": every(np.concatenate([i["L2_attn_q_b"], i["L2_attn_k_b"], i["L2_attn_v_b"]])),
        "br": every(i["L2_ffn_br"]), "WC": i["L0_attn_WC"].T,
    }
    row, col = np.arange(P)[:, None], np.arange(P)[None, :]
    restart = np.ones((P, E, 16), f32)
    restart[:, :, 0] = 0.0
    part.update({
        "ident": (row == col), "tri": (row <= col), "ones": np.ones((P, P)),
        "headmask": row // DH == np.arange(H)[None, :],
        "rpos": (np.arange(NT)[None, :] * P + row + 1.0) ** -0.5,
        "slot": np.broadcast_to(np.arange(CAP), (P, CAP)), "down8": np.broadcast_to(E - np.arange(E), (P, E)),
        "restart": restart.reshape(P, -1), "low": row < 64, "high": row >= 64,
    })
    pick = np.zeros((2, 8, DH, 2, 4, 3, 2, 64), f32)
    for head in range(8):
        for d in range(DH):
            for qk, pattern in enumerate((PARTS_Q, PARTS_K)):
                for run, a_part in enumerate(pattern):
                    pick[:, head, d, qk, head // 2, a_part, head % 2, run * DH + d] = 1.0
    ones_of = np.zeros((P, 4, P), f32)
    for head in range(4):
        for a_part in range(3):
            ones_of[a_part * 4 + head, head] = 1.0
    part.update({
        "pick": pick.reshape(P, -1), "extra": (col % 64 == KEEP_ROW) & (row == 0),
        "ones_of": ones_of.reshape(P, -1),
    })

    def pack(columns, constant=f32):
        arrays = [np.asarray(part[name]).astype(constant) if name in dict(CONSTS + CONSTS16) else part[name] for name, _ in columns]
        for (name, n), a in zip(columns, arrays):
            assert a.shape[1] == n, (name, a.shape, n)
        return np.ascontiguousarray(np.concatenate(arrays, 1))

    out = {group: pack(columns) for group, columns in WEIGHTS.items()}
    out.update({"ctxw": pack(CTX_WEIGHTS), "vec": pack(VECTORS), "rows": pack(ROWS),
                "const": pack(CONSTS), "const16": pack(CONSTS16, np.bool_), "WC": pack([("WC", D)])})
    out.update({"x": i["x"], "ctx": i["ctx_768"],
                "ctxT": np.ascontiguousarray(i["ctx_768"].transpose(0, 2, 1)),
                "mask0": i["mask_BxS2_bk0"], "mask1": i["mask_BxS2_bf1"],
                "k0": i["L0_ffn_k0"], "k1": i["L0_ffn_k1"], "k2": i["L0_ffn_k2"]})
    return out


def kernel(**inputs):
    import numpy as np
    import concourse.bacc as bacc
    from concourse.bass_utils import run_bass_kernel_spmd as run

    arrays = layout({name: np.asarray(a) for name, a in inputs.items()})
    nc = bacc.Bacc("TRN2", target_bir_lowering=False, num_devices=1)
    dram, sent = {}, {}
    for name, a in arrays.items():
        a = np.ascontiguousarray(a)
        sent["in_" + name + "_dram"] = a
        dram[name] = nc.dram_tensor("in_" + name + "_dram", a.shape, mybir.dt.from_np(a.dtype),
                                    kind="ExternalInput").ap()
    dram["out"] = nc.dram_tensor("out_dram", (B, T, D), F32, kind="ExternalOutput").ap()
    build(nc, dram)
    return run(nc, [sent], core_ids=[0]).results[0]["out_dram"]
```
